# Optimizing a Trainium2 kernel written in Bass

```python
import numpy as np
import jax
import jax.numpy as jnp

def _softmax(x, axis=-1):
    return jax.nn.softmax(x, axis=axis)

def _gelu(x):
    return jax.nn.gelu(x, approximate=True)

def _silu(x):
    return jax.nn.silu(x)

def _sigmoid(x):
    return jax.nn.sigmoid(x)

def _layernorm(x, axis=-1, eps=1e-05):
    m = jnp.mean(x, axis=axis, keepdims=True)
    v = jnp.var(x, axis=axis, keepdims=True)
    return (x - m) / jnp.sqrt(v + eps)

def _scatter_add(tgt, idx, src, axis=0):
    return tgt.at[idx].add(src)

def _segment_sum(src, seg, n):
    return jax.ops.segment_sum(src, seg, n)
kernel_name = 'mk_adaln_d1_jaxref_r8_694864'

def setup_inputs(seed: int=0):
    np.random.seed(seed)
    _w = jnp.asarray

    def _L0_attn_setup():
        import jax, jax.numpy as jnp
        import numpy as np
        HIDDEN = 256
        NUM_HEADS = 16
        HEAD_DIM = HIDDEN // NUM_HEADS
        key = jax.random.key(seed)
        ks = jax.random.split(key, 5)
        B, S, H = (2, 256, HIDDEN)
        qkv_bound = float(np.sqrt(6.0 / (H + 3 * H)))
        out_bound = float(np.sqrt(6.0 / (H + H)))
        return {'x': jax.random.normal(ks[0], (B, S, H), dtype=jnp.float32), 'W_qkv': jax.random.uniform(ks[1], (3 * H, H), minval=-qkv_bound, maxval=qkv_bound, dtype=jnp.float32), 'b_qkv': jnp.zeros((3 * H,), dtype=jnp.float32), 'W_out': jax.random.uniform(ks[2], (H, H), minval=-out_bound, maxval=out_bound, dtype=jnp.float32), 'b_out': jnp.zeros((H,), dtype=jnp.float32)}
    _L0_attn_in = _L0_attn_setup()

    def _L0_ffn_setup():
        import jax, jax.numpy as jnp
        import numpy as np
        H = 256
        I = 176
        E = 16
        G = 4
        TOPK_GROUP = 2
        K = 4
        SI = 2 * I
        SCALE = 1.0
        NORM = True
        B, S = (4, 64)

        def _swiglu(h):
            g, u = jnp.split(h, 2, axis=-1)
            return jax.nn.silu(g) * u

        def _combine_weights(xt, gate_w):
            T = xt.shape[0]
            scores = jax.nn.softmax(xt @ gate_w.T, axis=-1)
            group_scores = scores.reshape(T, G, E // G).max(axis=-1)
            _, gidx = jax.lax.top_k(group_scores, TOPK_GROUP)
            gmask = jnp.zeros((T, G), bool).at[jnp.arange(T)[:, None], gidx].set(True)
            emask = jnp.repeat(gmask, E // G, axis=1)
            masked = jnp.where(emask, scores, 0.0)
            w, eidx = jax.lax.top_k(masked, K)
            if NORM:
                w = w / (w.sum(-1, keepdims=True) + 1e-20)
            w = w * SCALE
            return jnp.zeros((T, E), xt.dtype).at[jnp.arange(T)[:, None], eidx].add(w)
        key = jax.random.key(seed)
        ks = jax.random.split(key, 6)
        sc = lambda fan_in: 1.0 / np.sqrt(fan_in)
        return {'x': jax.random.normal(ks[0], (B, S, H), jnp.float32), 'gate_w': jax.random.normal(ks[1], (E, H), jnp.float32) * sc(H), 'expert_up_w': jax.random.normal(ks[2], (E, 2 * I, H), jnp.float32) * sc(H), 'expert_down_w': jax.random.normal(ks[3], (E, H, I), jnp.float32) * sc(I), 'shared_up_w': jax.random.normal(ks[4], (2 * SI, H), jnp.float32) * sc(H), 'shared_down_w': jax.random.normal(ks[5], (H, SI), jnp.float32) * sc(SI)}
    _L0_ffn_in = _L0_ffn_setup()
    _L0_c = _w((lambda *s: np.random.randn(*s).astype(np.float32) * 0.05)(2, 256))
    _L0_wmod = _w((lambda *s: np.random.randn(*s).astype(np.float32) * 0.05)(256, 6 * 256) * 256 ** (-0.5))
    _d = {'L0_attn_x': _L0_attn_in['x'], 'L0_attn_W_qkv': _L0_attn_in['W_qkv'], 'L0_attn_b_qkv': _L0_attn_in['b_qkv'], 'L0_attn_W_out': _L0_attn_in['W_out'], 'L0_attn_b_out': _L0_attn_in['b_out'], 'L0_ffn_gate_w': _L0_ffn_in['gate_w'], 'L0_ffn_expert_up_w': _L0_ffn_in['expert_up_w'], 'L0_ffn_expert_down_w': _L0_ffn_in['expert_down_w'], 'L0_ffn_shared_up_w': _L0_ffn_in['shared_up_w'], 'L0_ffn_shared_down_w': _L0_ffn_in['shared_down_w'], 'L0_c': _L0_c, 'L0_wmod': _L0_wmod}
    _x0 = _d['L0_attn_x']
    _d['L0_attn_x'] = jax.random.normal(jax.random.fold_in(jax.random.key(seed), 1), (2, 1024, 256), dtype=_x0.dtype)
    del _x0
    return _d

def reference(L0_attn_x, L0_attn_W_qkv, L0_attn_b_qkv, L0_attn_W_out, L0_attn_b_out, L0_ffn_gate_w, L0_ffn_expert_up_w, L0_ffn_expert_down_w, L0_ffn_shared_up_w, L0_ffn_shared_down_w, L0_c, L0_wmod):

    def _L0_attn_ref(x, W_qkv, b_qkv, W_out, b_out):
        import jax, jax.numpy as jnp
        import numpy as np
        HIDDEN = 256
        NUM_HEADS = 16
        HEAD_DIM = HIDDEN // NUM_HEADS
        B, S, H = x.shape
        qkv = x @ W_qkv.T + b_qkv
        q, k, v = jnp.split(qkv, 3, axis=-1)

        def to_heads(t):
            return t.reshape(B, S, NUM_HEADS, HEAD_DIM).transpose(0, 2, 1, 3)
        q, k, v = (to_heads(q), to_heads(k), to_heads(v))
        scale = HEAD_DIM ** (-0.5)
        scores = jnp.einsum('bnqd,bnkd->bnqk', q, k) * scale
        causal = jnp.triu(jnp.ones((S, S), dtype=bool), k=1)
        scores = jnp.where(causal, -jnp.inf, scores)
        attn = jax.nn.softmax(scores, axis=-1)
        out = jnp.einsum('bnqk,bnkd->bnqd', attn, v)
        out = out.transpose(0, 2, 1, 3).reshape(B, S, H)
        return out @ W_out.T + b_out

    def _L0_ffn_ref(x, gate_w, expert_up_w, expert_down_w, shared_up_w, shared_down_w):
        import jax, jax.numpy as jnp
        import numpy as np
        H = 256
        I = 176
        E = 16
        G = 4
        TOPK_GROUP = 2
        K = 4
        SI = 2 * I
        SCALE = 1.0
        NORM = True
        B, S = (4, 64)

        def _swiglu(h):
            g, u = jnp.split(h, 2, axis=-1)
            return jax.nn.silu(g) * u

        def _combine_weights(xt, gate_w):
            T = xt.shape[0]
            scores = jax.nn.softmax(xt @ gate_w.T, axis=-1)
            group_scores = scores.reshape(T, G, E // G).max(axis=-1)
            _, gidx = jax.lax.top_k(group_scores, TOPK_GROUP)
            gmask = jnp.zeros((T, G), bool).at[jnp.arange(T)[:, None], gidx].set(True)
            emask = jnp.repeat(gmask, E // G, axis=1)
            masked = jnp.where(emask, scores, 0.0)
            w, eidx = jax.lax.top_k(masked, K)
            if NORM:
                w = w / (w.sum(-1, keepdims=True) + 1e-20)
            w = w * SCALE
            return jnp.zeros((T, E), xt.dtype).at[jnp.arange(T)[:, None], eidx].add(w)
        Bq, Sq, _ = x.shape
        xt = x.reshape(-1, H)
        cw = _combine_weights(xt, gate_w)
        out = jnp.zeros_like(xt)
        for e in range(E):
            a = _swiglu(xt @ expert_up_w[e].T)
            out = out + cw[:, e:e + 1] * (a @ expert_down_w[e].T)
        out = out + _swiglu(xt @ shared_up_w.T) @ shared_down_w.T
        return out.reshape(Bq, Sq, H)
    x = L0_attn_x
    mod = (_silu(L0_c) @ L0_wmod).reshape(L0_c.shape[0], 6, 1, -1)
    sa, ca, ga, sb, cb, gb = (mod[:, 0], mod[:, 1], mod[:, 2], mod[:, 3], mod[:, 4], mod[:, 5])
    ga = (2 * (ga >= 0) - 1) * jnp.maximum(jnp.abs(ga), 0.25)
    gb = (2 * (gb >= 0) - 1) * jnp.maximum(jnp.abs(gb), 0.25)
    h = _layernorm(x, axis=-1) * (1 + ca) + sa
    x = x + ga * _L0_attn_ref(h, L0_attn_W_qkv, L0_attn_b_qkv, L0_attn_W_out, L0_attn_b_out)
    h = _layernorm(x, axis=-1) * (1 + cb) + sb
    x = x + gb * _L0_ffn_ref(h, L0_ffn_gate_w, L0_ffn_expert_up_w, L0_ffn_expert_down_w, L0_ffn_shared_up_w, L0_ffn_shared_down_w)
    return x

_drawn_inputs = setup_inputs


def setup_inputs(seed=0):
    import zlib

    import numpy as np

    out = dict(_drawn_inputs(seed))
    spreads = {'L0_attn_b_qkv': (0.0, 0.309), 'L0_attn_b_out': (0.0, 0.303)}
    factors = {'L0_attn_W_qkv': 2.676}
    for name, (base, spread) in spreads.items():
        noise = np.random.default_rng([zlib.crc32(name.encode()), seed]).standard_normal(out[name].shape)
        drawn = base * np.exp(spread * noise) if base else spread * noise
        out[name] = jnp.asarray(drawn.astype(out[name].dtype))
    for name, factor in factors.items():
        out[name] = (out[name] * factor).astype(out[name].dtype)
    return out
```

```python
from contextlib import ExitStack

import concourse.bass as bass
from concourse import mybir

F32 = mybir.dt.float32
BF16 = mybir.dt.bfloat16
ALU = mybir.AluOpType
ACT = mybir.ActivationFunctionType
AX = mybir.AxisListType

P = 128
B, S, H = 2, 1024, 256
NH, HD = 16, 16
T = B * S
KH = H // P
NT = T // P
CH = 512
NC = T // CH
TPC = CH // P
HG = 4
NG = NH // HG
NIT = B * NG
KT = S // P
EPS = 1e-5
SCALE = float(HD) ** -0.5
NEG = -1.0e30
F32R = mybir.dt.float32r

NE, EI = 16, 176
NGR, TOPG, TOPK = 4, 2, 4
EPG = NE // NGR
SI = 2 * EI
NSH = -(-SI // P)
NRT = NE * EI // P
NFT = NSH + NRT
WF = 2 * KH * P + H
PROWS = 32
WRING = 5
AHEAD = 2
assert NFT % WRING == 0
ROUTE_STEPS = 30
SLOTS = 3

Q_PARTS = (0, 1, 2, 0, 1, 0)
K_PARTS = (0, 0, 0, 1, 1, 2)
NPR = len(Q_PARTS) * HD
NAUG = NPR + 3
STAGE_DMAS = 3 * len(Q_PARTS) + 1

ROWS = [(i, True, 0, (i + 1) * P) for i in range(TPC)]
for _i in range(TPC, KT):
    ROWS += [(_i, False, 0, CH), (_i, True, CH, (_i + 1) * P - CH)]
STEPS = [(qc, kt) for qc in range(S // CH) for kt in range(TPC * (qc + 1))]
NS = len(STEPS)
UNITS = len(ROWS) * HG
assert len(ROWS) == NS


def on_diagonal(s):
    qc, kt = STEPS[s]
    return kt >= TPC * qc


def program(nc, x, wqk, bqk, wv, bv, wout, bout, cT, wmod, wgate, wffn, qkd, out):
    with ExitStack() as ctx:
        scope = [ctx]

        def sb(name, shape, dt):
            return scope[-1].enter_context(nc.sbuf_tensor(name, shape, dt))

        def sem(name):
            return ctx.enter_context(nc.semaphore(name))

        X = sb("X", [P, NT, H], F32)
        Wo = sb("Wo", [P, KH, H], F32)
        Bo = sb("Bo", [P, H], F32)
        cS = sb("cS", [P, KH, B], F32)
        cE = sb("cE", [P, 3, KH, B], F32)
        modT = sb("modT", [P, 10, B], F32)
        gbS, gbN, gbA = (sb(n, [P, KH, B], F32) for n in ("gbS", "gbN", "gbA"))
        gate = sb("gate", [P, B, H], F32)
        ident = sb("ident", [P, P], F32)
        identb = sb("identb", [P, P], BF16)
        mask = sb("mask", [P, P], BF16)
        maskT = sb("maskT", [P, P], BF16)
        stats = sb("stats", [P, 2, NT, 6], F32)
        mv = sb("mv", [P, 2, NT, 2], F32)
        vare, rvar, rstd = (sb(n, [P, 2, NT], F32) for n in ("vare", "rvar", "rstd"))

        scope.append(ctx.enter_context(ExitStack()))
        hT = sb("hT", [P, KH, T], F32)
        Vall = sb("Vall", [P, NIT, KT, HG, 32], F32)
        Vst = [sb(f"Vst{i}", [P, KT, HG * 32], F32) for i in range(SLOTS)]
        Qs = [sb(f"Qs{i}", [P, S // CH, HG, CH], BF16) for i in range(SLOTS)]
        Ks = [sb(f"Ks{i}", [P, HG, S], BF16) for i in range(SLOTS)]
        AP = sb("AP", [P, 2, 3, 4, CH], BF16)
        PT = [AP[:, i] for i in range(2)]
        A = AP[:, :, :, :, :].rearrange("p i a m c -> p (i a m c)").bitcast(F32)[:, 0:NIT * CH].rearrange(
            "p (q t n d) -> p q t n d", n=NIT, q=S // CH, t=TPC)
        Pr = [sb(f"Pr{i}", [P, 2, CH], F32) for i in range(4)]
        OT = [sb(f"OT{i}", [P, CH], F32) for i in range(2)]
        xn = [Pr[i][:, :, :].rearrange("p a (t h) -> p (a t) h", h=H) for i in range(2)]
        Fq = [Pr[2 + m // 2][:, m % 2, :] for m in range(4)]
        AT = [Pr[i] for i in range(2)]
        Rq = [sb(f"Rq{i}", [P, CH], F32) for i in range(2)]
        Wqk = sb("Wqk", [P, KH, 2 * H], F32)
        Wv = sb("Wv", [P, KH, H], F32)
        Wm = sb("Wm", [P, KH, 6 * H], F32)
        Bqk = sb("Bqk", [P, 4], F32)
        Bv = sb("Bv", [P, H], F32)
        cB = sb("cB", [P, KH, B, P], F32)
        gsgn, gneg, gabs = (Vst[i][:, 0:KT // 2, :].rearrange("p k (b h) -> p (k b h)", b=1).rearrange(
            "p (b h) -> p b h", b=B) for i in range(3))
        gbias = sb("gbias", [P, B, H], F32)
        gy = sb("gy", [P, 2, H], F32)
        mxA = sb("mxA", [P, KT, HG], F32)
        mxB = sb("mxB", [P, TPC, HG], F32)
        mr = sb("mr", [P, HG, TPC], F32)
        MP = sb("MP", [P, 3, HG, TPC], BF16)
        MT = [sb(f"MT{i}", [3 * HG * TPC, P], BF16) for i in range(2)]
        R = sb("R", [P, TPC, HG], F32)
        scope.pop().close()

        Hh = sb("Hh", [P, KH, T], F32R)
        Hl = sb("Hl", [P, KH, T], F32R)
        Wr = [sb(f"Wr{i}", [P, WF], F32) for i in range(WRING)]
        Wh = [sb(f"Wh{i}", [P, WF], F32R) for i in range(WRING)]
        Wl = [sb(f"Wl{i}", [P, WF], F32R) for i in range(WRING)]
        xm = [sb(f"xm{i}", [P, TPC, H], F32) for i in range(2)]
        hv = [sb(f"hv{i}", [P, KH, CH], F32) for i in range(2)]
        Wg = sb("Wg", [P, KH, NE], F32)
        lower = sb("lower", [P, NE, NE], F32)
        lowg = sb("lowg", [P, NGR, NGR], F32)
        sel = sb("sel", [3 * PROWS, NRT, P], BF16)
        CP = sb("CP", [P, NT, 3, PROWS], BF16)
        CWT = sb("CWT", [3 * PROWS, T], BF16)
        rt = {name: sb("rt_" + name, [P, TPC] + shape, F32) for name, shape in (
            ("max", []), ("sum", []), ("rec", []), ("logit", [NE]), ("exp", [NE]), ("score", [NE]), ("group", [NGR]),
            ("ggt", [NGR, NGR]), ("geq", [NGR, NGR]), ("gtie", [NGR, NGR]), ("gcmp", [NGR, NGR]), ("grank", [NGR]),
            ("gsel", [NGR]), ("kept", [NE]), ("masked", [NE]), ("gt", [NE, NE]), ("eq", [NE, NE]), ("tie", [NE, NE]),
            ("cmp", [NE, NE]), ("rank", [NE]), ("w", [NE]), ("wsum", []), ("weps", []), ("wrec", []), ("cw", [NE]), ("rem", [NE]))}
        sg = [sb(f"sg{i}", [P, CH], F32) for i in range(2)]
        su = [sb(f"su{i}", [P, CH], F32) for i in range(2)]
        sw = [sb(f"sw{i}", [P, CH], F32) for i in range(2)]
        ah = [sb(f"ah{i}", [P, CH], F32R) for i in range(2)]
        al = [sb(f"al{i}", [P, CH], F32R) for i in range(2)]
        Ys = sb("Ys", [P, KH, CH], F32)
        gbC = sb("gbC", [P, KH, NC], F32)

        bank = [ctx.enter_context(nc.psum_tensor(f"bank{i}", [P, CH], F32)) for i in range(2)]
        epair = [ctx.enter_context(nc.psum_tensor(f"epair{i}", [P, 2, CH], F32)) for i in range(2)]
        pvb = ctx.enter_context(nc.psum_tensor("pvb", [P, CH], F32))
        tb = ctx.enter_context(nc.psum_tensor("tb", [P, CH], F32))
        allb = [bank[0][:, :], bank[1][:, :], epair[0][:, 0, :], epair[0][:, 1, :],
                epair[1][:, 0, :], epair[1][:, 1, :], pvb[:, :], tb[:, :]]

        x_in = [sem(f"x_in{c}") for c in range(NC)]
        w_in = sem("w_in")
        const_done = sem("const_done")
        negc_exp = sem("negc_exp")
        silu_c = sem("silu_c")
        mod_ps = sem("mod_ps")
        mod_read = sem("mod_read")
        gate_ps = sem("gate_ps")
        gate_step = sem("gate_step")
        ln_step = sem("ln_step")
        rstd_done = sem("rstd_done")
        xn_ready = sem("xn_ready")
        xnT_ps = sem("xnT_ps")
        hT_ready = sem("hT_ready")
        qk_ps = sem("qk_ps")
        qk_read = sem("qk_read")
        parts_done = sem("parts_done")
        split_step = sem("split_step")
        parts_out = [sem(f"parts_out{i}") for i in range(2)]
        v_ps = sem("v_ps")
        v_read = sem("v_read")
        staged = [sem(f"staged{i}") for i in range(SLOTS)]
        m_ps = sem("m_ps")
        m_red = sem("m_red")
        mp_step = sem("mp_step")
        mpT_ps = sem("mpT_ps")
        t_read = sem("t_read")
        aug_in = [[sem(f"aug_in{i}_{h}") for h in range(2)] for i in range(SLOTS)]
        e_ps = sem("e_ps")
        exp_done = sem("exp_done")
        pv_done = sem("pv_done")
        ot_ready = sem("ot_ready")
        oT_ps = sem("oT_ps")
        rec_done = sem("rec_done")
        aT_ps = sem("aT_ps")
        aT_ready = sem("aT_ready")
        y_ps = sem("y_ps")
        xb_ready = sem("xb_ready")
        x1g = sem("x1g")
        x1_ready = sem("x1_ready")
        out_done = sem("out_done")
        fconst = sem("fconst")
        wg_in = sem("wg_in")
        x2T_ps = sem("x2T_ps")
        h2_ready = sem("h2_ready")
        h2_hi = sem("h2_hi")
        h2_split = sem("h2_split")
        logit_ps = sem("logit_ps")
        logit_read = sem("logit_read")
        rexp_done = sem("rexp_done")
        route_step = sem("route_step")
        cwT_ps = sem("cwT_ps")
        cwT_ready = sem("cwT_ready")
        w_raw = [sem(f"w_raw{i}") for i in range(WRING)]
        w_hi = sem("w_hi")
        w_lo = sem("w_lo")
        cwb_ps = sem("cwb_ps")
        silu_done = sem("silu_done")
        u_read = sem("u_read")
        u_ps = sem("u_ps")
        g_ps = sem("g_ps")
        hi_done = sem("hi_done")
        cwb_read = sem("cwb_read")
        a_ready = sem("a_ready")
        down_done = sem("down_done")
        y_read = sem("y_read")
        yT_ps = sem("yT_ps")
        fin_done = sem("fin_done")

        W_DMAS = 8
        N_CONST = 4 + SLOTS + 5
        block = ctx.enter_context(nc.Block())

        def t_event(n, kind):
            last = isinstance(n, int) and n == NIT - 1
            return n * 4 + {"max1": 2, "out1": 3, "max0": 4, "out0": 4 if last else 5}[kind]

        def attention(body):
            def place(n, k=0):
                return lambda d=0: ((n + d) % SLOTS, k + (n + d) // SLOTS)

            def run(eng):
                body(-1, place(-1), True, False)
                body(0, place(0), True, False)
                with eng.Fori(0, (NIT - 2) // SLOTS) as k:
                    for j in range(SLOTS):
                        body(k * SLOTS + (1 + j), place(1 + j, k), False, False)
                body(NIT - 1, place(NIT - 1), False, True)
            return run

        def attention_loads(body):
            def run(eng):
                body(-1, 2, False)
                with eng.Fori(0, (NIT - 2) // SLOTS) as k:
                    for j in range(SLOTS):
                        body(k * SLOTS + j, j, True)
                for n in (NIT - 2, NIT - 1):
                    body(n, n % SLOTS, False)
            return run

        @block.sync
        def _(sp):
            for c in range(NC):
                sp.dma_start(X[:, c * TPC:(c + 1) * TPC, :],
                             x[c * CH:(c + 1) * CH, :].rearrange("(t p) h -> p t h", p=P)).then_inc(x_in[c], 16)
                if c == 0:
                    sp.dma_start(cS[:, :, :], cT).then_inc(w_in, 16)
                    sp.dma_start(Wm[:, :, :], wmod).then_inc(w_in, 16)
            sp.dma_start(Wqk[:, :, :], wqk).then_inc(w_in, 16)
            sp.dma_start(Bqk[:, :], bqk).then_inc(w_in, 16)
            sp.dma_start(Wv[:, :, :], wv).then_inc(w_in, 16)
            sp.dma_start(Bv[:, :], bv.rearrange("(a n) -> a n", a=1).broadcast_to([P, H])).then_inc(w_in, 16)
            sp.dma_start(Wo[:, :, :], wout).then_inc(w_in, 16)
            sp.dma_start(Bo[:, :], bout.rearrange("(a n) -> a n", a=1).broadcast_to([P, H])).then_inc(w_in, 16)
            for c in range(NC):
                sp.wait_ge(parts_done, 4 * (c + 1))
                b, half = c // (S // CH), c % (S // CH)
                for part in range(3):
                    for m in range(4):
                        sp.dma_start(qkd[part, m // KH, b, (m % KH) * P:(m % KH + 1) * P, half * CH:(half + 1) * CH],
                                     PT[c % 2][:, part, m, :]).then_inc(parts_out[c % 2], 16)
            for i in range(2):
                sp.wait_ge(parts_out[i], 16 * 12 * (NC // 2))
            sp.wait_ge(v_read, 2 * NC)

            def stage(n, slot):
                for blk in range(len(Q_PARTS)):
                    q, k = (qkd[part, t].rearrange("b (g j d) s -> (b g) d j s", g=NG, j=HG)[bass.ds(n, 1)].rearrange(
                        "a d j s -> (a d) j s") for t, part in ((0, Q_PARTS[blk]), (1, K_PARTS[blk])))
                    rows = slice(blk * HD, (blk + 1) * HD)
                    for half in range(S // CH):
                        sp.dma_start(Qs[slot][rows, half, :, :], q[:, :, half * CH:(half + 1) * CH]).then_inc(staged[slot], 16)
                    sp.dma_start(Ks[slot][rows, :, :], k).then_inc(staged[slot], 16)
                sp.dma_start(Vst[slot][:, :, :],
                             Vall[:, bass.ds(n, 1), :, :, :].rearrange("p a k j d -> p (a k) (j d)")).then_inc(staged[slot], 16)

            def aug(slot, half):
                for part in range(3):
                    sp.dma_start(
                        Qs[slot][NPR + part:NPR + part + 1, half, :, :].rearrange("o j (i q) -> o (j i) q", i=TPC),
                        MT[half][part * HG * TPC:(part + 1) * HG * TPC, :]
                    ).then_inc(aug_in[slot][half], 16)

            def body(n, slot, stages):
                if isinstance(n, int) and n == -1:
                    for s in range(SLOTS - 1):
                        stage(s, s)
                    sp.wait_ge(t_read, 1)
                    aug(0, 0)
                    return
                sp.wait_ge(t_read, t_event(n, "max1") + 1)
                aug(slot, 1)
                if stages:
                    sp.wait_ge(e_ps, n * (2 * NS) + 1)
                    sp.wait_ge(pv_done, n * NS + 1)
                    stage(n + (SLOTS - 1), (slot + SLOTS - 1) % SLOTS)
                if not (isinstance(n, int) and n == NIT - 1):
                    sp.wait_ge(t_read, t_event(n, "max0") + 1)
                    aug((slot + 1) % SLOTS, 0)

            attention_loads(body)(sp)

            sp.wait_ge(x1_ready, NT)
            sp.dma_start(Wg[:, :, :], wgate).then_inc(wg_in, 16)

            def ffn(c):
                for f in range(NFT):
                    r = f % WRING
                    if not (isinstance(c, int) and c == 0 and f < WRING):
                        sp.wait_ge(w_hi, c * NFT + (f - WRING + 1))
                        sp.wait_ge(w_lo, c * NFT + (f - WRING + 1))
                    sp.dma_start(Wr[r][:, :], wffn[f]).then_inc(w_raw[r], 16)
                    if f == 12 and not (isinstance(c, int) and c == 0):
                        store(c - 1)

            def store(c):
                sp.wait_ge(fin_done, c * 2 + 2)
                sp.dma_start(out[bass.ds(c * CH, CH), :].rearrange("(t p) h -> p t h", p=P),
                             X[:, bass.ds(c * TPC, TPC), :]).then_inc(out_done, 16)

            ffn(0)
            with sp.Fori(1, NC) as c:
                ffn(c)
            store(NC - 1)
            sp.wait_ge(out_done, 16 * NC)

        @block.gpsimd
        def _(pool):
            nc.gpsimd.memset(ident[:, :], 0.0).then_inc(const_done, 1)
            nc.gpsimd.memset(mask[:, :], 0.0).then_inc(const_done, 1)
            nc.gpsimd.memset(maskT[:, :], 0.0).then_inc(const_done, 1)
            nc.gpsimd.memset(Vall[:, :, :, :, HD:32], 0.0).then_inc(const_done, 1)
            pool.wait_ge(const_done, 4)
            for i in range(SLOTS):
                nc.gpsimd.memset(Ks[i][NPR:P, :, :], 1.0).then_inc(const_done, 1)
            pool.wait_ge(const_done, 4 + SLOTS)
            nc.gpsimd.affine_select(out=ident[:, :], in_=ident[:, :], compare_op=ALU.not_equal, fill=1.0,
                                    base=0, pattern=[[-1, P]], channel_multiplier=1).then_inc(const_done, 1)
            nc.gpsimd.affine_select(out=mask[:, :], in_=mask[:, :], compare_op=ALU.is_ge, fill=NEG,
                                    base=0, pattern=[[-1, P]], channel_multiplier=1).then_inc(const_done, 1)
            nc.gpsimd.affine_select(out=maskT[:, :], in_=maskT[:, :], compare_op=ALU.is_ge, fill=NEG,
                                    base=0, pattern=[[1, P]], channel_multiplier=-1).then_inc(const_done, 1)
            nc.gpsimd.memset(Vall[:, :, :, :, HD:HD + 1], 1.0).then_inc(const_done, 1)
            pool.wait_ge(const_done, 4 + SLOTS + 4)
            nc.gpsimd.tensor_copy(identb[:, :], ident[:, :]).then_inc(const_done, 1)

            pool.wait_ge(x1_ready, NT)
            nc.gpsimd.memset(CP[:, :, :, :], 0.0).then_inc(fconst, 1)
            nc.gpsimd.memset(lower[:, :, :], 0.0).then_inc(fconst, 1)
            nc.gpsimd.memset(lowg[:, :, :], 0.0).then_inc(fconst, 1)
            pool.wait_ge(fconst, 3)
            nc.gpsimd.affine_select(out=lower[:, :, :], in_=lower[:, :, :], compare_op=ALU.is_ge, fill=1.0,
                                    base=0, pattern=[[-1, NE], [1, NE]], channel_multiplier=0).then_inc(fconst, 1)
            nc.gpsimd.affine_select(out=lowg[:, :, :], in_=lowg[:, :, :], compare_op=ALU.is_ge, fill=1.0,
                                    base=0, pattern=[[-1, NGR], [1, NGR]], channel_multiplier=0).then_inc(fconst, 1)
            nc.gpsimd.memset(sel[:, :, :], 1.0).then_inc(fconst, 1)
            pool.wait_ge(fconst, 6)
            for part in range(3):
                v = sel[part * PROWS:(part + 1) * PROWS, :, :]
                nc.gpsimd.affine_select(out=v, in_=v, compare_op=ALU.is_ge, fill=0.0, base=0,
                                        pattern=[[P, NRT], [1, P]], channel_multiplier=-EI).then_inc(fconst, 1)
                pool.wait_ge(fconst, 6 + 2 * part + 1)
                nc.gpsimd.affine_select(out=v, in_=v, compare_op=ALU.is_ge, fill=0.0, base=EI - 1,
                                        pattern=[[-P, NRT], [-1, P]], channel_multiplier=EI).then_inc(fconst, 1)
                pool.wait_ge(fconst, 6 + 2 * part + 2)

            def ffn(c):
                for f in range(NFT):
                    r = f % WRING
                    pool.wait_ge(w_hi, c * NFT + (f + 1))
                    if not (isinstance(c, int) and c == 0 and f < WRING):
                        pool.wait_ge(down_done, c * NFT + (f - WRING + 1))
                    nc.gpsimd.tensor_tensor(Wl[r][:, :], Wr[r][:, :], Wh[r][:, :].bitcast(F32), ALU.subtract).then_inc(w_lo, 1)

            ffn(0)
            with pool.Fori(1, NC) as c:
                ffn(c)

        @block.scalar
        def _(act):
            act.wait_ge(w_in, 16 * W_DMAS)
            nc.scalar.activation(cE[:, 0], cS[:, :, :], ACT.Exp, scale=-1.0).then_inc(negc_exp, 1)
            act.wait_ge(ln_step, 2 * NT + 2)
            nc.scalar.activation(rstd[:, 0, :], rvar[:, 0, :], ACT.Sqrt).then_inc(rstd_done, 1)

            def hT_evict(c):
                b = c // (S // CH)
                for k in range(KH):
                    n = KH * c + k
                    act.wait_ge(xnT_ps, n + 1)
                    if n == 0:
                        act.wait_ge(mod_read, 2)
                    nc.scalar.activation(hT[:, k, c * CH:(c + 1) * CH], allb[k], ACT.Identity,
                                         scale=modT[:, 2 + k, b:b + 1], bias=modT[:, k, b:b + 1]).then_inc(hT_ready, 1)
            hT_evict(0)
            for c in range(NC):
                if c + 1 < NC:
                    hT_evict(c + 1)
                for m in range(4):
                    n = 4 * c + m
                    act.wait_ge(qk_ps, n + 1)
                    if n >= 4:
                        act.wait_ge(parts_done, n - 3)
                    nc.scalar.activation(Fq[m], allb[2 + m], ACT.Identity,
                                         bias=Bqk[:, m:m + 1]).then_inc(qk_read, 1)
                    if c >= 2:
                        act.wait_ge(parts_out[c % 2], 16 * 12)
                    nc.scalar.activation(PT[c % 2][:, 0, m, :], allb[2 + m], ACT.Identity,
                                         bias=Bqk[:, m:m + 1]).then_inc(qk_read, 1)

            def evict(o, qc):
                act.wait_ge(pv_done, (o - qc) * (NS // 2) + (TPC if qc == 0 else NS))
                if not (isinstance(o, int) and o < 2):
                    act.wait_ge(oT_ps, o - 1)
                nc.scalar.activation(OT[qc][:, :], pvb[:, :], ACT.Copy).then_inc(ot_ready, 1)

            def body(n, at, first, last):
                if isinstance(n, int) and n == -1:
                    return
                for s in range(NS):
                    qc, kt = STEPS[s]
                    w = CH - (max(0, kt - TPC * qc)) * P
                    for pair in range(2):
                        act.wait_ge(e_ps, n * (2 * NS) + (2 * s + pair + 1))
                        if not (first and s < 2):
                            act.wait_ge(pv_done, n * NS + (s - 1))
                        nc.scalar.activation(Pr[(2 * s + pair) % 4][:, :, 0:w], epair[pair][:, :, 0:w],
                                             ACT.Exp, scale=SCALE).then_inc(exp_done, 1)
                    if s == 0 and not first:
                        evict(n * 2 - 1, 1)
                    if s == TPC:
                        evict(n * 2, 0)
            attention(body)(act)
            evict(2 * NIT - 1, 1)

            for c in range(NC):
                for k in range(KH):
                    n = KH * c + k
                    act.wait_ge(aT_ps, n + 1)
                    if c >= 2:
                        act.wait_ge(y_ps, TPC * (c - 1))
                    nc.scalar.activation(AT[c % 2][:, k, :], allb[k], ACT.Copy).then_inc(aT_ready, 1)

            act.wait_ge(ln_step, 2 * (2 * NT + 2))
            nc.scalar.activation(rstd[:, 1, :], rvar[:, 1, :], ACT.Sqrt).then_inc(rstd_done, 1)

            for c in range(NC):
                b = c // (S // CH)
                for k in range(KH):
                    act.wait_ge(x2T_ps, KH * c + k + 1)
                    if c >= 2:
                        act.wait_ge(h2_split, KH * (c - 2) + k + 1)
                        act.wait_ge(logit_ps, c - 1)
                    nc.scalar.activation(hv[c % 2][:, k, :], allb[k], ACT.Identity,
                                         scale=modT[:, 6 + k, b:b + 1], bias=modT[:, 4 + k, b:b + 1]).then_inc(h2_ready, 1)
                act.wait_ge(route_step, c * ROUTE_STEPS + 2)
                nc.scalar.activation(rt["exp"][:, :, :], rt["logit"][:, :, :], ACT.Exp).then_inc(rexp_done, 1)

            def split_weights(c, f):
                r = f % WRING
                act.wait_ge(w_raw[r], c * (16 * (NFT // WRING)) + 16 * (f // WRING + 1))
                if not (isinstance(c, int) and c == 0 and f < WRING):
                    act.wait_ge(down_done, c * NFT + (f - WRING + 1))
                nc.scalar.activation(Wh[r][:, :], Wr[r][:, :], ACT.Copy).then_inc(w_hi, 1)

            def scale_out(c):
                act.wait_ge(down_done, c * NFT + NFT)
                if not (isinstance(c, int) and c == 0):
                    act.wait_ge(yT_ps, c * 2)
                for k in range(KH):
                    nc.scalar.activation(Ys[:, k, :], allb[5 + k], ACT.Copy,
                                         scale=gbC[:, k, bass.ds(c, 1)]).then_inc(y_read, 1)

            def ffn(c, last):
                for f in range(NFT):
                    act.wait_ge(g_ps, c * NFT + (f + 1))
                    if not (isinstance(c, int) and c == 0 and f < 2):
                        act.wait_ge(u_read, c * NFT + (f if f == 0 else f - 1))
                    nc.scalar.activation(sg[f % 2][:, :], allb[2 * (f % 2)], ACT.Silu).then_inc(silu_done, 1)
                    if f == 0 and not (isinstance(c, int) and c == 0):
                        scale_out(c - 1)
                    if f + AHEAD < NFT or not last:
                        split_weights(c, f + AHEAD)

            for f in range(AHEAD):
                split_weights(0, f)
            ffn(0, False)
            with act.Fori(1, NC - 1) as c:
                ffn(c, False)
            ffn(NC - 1, True)
            scale_out(NC - 1)

        @block.vector
        def _(dve):
            def statistics(which):
                k = which * (2 * NT + 2)
                for t in range(NT):
                    if which == 0 and t % TPC == 0:
                        dve.wait_ge(x_in[t // TPC], 16)
                    if which == 1:
                        dve.wait_ge(x1_ready, t + 1)
                    nc.vector.bn_stats(stats[:, which, t, :], X[:, t, :]).then_inc(ln_step, 1)
                for t in range(NT):
                    dve.wait_ge(ln_step, k + t + 1)
                    nc.vector.bn_aggr(mv[:, which, t, :], stats[:, which, t, :]).then_inc(ln_step, 1)
                dve.wait_ge(ln_step, k + 2 * NT)
                nc.vector.tensor_scalar(vare[:, which, :], mv[:, which, :, 1], EPS, None, ALU.add).then_inc(ln_step, 1)
                dve.wait_ge(ln_step, k + 2 * NT + 1)
                nc.vector.reciprocal(rvar[:, which, :], vare[:, which, :]).then_inc(ln_step, 1)

            statistics(0)

            def normalise_tokens(which, c, dst):
                for t in range(c * TPC, (c + 1) * TPC):
                    nc.vector.tensor_scalar(dst[:, t - c * TPC, :], X[:, t, :], mv[:, which, t, 0:1], rstd[:, which, t:t + 1],
                                            ALU.subtract, ALU.mult).then_inc(xn_ready, 1)

            dve.wait_ge(negc_exp, 1)
            nc.vector.tensor_scalar(cE[:, 1], cE[:, 0], 1.0, None, ALU.add).then_inc(silu_c, 1)
            dve.wait_ge(silu_c, 1)
            nc.vector.reciprocal(cE[:, 2], cE[:, 1]).then_inc(silu_c, 1)
            dve.wait_ge(silu_c, 2)
            nc.vector.tensor_tensor(cS[:, :, :], cS[:, :, :], cE[:, 2], ALU.mult).then_inc(silu_c, 1)
            dve.wait_ge(silu_c, 3)
            nc.vector.tensor_copy(cB[:, :, :, :], cS[:, :, :].unsqueeze(3).broadcast_to([P, KH, B, P])).then_inc(silu_c, 1)
            dve.wait_ge(rstd_done, 1)
            normalise_tokens(0, 0, xn[0])
            dve.wait_ge(mod_ps, 1)
            for n in range(2):
                nc.vector.tensor_copy(modT[:, 4 * n:4 * n + 2, :],
                                      allb[7][:, 8 * n:8 * n + 4].rearrange("p (m b) -> p m b", b=B)).then_inc(mod_read, 1)
                ins = nc.vector.tensor_scalar(modT[:, 4 * n + 2:4 * n + 4, :],
                                              allb[7][:, 8 * n + 4:8 * n + 8].rearrange("p (m b) -> p m b", b=B),
                                              1.0, None, ALU.add)
                ins.then_inc(mod_read, 1)
            nc.vector.tensor_copy(modT[:, 8:10, :], allb[7][:, 16:20].rearrange("p (m b) -> p m b", b=B)).then_inc(mod_read, 1)
            dve.wait_ge(gate_ps, 1)
            dve.wait_ge(mod_read, 5)
            ps = allb[5].rearrange("p (b h) -> p b h", b=B)
            for g, sgn, neg in ((ps, gsgn, gneg), (modT[:, 8:10, :], gbS[:, :, :], gbN[:, :, :])):
                nc.vector.tensor_scalar(sgn, g, 0.0, 2.0, ALU.is_ge, ALU.mult).then_inc(gate_step, 1)
                nc.vector.tensor_scalar(neg, g, -1.0, 0.25, ALU.mult, ALU.max).then_inc(gate_step, 1)
            dve.wait_ge(gate_step, 4)
            nc.vector.tensor_tensor(gabs, ps, gneg, ALU.max).then_inc(gate_step, 1)
            nc.vector.tensor_tensor(gbA[:, :, :], modT[:, 8:10, :], gbN[:, :, :], ALU.max).then_inc(gate_step, 1)
            dve.wait_ge(gate_step, 6)
            for dst, sgn, mag in ((gate[:, :, :], gsgn, gabs), (modT[:, 8:10, :], gbS[:, :, :], gbA[:, :, :])):
                nc.vector.scalar_tensor_tensor(out=dst, in0=sgn, scalar=-1.0, in1=mag,
                                               op0=ALU.add, op1=ALU.mult).then_inc(gate_step, 1)

            for c in range(NC):
                if c + 1 < NC:
                    if c >= 1:
                        dve.wait_ge(xnT_ps, KH * c)
                    normalise_tokens(0, c + 1, xn[(c + 1) % 2])
                for m in range(4):
                    n = 4 * c + m
                    dve.wait_ge(qk_read, 2 * n + 2)
                    if n >= 2:
                        dve.wait_ge(parts_done, n - 1)
                    nc.vector.tensor_tensor(Rq[m % 2][:, :], Fq[m], PT[c % 2][:, 0, m, :], ALU.subtract).then_inc(split_step, 1)
                    dve.wait_ge(split_step, 2 * n + 1)
                    nc.vector.tensor_copy(PT[c % 2][:, 1, m, :], Rq[m % 2][:, :]).then_inc(split_step, 1)
                    dve.wait_ge(split_step, 2 * n + 2)
                    nc.vector.tensor_tensor(PT[c % 2][:, 2, m, :], Rq[m % 2][:, :], PT[c % 2][:, 1, m, :], ALU.subtract).then_inc(parts_done, 1)
                for v in range(2):
                    dve.wait_ge(v_ps, 2 * c + v + 1)
                    if c == 0 and v == 0:
                        dve.wait_ge(const_done, N_CONST)
                    b, kt = c // (S // CH), (c % (S // CH)) * TPC + 2 * v
                    for u in range(2):
                        ins = nc.vector.tensor_tensor(
                            Vall[:, b * NG:(b + 1) * NG, kt + u, :, 0:HD],
                            allb[6 + v][:, u * H:(u + 1) * H].rearrange("p (g j d) -> p g j d", g=NG, j=HG),
                            Bv[:, :].rearrange("p (g j d) -> p g j d", g=NG, j=HG), ALU.add)
                    ins.then_inc(v_read, 1)

            def score_row(n, r):
                i, diag, k0, w = ROWS[r]
                for j in range(HG):
                    dve.wait_ge(m_ps, n * UNITS + (HG * r + j + 1))
                    ps = bank[j % 2]
                    dst = mxA[:, i, j:j + 1] if diag else mxB[:, i - TPC, j:j + 1]
                    nc.vector.tensor_reduce(dst, ps[:, 0:w], AX.X, ALU.max).then_inc(m_red, 1)

            def max_parts(n, half):
                k = n * 9 + 4 * half
                src = mxA[:, half * TPC:(half + 1) * TPC, :]
                if half:
                    dve.wait_ge(m_red, n * UNITS + UNITS)
                    nc.vector.tensor_tensor(src, src, mxB[:, :, :], ALU.max).then_inc(mp_step, 1)
                    dve.wait_ge(mp_step, k + 1)
                    k = k + 1
                else:
                    dve.wait_ge(m_red, n * UNITS + TPC * HG)
                v = src.rearrange("p i j -> p j i")
                if not (isinstance(n, int) and n == 0 and half == 0):
                    dve.wait_ge(mp_step, k)
                nc.vector.tensor_scalar(MP[:, 0], v, -1.0, None, ALU.mult).then_inc(mp_step, 1)
                dve.wait_ge(mp_step, k + 1)
                nc.vector.scalar_tensor_tensor(out=mr[:, :, :], in0=v, scalar=-1.0, in1=MP[:, 0],
                                               op0=ALU.mult, op1=ALU.subtract).then_inc(mp_step, 1)
                dve.wait_ge(mp_step, k + 2)
                nc.vector.tensor_copy(MP[:, 1], mr[:, :, :]).then_inc(mp_step, 1)
                dve.wait_ge(mp_step, k + 3)
                nc.vector.tensor_tensor(MP[:, 2], mr[:, :, :], MP[:, 1], ALU.subtract).then_inc(mp_step, 1)

            def max_copy(n, half, before):
                dve.wait_ge(mpT_ps, n * 2 + (half + 1))
                if before is not None:
                    dve.wait_ge(aug_in[before[0]][half], before[1] * 48 + 48)
                nc.vector.tensor_copy(MT[half][:, :], tb[:, :].bitcast(BF16)[0:3 * HG * TPC, 0:P]).then_inc(
                    t_read, 2 if before is None else 1)

            def normalise(o, n, qc):
                ps = tb[:, :].rearrange("p (t j d) -> p t j d", t=TPC, j=HG)
                dve.wait_ge(oT_ps, o + 1)
                nc.vector.reciprocal(R[:, :, :], ps[:, :, :, HD]).then_inc(rec_done, 1)
                dve.wait_ge(rec_done, o + 1)
                dst = A[:, qc, :, bass.ds(n, 1), :].rearrange("p t a (j d) -> p (t a) j d", j=HG)
                nc.vector.tensor_tensor(dst, ps[:, :, :, 0:HD],
                                        R[:, :, :].unsqueeze(3).broadcast_to([P, TPC, HG, HD]), ALU.mult).then_inc(t_read, 1)

            def body(n, at, first, last):
                if isinstance(n, int) and n == -1:
                    for r in range(NS):
                        score_row(0, r)
                        if r == TPC:
                            max_parts(0, 0)
                        if r == 6:
                            max_copy(0, 0, None)
                    return
                max_parts(n, 1)
                for s in range(NS):
                    if not last:
                        score_row(n + 1, s)
                    if s == 1:
                        max_copy(n, 1, None if first else at(-1))
                    if s == 3 and not first:
                        normalise(n * 2 - 1, n - 1, 1)
                    if s == TPC and not last:
                        max_parts(n + 1, 0)
                    if s == 6 and not last:
                        max_copy(n + 1, 0, at(0))
                    if s == 8:
                        normalise(n * 2, n, 0)

            attention(body)(dve)
            normalise(2 * NIT - 1, NIT - 1, 1)

            for t in range(NT):
                b = t // KT
                if t % KT == 0:
                    nc.vector.tensor_tensor(gbias[:, b, :], gate[:, b, :], Bo[:, :], ALU.mult).then_inc(xb_ready, 1)
                    dve.wait_ge(xb_ready, KT * b + b + 1)
                nc.vector.tensor_tensor(X[:, t, :], X[:, t, :], gbias[:, b, :], ALU.add).then_inc(xb_ready, 1)
            dve.wait_ge(xb_ready, NT + B)
            for t in range(NT):
                b = t // KT
                dve.wait_ge(y_ps, t + 1)
                if t >= 2:
                    dve.wait_ge(x1_ready, t - 1)
                nc.vector.tensor_tensor(gy[:, t % 2, :], allb[4 + t % 4][:, 0:H], gate[:, b, :], ALU.mult).then_inc(x1g, 1)
                dve.wait_ge(x1g, t + 1)
                nc.vector.tensor_tensor(X[:, t, :], X[:, t, :], gy[:, t % 2, :], ALU.add).then_inc(x1_ready, 1)

            statistics(1)
            for c in range(NC):
                nc.vector.tensor_copy(gbC[:, :, c], modT[:, 8:10, c // (S // CH)]).then_inc(rec_done, 1)
            dve.wait_ge(rstd_done, 2)
            dve.wait_ge(fconst, 12)

            def routing(c):
                did = [c * ROUTE_STEPS]
                r = {k: (v[:, :, :] if len(v.shape) == 3 else v[:, :, :, :] if len(v.shape) == 4 else v[:, :])
                     for k, v in rt.items()}

                def step(ins):
                    did[0] += 1
                    ins.then_inc(route_step, 1)
                    dve.wait_ge(route_step, did[0])

                def wide(ap, n):
                    return ap.unsqueeze(3).broadcast_to([P, TPC, ap.shape[2], n])

                def each(ap, n):
                    return ap.unsqueeze(2).broadcast_to([P, TPC, n])

                def other(ap):
                    n = ap.shape[2]
                    return ap.unsqueeze(2).broadcast_to([P, TPC, n, n])

                tt, ts, red = nc.vector.tensor_tensor, nc.vector.tensor_scalar, nc.vector.tensor_reduce
                logits = allb[2 + c % 2][:, 0:TPC * NE].rearrange("p (t e) -> p t e", e=NE)
                if c:
                    dve.wait_ge(route_step, c * ROUTE_STEPS)
                dve.wait_ge(logit_ps, c + 1)
                step(red(r["max"], logits, AX.X, ALU.max))
                step(tt(r["logit"], logits, each(r["max"], NE), ALU.subtract))
                dve.wait_ge(rexp_done, c + 1)
                step(red(r["sum"], r["exp"], AX.X, ALU.add))
                step(nc.vector.reciprocal(r["rec"], r["sum"]))
                step(tt(r["score"], r["exp"], each(r["rec"], NE), ALU.mult))
                step(red(r["group"], r["score"].rearrange("p t (g e) -> p t g e", g=NGR), AX.X, ALU.max))
                step(tt(r["ggt"], other(r["group"]), wide(r["group"], NGR), ALU.is_gt))
                step(tt(r["geq"], other(r["group"]), wide(r["group"], NGR), ALU.is_equal))
                step(tt(r["gtie"], r["geq"], lowg[:, :, :].unsqueeze(1).broadcast_to([P, TPC, NGR, NGR]), ALU.mult))
                step(tt(r["gcmp"], r["ggt"], r["gtie"], ALU.add))
                step(red(r["grank"], r["gcmp"], AX.X, ALU.add))
                step(ts(r["gsel"], r["grank"], float(TOPG), None, ALU.is_lt))
                by_group = "p t (g e) -> p t g e"
                step(tt(r["kept"].rearrange(by_group, g=NGR), r["score"].rearrange(by_group, g=NGR),
                        wide(r["gsel"], EPG), ALU.mult))
                step(nc.vector.scalar_tensor_tensor(out=r["masked"].rearrange(by_group, g=NGR), in0=wide(r["gsel"], EPG),
                                                    scalar=-1.0, in1=r["kept"].rearrange(by_group, g=NGR),
                                                    op0=ALU.add, op1=ALU.add))
                step(tt(r["gt"], other(r["masked"]), wide(r["masked"], NE), ALU.is_gt))
                step(tt(r["eq"], other(r["masked"]), wide(r["masked"], NE), ALU.is_equal))
                step(tt(r["tie"], r["eq"], lower[:, :, :].unsqueeze(1).broadcast_to([P, TPC, NE, NE]), ALU.mult))
                step(tt(r["cmp"], r["gt"], r["tie"], ALU.add))
                step(red(r["rank"], r["cmp"], AX.X, ALU.add))
                step(nc.vector.scalar_tensor_tensor(out=r["w"], in0=r["rank"], scalar=float(TOPK), in1=r["score"],
                                                    op0=ALU.is_lt, op1=ALU.mult))
                step(red(r["wsum"], r["w"], AX.X, ALU.add))
                step(ts(r["weps"], r["wsum"], 1e-20, None, ALU.add))
                step(nc.vector.reciprocal(r["wrec"], r["weps"]))
                step(tt(r["cw"], r["w"], each(r["wrec"], NE), ALU.mult))
                parts = [CP[:, c * TPC:(c + 1) * TPC, i, 0:NE] for i in range(3)]
                step(nc.vector.tensor_copy(parts[0], r["cw"]))
                step(tt(r["rem"], r["cw"], parts[0], ALU.subtract))
                step(nc.vector.tensor_copy(parts[1], r["rem"]))
                step(tt(parts[2], r["rem"], parts[1], ALU.subtract))
                nc.vector.tensor_copy(r["wsum"], r["wrec"]).then_inc(route_step, c * ROUTE_STEPS + ROUTE_STEPS - did[0])

            def turn_weights(c):
                dve.wait_ge(cwT_ps, c + 1)
                nc.vector.tensor_copy(CWT[:, c * CH:(c + 1) * CH],
                                      allb[4 + c % 2].bitcast(BF16)[0:3 * PROWS, 0:CH]).then_inc(cwT_ready, 1)

            normalise_tokens(1, 0, xm[0])
            for c in range(NC):
                if c + 1 < NC:
                    if c >= 1:
                        dve.wait_ge(x2T_ps, KH * c)
                    normalise_tokens(1, c + 1, xm[(c + 1) % 2])
                for k in range(KH):
                    n = KH * c + k
                    dve.wait_ge(h2_ready, n + 1)
                    nc.vector.tensor_copy(Hh[:, k, c * CH:(c + 1) * CH], hv[c % 2][:, k, :]).then_inc(h2_hi, 1)
                    dve.wait_ge(h2_hi, n + 1)
                    nc.vector.tensor_tensor(Hl[:, k, c * CH:(c + 1) * CH], hv[c % 2][:, k, :],
                                            Hh[:, k, c * CH:(c + 1) * CH].bitcast(F32), ALU.subtract).then_inc(h2_split, 1)
                routing(c)
                if c >= 1:
                    turn_weights(c - 1)
            turn_weights(NC - 1)

            def finish(c, half):
                dve.wait_ge(yT_ps, c * 2 + (half + 1))
                t = X[:, bass.ds(c * TPC + 2 * half, 2), :]
                nc.vector.tensor_tensor(t, allb[7].rearrange("p (t h) -> p t h", h=H), t, ALU.add).then_inc(fin_done, 1)

            def ffn(c):
                start = isinstance(c, int) and c == 0
                for f in range(NFT):
                    free = f if f == 0 else f - 1
                    dve.wait_ge(u_ps, c * NFT + (f + 1))
                    dve.wait_ge(silu_done, c * NFT + (f + 1))
                    if not (start and f < 2):
                        dve.wait_ge(a_ready, c * NFT + free)
                    nc.vector.tensor_tensor(su[f % 2][:, :], allb[2 * (f % 2) + 1], sg[f % 2][:, :], ALU.mult).then_inc(u_read, 1)
                    dve.wait_ge(u_read, c * NFT + (f + 1))
                    src = su[f % 2]
                    if f >= NSH:
                        dve.wait_ge(cwb_ps, c * NRT + (f - NSH + 1))
                        nc.vector.tensor_tensor(sw[f % 2][:, :], allb[4], su[f % 2][:, :], ALU.mult).then_inc(cwb_read, 1)
                        dve.wait_ge(cwb_read, c * NRT + (f - NSH + 1))
                        src = sw[f % 2]
                    if not (start and f < 2):
                        dve.wait_ge(down_done, c * NFT + free)
                    nc.vector.tensor_copy(ah[f % 2][:, :], src[:, :]).then_inc(hi_done, 1)
                    dve.wait_ge(hi_done, c * NFT + (f + 1))
                    nc.vector.tensor_tensor(al[f % 2][:, :], src[:, :], ah[f % 2][:, :].bitcast(F32),
                                            ALU.subtract).then_inc(a_ready, 1)
                    if f in (3, 5) and not start:
                        finish(c - 1, (f - 3) // 2)

            ffn(0)
            with dve.Fori(1, NC) as c:
                ffn(c)
            finish(NC - 1, 0)
            finish(NC - 1, 1)

        @block.tensor
        def _(pe):
            pe.wait_ge(silu_c, 4)
            pe.wait_ge(const_done, N_CONST)
            for n, m in enumerate((0, 1, 2, 3, 6, 7, 8, 9, 10, 11)):
                for k in range(KH):
                    ins = nc.tensor.matmul(allb[7][:, n * B:(n + 1) * B], Wm[:, k, m * P:(m + 1) * P], cS[:, k, :],
                                           start=(k == 0), stop=(k == KH - 1))
            ins.then_inc(mod_ps, 1)
            for b in range(B):
                for k in range(KH):
                    ins = nc.tensor.matmul(allb[5][:, b * H:(b + 1) * H], cB[:, k, b, :],
                                           Wm[:, k, 2 * H:3 * H], start=(k == 0), stop=(k == KH - 1))
            ins.then_inc(gate_ps, 1)

            def turn(c):
                for k in range(KH):
                    n = KH * c + k
                    pe.wait_ge(xn_ready, TPC * (c + 1))
                    if n >= KH:
                        pe.wait_ge(hT_ready, n - KH + 1)
                    for t in range(TPC):
                        ins = nc.tensor.transpose(allb[k][:, t * P:(t + 1) * P], xn[c % 2][:, t, k * P:(k + 1) * P], ident[:, :])
                    ins.then_inc(xnT_ps, 1)

            turn(0)
            pe.wait_ge(gate_step, 6)
            pe.wait_ge(mod_read, 5)
            for c in range(NC):
                if c + 1 < NC:
                    turn(c + 1)
                pe.wait_ge(hT_ready, KH * (c + 1))
                for m in range(4):
                    n = 4 * c + m
                    if n >= 4:
                        pe.wait_ge(qk_read, 2 * (n - 3))
                    for k in range(KH):
                        ins = nc.tensor.matmul(allb[2 + m], Wqk[:, k, m * P:(m + 1) * P], hT[:, k, c * CH:(c + 1) * CH],
                                               start=(k == 0), stop=(k == KH - 1))
                    ins.then_inc(qk_ps, 1)
                for v in range(2):
                    if c:
                        pe.wait_ge(v_read, 2 * (c - 1) + v + 1)
                    for u in range(2):
                        t0 = c * CH + (2 * v + u) * P
                        for k in range(KH):
                            ins = nc.tensor.matmul(allb[6 + v][:, u * H:(u + 1) * H], hT[:, k, t0:t0 + P], Wv[:, k, :],
                                                   start=(k == 0), stop=(k == KH - 1))
                    ins.then_inc(v_ps, 1)

            def score_row(n, slot, r):
                i, diag, k0, w = ROWS[r]
                for j in range(HG):
                    if not (isinstance(n, int) and n == 0 and r == 0 and j < 2):
                        pe.wait_ge(m_red, n * UNITS + (HG * r + j - 1))
                    if diag:
                        nc.tensor.matmul(bank[j % 2][:, w - P:w], identb[:, :], mask[:, :], start=True, stop=False,
                                         skip_group_check=True)
                    ins = nc.tensor.matmul(bank[j % 2][:, 0:w], Qs[slot][0:NPR, i // TPC, j, (i % TPC) * P:(i % TPC + 1) * P],
                                           Ks[slot][0:NPR, j, k0:k0 + w], start=not diag, stop=True, skip_group_check=True)
                    ins.then_inc(m_ps, 1)

            def turn_max_waits(n, half, event):
                pe.wait_ge(mp_step, n * 9 + (9 if half else 4))
                if event is not None:
                    pe.wait_ge(t_read, event)

            def turn_max():
                nc.tensor.transpose(tb[:, :].bitcast(BF16)[0:3 * HG * TPC, 0:P],
                                    MP[:, :, :, :].rearrange("p a j i -> p (a j i)"), identb[:, :]).then_inc(mpT_ps, 1)

            def turn_out(o, qc, event):
                pe.wait_ge(ot_ready, o + 1)
                pe.wait_ge(t_read, event)
                for t in range(TPC):
                    ins = nc.tensor.transpose(tb[:, t * P:(t + 1) * P], OT[qc][:, t * P:(t + 1) * P], ident[:, :])
                ins.then_inc(oT_ps, 1)

            def products(n, slot, s):
                qc, kt = STEPS[s]
                q0 = max(0, kt - TPC * qc) * P
                w = CH - q0
                pe.wait_ge(exp_done, n * (2 * NS) + 2 * (s + 1))
                if kt == 0 and not (isinstance(n, int) and n == 0 and qc == 0):
                    pe.wait_ge(ot_ready, n * 2 + qc)
                for j in range(HG):
                    ins = nc.tensor.matmul(pvb[32 * j:32 * j + 32, q0:CH], Vst[slot][:, kt, 32 * j:32 * j + 32],
                                           Pr[(2 * s + j // 2) % 4][:, j % 2, 0:w],
                                           start=(kt == 0), stop=(kt == TPC * (qc + 1) - 1), skip_group_check=True)
                ins.then_inc(pv_done, 1)

            def body(n, at, first, last):
                if isinstance(n, int) and n == -1:
                    pe.wait_ge(v_read, 2 * NC)
                    pe.wait_ge(qk_read, 2 * 4 * NC)
                    pe.wait_ge(hT_ready, KH * NC)
                    pe.wait_ge(staged[0], 16 * STAGE_DMAS)
                    for r in range(NS):
                        score_row(0, 0, r)
                        if r == 6:
                            turn_max_waits(0, 0, None)
                            turn_max()
                    return
                (slot, turn), (nxt, nxt_turn) = at(0), at(1)
                if not last:
                    pe.wait_ge(staged[nxt], nxt_turn * (16 * STAGE_DMAS) + 16 * STAGE_DMAS)
                for s in range(NS):
                    qc, kt = STEPS[s]
                    q0 = max(0, kt - TPC * qc) * P
                    if kt == 0:
                        pe.wait_ge(aug_in[slot][qc], turn * 48 + 48)
                    for pair in range(2):
                        if not (first and s == 0):
                            pe.wait_ge(exp_done, n * (2 * NS) + (2 * s + pair - 1))
                        for h in range(2):
                            j = 2 * pair + h
                            if on_diagonal(s):
                                nc.tensor.matmul(epair[pair][:, h, 0:P], identb[:, :], maskT[:, :], start=True, stop=False,
                                                 skip_group_check=True)
                            ins = nc.tensor.matmul(epair[pair][:, h, 0:CH - q0], Ks[slot][0:NAUG, j, kt * P:(kt + 1) * P],
                                                   Qs[slot][0:NAUG, qc, j, q0:CH], start=not on_diagonal(s), stop=True,
                                                   skip_group_check=True)
                        ins.then_inc(e_ps, 1)
                    if not last:
                        score_row(n + 1, nxt, s)
                    if s == 1:
                        turn_max_waits(n, 1, t_event(n, "max1"))
                    if s == 6 and not last:
                        turn_max_waits(n + 1, 0, t_event(n, "max0"))
                    if s > 0:
                        products(n, slot, s - 1)
                    elif not first:
                        products(n - 1, at(-1)[0], NS - 1)
                    if s == 1:
                        turn_max()
                    if s == 3 and not first:
                        turn_out(n * 2 - 1, 1, t_event(n, "out1"))
                    if s == 6 and not last:
                        turn_max()
                    if s == 8:
                        turn_out(n * 2, 0, t_event(n, "out0"))
            attention(body)(pe)
            products(NIT - 1, (NIT - 1) % SLOTS, NS - 1)
            turn_out(2 * NIT - 1, 1, t_event(NIT - 1, "out0") + 1)

            pe.wait_ge(t_read, t_event(NIT - 1, "out0") + 2)
            for c in range(NC):
                b, qc = c // (S // CH), c % (S // CH)
                for k in range(KH):
                    n = KH * c + k
                    if n >= KH:
                        pe.wait_ge(aT_ready, n - KH + 1)
                    for t in range(TPC):
                        src = A[:, qc, t, b * NG + 2 * k:b * NG + 2 * k + 2, :].rearrange("p g d -> p (g d)")
                        ins = nc.tensor.transpose(allb[k][:, t * P:(t + 1) * P], src, ident[:, :])
                    ins.then_inc(aT_ps, 1)
                pe.wait_ge(aT_ready, KH * (c + 1))
                for t in range(TPC):
                    n = c * TPC + t
                    if n >= 4:
                        pe.wait_ge(x1g, n - 3)
                    for k in range(KH):
                        ins = nc.tensor.matmul(allb[4 + n % 4][:, 0:H], AT[c % 2][:, k, t * P:(t + 1) * P], Wo[:, k, :],
                                               start=(k == 0), stop=(k == KH - 1))
                    ins.then_inc(y_ps, 1)

            pe.wait_ge(wg_in, 16)

            def turn2(c):
                pe.wait_ge(xn_ready, NT + TPC * (c + 1))
                for k in range(KH):
                    if c:
                        pe.wait_ge(h2_ready, KH * (c - 1) + k + 1)
                    for t in range(TPC):
                        ins = nc.tensor.transpose(allb[k][:, t * P:(t + 1) * P], xm[c % 2][:, t, k * P:(k + 1) * P], ident[:, :])
                    ins.then_inc(x2T_ps, 1)

            def turn_weights(c):
                pe.wait_ge(route_step, (c + 1) * ROUTE_STEPS)
                if c >= 2:
                    pe.wait_ge(cwT_ready, c - 1)
                for t in range(TPC):
                    ins = nc.tensor.transpose(allb[4 + c % 2].bitcast(BF16)[0:3 * PROWS, t * P:(t + 1) * P],
                                              CP[:, c * TPC + t, :, :].rearrange("p a e -> p (a e)"), identb[:, :])
                ins.then_inc(cwT_ps, 1)

            turn2(0)
            for c in range(NC):
                if c + 1 < NC:
                    turn2(c + 1)
                pe.wait_ge(h2_ready, KH * (c + 1))
                if c >= 2:
                    pe.wait_ge(route_step, (c - 2) * ROUTE_STEPS + 2)
                for t in range(TPC):
                    for k in range(KH):
                        ins = nc.tensor.matmul(allb[2 + c % 2][:, t * NE:(t + 1) * NE], hv[c % 2][:, k, t * P:(t + 1) * P],
                                               Wg[:, k, :], start=(k == 0), stop=(k == KH - 1))
                ins.then_inc(logit_ps, 1)
                if c >= 1:
                    turn_weights(c - 1)
            turn_weights(NC - 1)
            pe.wait_ge(cwT_ready, NC)
            pe.wait_ge(h2_split, KH * NC)

            def up(c, f):
                r = f % WRING
                pe.wait_ge(w_lo, c * NFT + (f + 1))
                if not (isinstance(c, int) and c == 0 and f < 2):
                    pe.wait_ge(u_read, c * NFT + (f if f == 0 else f - 1))
                cols = bass.ds(c * CH, CH)
                for which, done in ((0, g_ps), (1, u_ps)):
                    for k in range(KH):
                        w = slice((which * KH + k) * P, (which * KH + k + 1) * P)
                        for n, (wt, ht) in enumerate(((Wh, Hh), (Wh, Hl), (Wl, Hh))):
                            ins = nc.tensor.matmul(allb[2 * (f % 2) + which], wt[r][:, w], ht[:, k, cols],
                                                   start=(k == 0 and n == 0), stop=(k == KH - 1 and n == 2))
                    ins.then_inc(done, 1)

            def down(c, f):
                r = f % WRING
                pe.wait_ge(a_ready, c * NFT + (f + 1))
                if f == 0 and not (isinstance(c, int) and c == 0):
                    pe.wait_ge(y_read, c * 2)
                for m in range(KH):
                    w = slice(2 * KH * P + m * P, 2 * KH * P + (m + 1) * P)
                    for n, (wt, at) in enumerate(((Wh, ah), (Wh, al), (Wl, ah))):
                        ins = nc.tensor.matmul(allb[5 + m], wt[r][:, w], at[f % 2][:, :],
                                               start=(f == 0 and n == 0), stop=(f == NFT - 1 and n == 2))
                ins.then_inc(down_done, 1)

            def spread(c, f):
                if not (isinstance(c, int) and c == 0 and f == NSH):
                    pe.wait_ge(cwb_read, c * NRT + (f - NSH))
                nc.tensor.matmul(allb[4], sel[:, f - NSH, :], CWT[:, bass.ds(c * CH, CH)],
                                 start=True, stop=True).then_inc(cwb_ps, 1)

            def turn_back(c, half):
                pe.wait_ge(y_read, c * 2 + 2)
                if not (isinstance(c, int) and c == 0 and half == 0):
                    pe.wait_ge(fin_done, c * 2 + half)
                for t in range(2):
                    for m in range(KH):
                        ins = nc.tensor.transpose(allb[7][:, t * H + m * P:t * H + (m + 1) * P],
                                                  Ys[:, m, (2 * half + t) * P:(2 * half + t + 1) * P], ident[:, :])
                ins.then_inc(yT_ps, 1)

            def ffn(c):
                start = isinstance(c, int) and c == 0
                for f in range(NFT):
                    up(c, f)
                    if f:
                        down(c, f - 1)
                    elif not start:
                        down(c - 1, NFT - 1)
                    if f >= NSH:
                        spread(c, f)
                    if f in (2, 4) and not start:
                        turn_back(c - 1, (f - 2) // 2)

            ffn(0)
            with pe.Fori(1, NC) as c:
                ffn(c)
            down(NC - 1, NFT - 1)
            turn_back(NC - 1, 0)
            turn_back(NC - 1, 1)


def kernel(**inputs):
    import numpy as np
    import concourse.bacc as bacc
    from concourse.bass_utils import run_bass_kernel_spmd as run

    def kmajor(w):
        w = np.asarray(w).T
        return np.ascontiguousarray(w.reshape(w.shape[0] // 128, 128, w.shape[1]).transpose(1, 0, 2))

    nc = bacc.Bacc("TRN2", target_bir_lowering=False, num_devices=1)
    wqkv = np.asarray(inputs["L0_attn_W_qkv"])
    bqkv = np.asarray(inputs["L0_attn_b_qkv"])
    arrays = {
        "x": np.asarray(inputs["L0_attn_x"]).reshape(T, H),
        "wqk": kmajor(wqkv[:2 * H]),
        "bqk": bqkv[:2 * H].reshape(4, 128).T,
        "wv": kmajor(wqkv[2 * H:]),
        "bv": bqkv[2 * H:],
        "wout": kmajor(inputs["L0_attn_W_out"]),
        "bout": np.asarray(inputs["L0_attn_b_out"]),
        "cT": kmajor(inputs["L0_c"]),
        "wmod": kmajor(np.asarray(inputs["L0_wmod"]).T),
    }
    up, down = np.asarray(inputs["L0_ffn_expert_up_w"]), np.asarray(inputs["L0_ffn_expert_down_w"])
    sup, sdown = np.asarray(inputs["L0_ffn_shared_up_w"]), np.asarray(inputs["L0_ffn_shared_down_w"])

    def tiles(gate, upw, downw):
        n = -(-gate.shape[0] // 128)
        room = ((0, n * 128 - gate.shape[0]), (0, 0))
        g, u, d = (np.pad(a, room).reshape(n, 128, 256) for a in (gate, upw, downw.T))
        g, u = (a.reshape(n, 128, 2, 128).transpose(0, 3, 2, 1).reshape(n, 128, 256) for a in (g, u))
        return np.concatenate([g, u, d], axis=2)

    arrays["wgate"] = kmajor(inputs["L0_ffn_gate_w"])
    arrays["wffn"] = np.concatenate([
        tiles(sup[:SI], sup[SI:], sdown),
        tiles(up[:, :EI].reshape(-1, H), up[:, EI:].reshape(-1, H), down.transpose(1, 0, 2).reshape(H, -1)),
    ])
    maps, args = {}, []
    for name, a in arrays.items():
        a = np.ascontiguousarray(a)
        maps["in_" + name] = a
        args.append(nc.dram_tensor("in_" + name, a.shape, mybir.dt.from_np(a.dtype), kind="ExternalInput").ap())
    args.append(nc.dram_tensor("qk_parts", (3, 2, B, H, S), BF16, kind="Internal").ap())
    args.append(nc.dram_tensor("out", (T, H), F32, kind="ExternalOutput").ap())
    program(nc, *args)
    r = run(nc, [maps], core_ids=[0])
    return r.results[0]["out"].reshape(B, S, H)
```

```python
from contextlib import ExitStack

import concourse.bass as bass
from concourse import mybir

F32 = mybir.dt.float32
BF16 = mybir.dt.bfloat16
ALU = mybir.AluOpType
ACT = mybir.ActivationFunctionType
AX = mybir.AxisListType

P = 128
B, S, H = 2, 1024, 256
NH, HD = 16, 16
T = B * S
KH = H // P
NT = T // P
CH = 512
NC = T // CH
TPC = CH // P
HG = 4
NG = NH // HG
NIT = B * NG
KT = S // P
EPS = 1e-5
SCALE = float(HD) ** -0.5
NEG = -1.0e30
F32R = mybir.dt.float32r

NE, EI = 16, 176
NGR, TOPG, TOPK = 4, 2, 4
EPG = NE // NGR
SI = 2 * EI
NSH = -(-SI // P)
NRT = NE * EI // P
NFT = NSH + NRT
WF = 2 * KH * P + H
CWRING = 2
CW_LAG = 4
WRING = 5
AHEAD = 2
assert NFT % WRING == 0 and NRT % CWRING == 0
CW_RUNS = [[(e, max(0, e * EI - i * P), min(P, (e + 1) * EI - i * P))
            for e in range(i * P // EI, ((i + 1) * P - 1) // EI + 1)] for i in range(NRT)]


def cw_count(i):
    return 16 * sum(len(CW_RUNS[k]) for k in range(i % CWRING, i + 1, CWRING))


ROUTE_STEPS = 24
SLOTS = 3
LAST_SLOT = (NIT - 1) % SLOTS
SLOT_ORDER = [i for i in range(SLOTS) if i != LAST_SLOT] + [LAST_SLOT]
EARLY_BYTES = 4 * (KH * T + 2 * CH + KH * 2 * H + KH * H + KH * 6 * H + 4 + H + KH * B * P)
LATE_BYTES = 4 * (2 * KH * CH + TPC * H + B * KH * H + KH * NE + NE * NE + NGR * NGR
                  + TPC * (6 + 8 * NE + 3 * NGR + 2 * NGR * NGR + 2 * NE * NE)
                  + (CWRING + 1) * CH)

Q_PARTS = (0, 1, 2, 0, 1, 0)
K_PARTS = (0, 0, 0, 1, 1, 2)
NPR = len(Q_PARTS) * HD
NAUG = NPR + 3
STAGE_DMAS = S // CH + 1
PART_RUNS = (((0, 3, 0), (3, 2, 0), (5, 1, 0)), ((0, 3, 0), (3, 2, 1), (5, 1, 2)))
assert all(Q_PARTS[f + i] == p + i for f, n, p in PART_RUNS[0] for i in range(n))
assert all(K_PARTS[f + i] == p for f, n, p in PART_RUNS[1] for i in range(n))

ROWS = [(i, True, 0, (i + 1) * P) for i in range(TPC)]
for _i in range(TPC, KT):
    ROWS += [(_i, False, 0, CH), (_i, True, CH, (_i + 1) * P - CH)]
STEPS = [(qc, kt) for qc in range(S // CH) for kt in range(TPC * (qc + 1))]
NS = len(STEPS)
UNITS = len(ROWS) * HG
HEADS = NS * HG
EXP = 2
RING = 3
assert UNITS % RING == 0 and HEADS % RING == 0
assert len(ROWS) == NS


def on_diagonal(s):
    qc, kt = STEPS[s]
    return kt >= TPC * qc


EXTRA = 60
PRODUCTS_AFTER = HG - 1


def interleave():
    unit_cost = [w + 80 for _, _, _, w in ROWS for _ in range(HG)]
    head_cost = [CH - max(0, kt - TPC * qc) * P + EXTRA for qc, kt in STEPS for _ in range(HG)]
    order, u, units, heads = [], 0, 0, 0
    for p in range(HEADS):
        s = p // HG
        order.append(("scores", p))
        heads += head_cost[p]
        while u < UNITS and units * sum(head_cost) < heads * sum(unit_cost):
            order.append(("unit", u))
            units += unit_cost[u]
            u += 1
            if u == HG * TPC:
                order.append(("parts", 0))
        if p % HG == PRODUCTS_AFTER:
            order.append(("products", s - 1))
            if s == 1:
                order.append(("max", 1))
            if s == 3:
                order.append(("out", 1))
            if s == 6:
                order.append(("max", 0))
            if s == 8:
                order.append(("out", 0))
    assert u == UNITS and order.index(("parts", 0)) < order.index(("max", 0))
    return order


ORDER = interleave()

M_ORDER = (0, 2, 1, 3)
QK_RING = 3
PER = 3
OVER = PER * (4 * KH + 4)

LN2_STEPS = 2 * TPC + 2
STATS_AT, AGGR_AT, ROOT_AT, NORM_AT = 1, 2, 3, 4
TURN2_AT = (6, 8)
LOGITS_AT = 10
SOFTMAX_AT, EXP_AT, ROUTE_AT = 11, 12, 13
TURNW_AT = NFT - 1
PROJECT = {}
for _c, _f in ((2, 12), (3, 18)):
    PROJECT.update({_f: [("turn", _c, 0)], _f + 1: [("turn", _c, 1)], _f + 2: [("project", _c, 0)],
                    _f + 4: [("project", _c, 1)]})


def LATE_BANK(c, i):
    return i if c < S // CH else 7


def program(nc, x, wqk, bqk, wv, bv, wout, bout, cT, wmod, wgate, wffn, qkd, cwd, out):
    with ExitStack() as ctx:
        scope = [ctx]

        def sb(name, shape, dt):
            return scope[-1].enter_context(nc.sbuf_tensor(name, shape, dt))

        def sem(name):
            return ctx.enter_context(nc.semaphore(name))

        X = sb("X", [P, NT, H], F32)
        Wo = sb("Wo", [P, KH, H], F32)
        Bo = sb("Bo", [P, H], F32)
        cS = sb("cS", [P, KH, B], F32)
        cE = sb("cE", [P, 3, KH, B], F32)
        modT = sb("modT", [P, 10, B], F32)
        gbS, gbN, gbA = (sb(n, [P, KH, B], F32) for n in ("gbS", "gbN", "gbA"))
        gate = sb("gate", [P, B, H], F32)
        gbias = sb("gbias", [P, B, H], F32)
        ident = sb("ident", [P, P], F32)
        identb = sb("identb", [P, P], BF16)
        mask = sb("mask", [P, P], BF16)
        maskT = sb("maskT", [P, P], BF16)
        stats = sb("stats", [P, NT, 6], F32)
        mv = sb("mv", [P, NT, 2], F32)
        vare, rvar, rstd = (sb(n, [P, NT], F32) for n in ("vare", "rvar", "rstd"))
        stats2 = sb("stats2", [P, TPC, 6], F32)
        mv2 = sb("mv2", [P, TPC, 2], F32)
        vare2, rvar2, rstd2 = (sb(n, [P, TPC], F32) for n in ("vare2", "rvar2", "rstd2"))
        modC = sb("modC", [P, 6, NC], F32)
        AP = sb("AP", [P, 2, 3, 4, CH], BF16)
        PT = [AP[:, i] for i in range(2)]
        A = AP[:, :, :, :, :].rearrange("p i a m c -> p (i a m c)").bitcast(F32)[:, 0:NIT * CH].rearrange(
            "p (q t n d) -> p q t n d", n=NIT, q=S // CH, t=TPC)
        OT = [sb(f"OT{i}", [P, CH], F32) for i in range(2)]
        mxA = sb("mxA", [P, KT, HG], F32)
        mxB = sb("mxB", [P, TPC, HG], F32)
        mr = sb("mr", [P, HG, TPC], F32)
        MP = sb("MP", [P, 3, HG, TPC], BF16)
        MT = [sb(f"MT{i}", [3 * HG * TPC, P], BF16) for i in range(2)]
        R = sb("R", [P, TPC, HG], F32)

        early = ctx.enter_context(ExitStack())
        scope.append(early)
        hT = sb("hT", [P, KH, T], F32)
        Rq = [sb(f"Rq{i}", [P, CH], F32) for i in range(2)]
        Wqk = sb("Wqk", [P, KH, 2 * H], F32)
        Wv = sb("Wv", [P, KH, H], F32)
        Wm = sb("Wm", [P, KH, 6 * H], F32)
        Bqk = sb("Bqk", [P, 4], F32)
        Bv = sb("Bv", [P, H], F32)
        cB = sb("cB", [P, KH, B, P], F32)
        scope.pop().close()

        AT = sb("AT", [P, KH, CH], F32)
        xm = sb("xm", [P, TPC, H], F32)
        hv = sb("hv", [P, KH, CH], F32)
        Wog = sb("Wog", [P, B, KH, H], F32)
        Wg = sb("Wg", [P, KH, NE], F32)
        lower = sb("lower", [P, NE, NE], F32)
        lowg = sb("lowg", [P, NGR, NGR], F32)
        cwT = sb("cwT", [NE, CH], F32)
        cwb = [sb(f"cwb{i}", [P, CH], F32) for i in range(CWRING)]
        rt = {name: sb("rt_" + name, [P, TPC] + shape, F32) for name, shape in (
            ("max", []), ("sum", []), ("rec", []), ("logit", [NE]), ("exp", [NE]), ("score", [NE]), ("group", [NGR]),
            ("ggt", [NGR, NGR]), ("geq", [NGR, NGR]), ("grank", [NGR]),
            ("gsel", [NGR]), ("kept", [NE]), ("masked", [NE]), ("gt", [NE, NE]), ("eq", [NE, NE]),
            ("rank", [NE]), ("w", [NE]), ("wsum", []), ("weps", []), ("wrec", []), ("cw", [NE]))}
        pad = EARLY_BYTES - LATE_BYTES
        if pad > 0:
            sb("room", [P, pad // 4], F32)

        scope.append(ctx.enter_context(ExitStack()))
        Vall = sb("Vall", [P, NIT, KT, HG, 32], F32)
        Qs, Ks, Vst = {}, {}, {}
        for i in SLOT_ORDER:
            Qs[i] = sb(f"Qs{i}", [P, S // CH, HG, CH], BF16)
            Ks[i] = sb(f"Ks{i}", [P, HG, S], BF16)
            Vst[i] = sb(f"Vst{i}", [P, KT, HG * 32], F32)
        Pr = [sb(f"Pr{i}", [P, 2, CH], F32) for i in range(4)]
        xn = [Pr[i][:, :, :].rearrange("p a (t h) -> p (a t) h", h=H) for i in range(2)]
        Fq = [Pr[2 + m // 2][:, m % 2, :] for m in range(4)]
        gsgn, gneg, gabs = (Vst[i][:, 0:KT // 2, :].rearrange("p k (b h) -> p (k b h)", b=1).rearrange(
            "p (b h) -> p b h", b=B) for i in range(3))
        scope.pop().close()

        Wr = [sb(f"Wr{i}", [P, WF], F32) for i in range(WRING)]
        Wh = [sb(f"Wh{i}", [P, WF], F32R) for i in range(WRING)]
        Wl = [sb(f"Wl{i}", [P, WF], F32R) for i in range(WRING)]
        Hh = sb("Hh", [P, NC, KH, CH], F32R)
        Hl = sb("Hl", [P, NC, KH, CH], F32R)
        sg = [sb(f"sg{i}", [P, CH], F32) for i in range(2)]
        su = [sb(f"su{i}", [P, CH], F32) for i in range(2)]
        sw = [sb(f"sw{i}", [P, CH], F32) for i in range(2)]
        ah = [sb(f"ah{i}", [P, CH], F32R) for i in range(2)]
        al = [sb(f"al{i}", [P, CH], F32R) for i in range(2)]
        Ys = sb("Ys", [P, KH, CH], F32)

        allb = [ctx.enter_context(nc.psum_tensor(f"bank{i}", [P, CH], F32))[:, :] for i in range(8)]
        mbank, ebank, pvb, tb = allb[0:RING], allb[RING:2 * RING], allb[6], allb[7]

        x_in = [sem(f"x_in{c}") for c in range(NC)]
        c_in = sem("c_in")
        mod_in = sem("mod_in")
        qk_in = sem("qk_in")
        v_in = sem("v_in")
        w_in = sem("w_in")
        ident_done = sem("ident_done")
        const_done = sem("const_done")
        negc_exp = sem("negc_exp")
        silu_c = sem("silu_c")
        mod_ps = sem("mod_ps")
        mod_read = sem("mod_read")
        gate_ps = sem("gate_ps")
        gate_step = sem("gate_step")
        modC_done = sem("modC_done")
        ln_step = sem("ln_step")
        rstd_done = sem("rstd_done")
        xn_ready = sem("xn_ready")
        xnT_ps = sem("xnT_ps")
        hT_ready = sem("hT_ready")
        qk_ps = sem("qk_ps")
        qk_read = sem("qk_read")
        parts_done = [sem(f"parts_done{i}") for i in range(B)]
        split_step = [sem(f"split_step{i}") for i in range(B)]
        parts_out = [sem(f"parts_out{i}") for i in range(2)]
        v_ps = sem("v_ps")
        v_read = sem("v_read")
        staged_v = [sem(f"staged_v{i}") for i in range(SLOTS)]
        staged = [sem(f"staged{i}") for i in range(SLOTS)]
        m_ps = sem("m_ps")
        m_red = sem("m_red")
        mp_step = sem("mp_step")
        mpT_ps = sem("mpT_ps")
        t_read = sem("t_read")
        aug_in = [[sem(f"aug_in{i}_{h}") for h in range(2)] for i in range(SLOTS)]
        e_ps = sem("e_ps")
        exp_done = sem("exp_done")
        pv_done = sem("pv_done")
        ot_ready = sem("ot_ready")
        oT_ps = sem("oT_ps")
        rec_done = sem("rec_done")
        aT_ps = sem("aT_ps")
        aT_ready = sem("aT_ready")
        y_ps = sem("y_ps")
        xb_ready = sem("xb_ready")
        wog_done = sem("wog_done")
        x1_ready = sem("x1_ready")
        out_done = sem("out_done")
        fconst = sem("fconst")
        ln2_step = sem("ln2_step")
        rstd2_done = sem("rstd2_done")
        xm_ready = sem("xm_ready")
        wg_in = sem("wg_in")
        x2T_ps = sem("x2T_ps")
        h2_ready = sem("h2_ready")
        h2_hi = sem("h2_hi")
        h2_split = sem("h2_split")
        logit_ps = sem("logit_ps")
        logit_read = sem("logit_read")
        rexp_done = sem("rexp_done")
        route_step = sem("route_step")
        cwT_ps = sem("cwT_ps")
        cwT_ready = sem("cwT_ready")
        w_raw = [sem(f"w_raw{i}") for i in range(WRING)]
        w_hi = sem("w_hi")
        w_lo = sem("w_lo")
        cw_out = sem("cw_out")
        cw_in = [sem(f"cw_in{i}") for i in range(CWRING)]
        silu_done = sem("silu_done")
        u_read = sem("u_read")
        u_ps = sem("u_ps")
        g_ps = sem("g_ps")
        hi_done = sem("hi_done")
        cwb_read = sem("cwb_read")
        a_ready = sem("a_ready")
        down_done = sem("down_done")
        y_read = sem("y_read")
        yT_ps = sem("yT_ps")
        fin_done = sem("fin_done")

        W_DMAS = 3
        N_CONST = 7 + SLOTS
        block = ctx.enter_context(nc.Block())

        def t_event(n, kind):
            last = isinstance(n, int) and n == NIT - 1
            return n * 4 + {"max1": 2, "out1": 3, "max0": 4, "out0": 4 if last else 5}[kind]

        def split_tile(eng, ops, c, i):
            b, m = c // (S // CH), M_ORDER[i]
            k = 4 * (c % (S // CH)) + i
            eng.wait_ge(qk_read, 2 * (4 * c + i) + 2)
            if k >= 2:
                eng.wait_ge(parts_done[b], k - 1)
            elif b:
                eng.wait_ge(parts_done[b - 1], 4 * (S // CH))
            ops.tensor_tensor(Rq[i % 2][:, :], Fq[m], PT[c % 2][:, 0, m, :], ALU.subtract).then_inc(split_step[b], 1)
            if b == 0:
                eng.wait_ge(split_step[b], 2 * k + 1)
                ops.tensor_copy(PT[c % 2][:, 1, m, :], Rq[i % 2][:, :]).then_inc(split_step[b], 1)
            eng.wait_ge(split_step[b], 2 * k + 2)
            ops.tensor_tensor(PT[c % 2][:, 2, m, :], Rq[i % 2][:, :], PT[c % 2][:, 1, m, :],
                              ALU.subtract).then_inc(parts_done[b], 1)

        def attention(body):
            def place(n, k=0):
                return lambda d=0: ((n + d) % SLOTS, k + (n + d) // SLOTS)

            def run(eng):
                body(-1, place(-1), True, False)
                body(0, place(0), True, False)
                with eng.Fori(0, (NIT - 2) // SLOTS) as k:
                    for j in range(SLOTS):
                        body(k * SLOTS + (1 + j), place(1 + j, k), False, False)
                body(NIT - 1, place(NIT - 1), False, True)
            return run

        def attention_loads(body):
            def run(eng):
                body(-1, 2, False)
                with eng.Fori(0, (NIT - 2) // SLOTS) as k:
                    for j in range(SLOTS):
                        body(k * SLOTS + j, j, True)
                for n in (NIT - 2, NIT - 1):
                    body(n, n % SLOTS, False)
            return run

        def chunks(body):
            def run(eng):
                body(0, True, False)
                with eng.Fori(1, NC - 1) as c:
                    body(c, False, False)
                body(NC - 1, False, True)
            return run

        @block.sync
        def _(sp):
            def load_x(c):
                sp.dma_start(X[:, c * TPC:(c + 1) * TPC, :],
                             x[c * CH:(c + 1) * CH, :].rearrange("(t p) h -> p t h", p=P)).then_inc(x_in[c], 16)

            load_x(0)
            sp.dma_start(cS[:, :, :], cT).then_inc(c_in, 16)
            sp.dma_start(Wm[:, :, 0:2 * H], wmod[:, :, 0:2 * H]).then_inc(mod_in, 16)
            sp.dma_start(Wqk[:, :, :], wqk).then_inc(qk_in, 16)
            sp.dma_start(Bqk[:, :], bqk).then_inc(qk_in, 16)
            load_x(1)
            sp.dma_start(Wv[:, :, :], wv).then_inc(v_in, 16)
            sp.dma_start(Bv[:, :], bv.rearrange("(a n) -> a n", a=1).broadcast_to([P, H])).then_inc(v_in, 16)
            for c in range(2, NC):
                load_x(c)
            sp.dma_start(Wm[:, :, 2 * H:6 * H], wmod[:, :, 2 * H:6 * H]).then_inc(w_in, 16)
            sp.dma_start(Wo[:, :, :], wout).then_inc(w_in, 16)
            sp.dma_start(Bo[:, :], bout.rearrange("(a n) -> a n", a=1).broadcast_to([P, H])).then_inc(w_in, 16)

            def write_parts(c):
                for i in range(4):
                    write_tile(c, i)

            def write_tile(c, i):
                b, half, m = c // (S // CH), c % (S // CH), M_ORDER[i]
                sp.wait_ge(parts_done[b], 4 * half + i + 1)
                rows = qkd[m // KH, b, (m % KH) * P:(m % KH + 1) * P, :, half * CH:(half + 1) * CH]
                for first, count, part in PART_RUNS[m // KH]:
                    src = PT[c % 2][:, part:part + 1, m, :].broadcast_to([P, count, CH]) if m // KH else (
                        PT[c % 2][:, part:part + count, m, :])
                    sp.dma_start(rows[:, first:first + count, :], src).then_inc(parts_out[c % 2], 16)

            def stage(n, slot):
                q, k = (qkd[t].rearrange("b (g j d) i s -> (b g) (d i) j s", g=NG, j=HG)[bass.ds(n, 1)].rearrange(
                    "a d j s -> (a d) j s") for t in range(2))
                for half in range(S // CH):
                    sp.dma_start(Qs[slot][0:NPR, half, :, :], q[:, :, half * CH:(half + 1) * CH]).then_inc(staged[slot], 16)
                sp.dma_start(Ks[slot][0:NPR, :, :], k).then_inc(staged[slot], 16)

            def stage_values(n, slot):
                sp.dma_start(Vst[slot][:, :, :],
                             Vall[:, bass.ds(n, 1), :, :, :].rearrange("p a k j d -> p (a k) (j d)")).then_inc(staged_v[slot], 16)

            def aug(slot, half):
                for part in range(3):
                    sp.dma_start(
                        Qs[slot][NPR + part:NPR + part + 1, half, :, :].rearrange("o j (i q) -> o (j i) q", i=TPC),
                        MT[half][part * HG * TPC:(part + 1) * HG * TPC, :]
                    ).then_inc(aug_in[slot][half], 16)

            def body(n, slot, stages):
                if isinstance(n, int) and n == -1:
                    write_parts(0)
                    write_tile(1, 0)
                    write_tile(1, 1)
                    sp.wait_ge(parts_out[0], 16 * 12)
                    sp.wait_ge(parts_out[1], 16 * 6)
                    for s in range(SLOTS - 1):
                        stage(s, s)
                    write_tile(1, 2)
                    write_tile(1, 3)
                    sp.wait_ge(v_read, 2 * (S // CH))
                    sp.wait_ge(const_done, N_CONST)
                    for s in range(SLOTS - 1):
                        stage_values(s, s)
                    write_parts(2)
                    write_parts(3)
                    for i in range(2):
                        sp.wait_ge(parts_out[i], 16 * 12 * B)
                    sp.wait_ge(v_read, 2 * NC)
                    sp.dma_start(Wg[:, :, :], wgate).then_inc(wg_in, 16)
                    sp.wait_ge(t_read, 1)
                    aug(0, 0)
                    return
                sp.wait_ge(t_read, t_event(n, "max1") + 1)
                aug(slot, 1)
                if stages:
                    sp.wait_ge(e_ps, n * HEADS + 1)
                    sp.wait_ge(pv_done, n * NS + 1)
                    stage(n + (SLOTS - 1), (slot + SLOTS - 1) % SLOTS)
                    stage_values(n + (SLOTS - 1), (slot + SLOTS - 1) % SLOTS)
                if not (isinstance(n, int) and n == NIT - 1):
                    sp.wait_ge(t_read, t_event(n, "max0") + 1)
                    aug((slot + 1) % SLOTS, 0)

            attention_loads(body)(sp)

            sp.wait_ge(staged_v[LAST_SLOT], 16 * (1 + (NIT - 1) // SLOTS))

            def ffn(c):
                for f in range(NFT):
                    r = f % WRING
                    if not (isinstance(c, int) and c == 0 and f < WRING):
                        sp.wait_ge(w_hi, c * NFT + (f - WRING + 1))
                        sp.wait_ge(w_lo, c * NFT + (f - WRING + 1))
                    sp.dma_start(Wr[r][:, :], wffn[f]).then_inc(w_raw[r], 16)
                    if f == NSH + CW_LAG - 1:
                        sp.wait_ge(cwT_ready, c + 1)
                        sp.dma_start(cwd[:, bass.ds(c * CH, CH)], cwT[:, :]).then_inc(cw_out, 16)
                    if f == NSH + CW_LAG:
                        sp.wait_ge(cw_out, c * 16 + 16)
                    if f >= CW_LAG:
                        spread(c, f - CW_LAG)
                    elif not (isinstance(c, int) and c == 0):
                        spread(c - 1, f - CW_LAG + NFT)
                    if f == 12 and not (isinstance(c, int) and c == 0):
                        store(c - 1)

            def spread(c, f):
                i = f - NSH
                if i < 0:
                    return
                if not (isinstance(c, int) and c == 0 and i < CWRING):
                    sp.wait_ge(cwb_read, c * NRT + (i - CWRING + 1))
                for e, lo, hi in CW_RUNS[i]:
                    sp.dma_start(cwb[i % CWRING][lo:hi, :],
                                 cwd[e:e + 1, bass.ds(c * CH, CH)].broadcast_to([hi - lo, CH])).then_inc(cw_in[i % CWRING], 16)

            def store(c):
                sp.wait_ge(fin_done, c * 2 + 2)
                sp.dma_start(out[bass.ds(c * CH, CH), :].rearrange("(t p) h -> p t h", p=P),
                             X[:, bass.ds(c * TPC, TPC), :]).then_inc(out_done, 16)

            ffn(0)
            with sp.Fori(1, NC) as c:
                ffn(c)
            for f in range(NFT - CW_LAG, NFT):
                spread(NC - 1, f)
            store(NC - 1)
            sp.wait_ge(out_done, 16 * NC)

        @block.gpsimd
        def _(pool):
            nc.gpsimd.memset(ident[:, :], 0.0).then_inc(ident_done, 1)
            pool.wait_ge(ident_done, 1)
            nc.gpsimd.affine_select(out=ident[:, :], in_=ident[:, :], compare_op=ALU.not_equal, fill=1.0,
                                    base=0, pattern=[[-1, P]], channel_multiplier=1).then_inc(ident_done, 1)
            nc.gpsimd.memset(mask[:, :], 0.0).then_inc(const_done, 1)
            nc.gpsimd.memset(maskT[:, :], 0.0).then_inc(const_done, 1)
            nc.gpsimd.memset(Vall[:, :, :, :, HD:HD + 1], 1.0).then_inc(const_done, 1)
            nc.gpsimd.memset(Vall[:, :, :, :, HD + 1:32], 0.0).then_inc(const_done, 1)
            pool.wait_ge(ident_done, 2)
            nc.gpsimd.tensor_copy(identb[:, :], ident[:, :]).then_inc(const_done, 1)
            pool.wait_ge(const_done, 5)
            nc.gpsimd.affine_select(out=mask[:, :], in_=mask[:, :], compare_op=ALU.is_ge, fill=NEG,
                                    base=0, pattern=[[-1, P]], channel_multiplier=1).then_inc(const_done, 1)
            nc.gpsimd.affine_select(out=maskT[:, :], in_=maskT[:, :], compare_op=ALU.is_ge, fill=NEG,
                                    base=0, pattern=[[1, P]], channel_multiplier=-1).then_inc(const_done, 1)
            pool.wait_ge(const_done, 7)
            for i in range(SLOTS):
                nc.gpsimd.memset(Ks[i][NPR:P, :, :], 1.0).then_inc(const_done, 1)

            pool.wait_ge(const_done, N_CONST)
            for c in range(S // CH, NC):
                for i in range(4):
                    split_tile(pool, nc.gpsimd, c, i)
            pool.wait_ge(gate_step, 8)
            pool.wait_ge(w_in, 16 * W_DMAS)
            for b in range(B):
                nc.gpsimd.tensor_tensor(gbias[:, b, :], gate[:, b, :], Bo[:, :], ALU.mult).then_inc(xb_ready, 1)
            pool.wait_ge(xb_ready, B)
            pool.wait_ge(xn_ready, NT)
            for t in range(NT):
                nc.gpsimd.tensor_tensor(X[:, t, :], X[:, t, :], gbias[:, t // KT, :], ALU.add).then_inc(xb_ready, 1)
            pool.wait_ge(v_read, 2 * NC)
            pool.wait_ge(parts_done[B - 1], 4 * (S // CH))
            for b in range(B):
                for k in range(KH):
                    nc.gpsimd.tensor_tensor(Wog[:, b, k, :], Wo[:, k, :], gate[:, b, :], ALU.mult).then_inc(wog_done, 1)

            nc.gpsimd.memset(lower[:, :, :], 0.0).then_inc(fconst, 1)
            nc.gpsimd.memset(lowg[:, :, :], 0.0).then_inc(fconst, 1)
            pool.wait_ge(fconst, 2)
            nc.gpsimd.affine_select(out=lower[:, :, :], in_=lower[:, :, :], compare_op=ALU.is_ge, fill=1.0,
                                    base=0, pattern=[[-1, NE], [1, NE]], channel_multiplier=0).then_inc(fconst, 1)
            nc.gpsimd.affine_select(out=lowg[:, :, :], in_=lowg[:, :, :], compare_op=ALU.is_ge, fill=1.0,
                                    base=0, pattern=[[-1, NGR], [1, NGR]], channel_multiplier=0).then_inc(fconst, 1)
            def ffn(c):
                for f in range(NFT):
                    r = f % WRING
                    pool.wait_ge(w_hi, c * NFT + (f + 1))
                    if not (isinstance(c, int) and c == 0 and f < WRING):
                        pool.wait_ge(down_done, c * NFT + (f - WRING + 1))
                    nc.gpsimd.tensor_tensor(Wl[r][:, :], Wr[r][:, :], Wh[r][:, :].bitcast(F32), ALU.subtract).then_inc(w_lo, 1)

            pool.wait_ge(e_ps, (NIT - 1) * HEADS)
            pool.wait_ge(pv_done, (NIT - 1) * NS)
            ffn(0)
            with pool.Fori(1, NC) as c:
                ffn(c)

        @block.scalar
        def _(act):
            act.wait_ge(c_in, 16)
            nc.scalar.activation(cE[:, 0], cS[:, :, :], ACT.Exp, scale=-1.0).then_inc(negc_exp, 1)

            def root_first(c):
                act.wait_ge(ln_step, LN2_STEPS * (c + 1))
                cols = slice(c * TPC, (c + 1) * TPC)
                nc.scalar.activation(rstd[:, cols], rvar[:, cols], ACT.Sqrt).then_inc(rstd_done, 1)

            root_first(0)
            root_first(1)

            def hT_evict(c):
                b = c // (S // CH)
                for k in range(KH):
                    n = KH * c + k
                    act.wait_ge(xnT_ps, n + 1)
                    if n == 0:
                        act.wait_ge(mod_read, 2)
                    nc.scalar.activation(hT[:, k, c * CH:(c + 1) * CH], allb[k], ACT.Identity,
                                         scale=modT[:, 2 + k, b:b + 1], bias=modT[:, k, b:b + 1]).then_inc(hT_ready, 1)
            def round_tile(c, i):
                act.wait_ge(split_step[1], 2 * (4 * (c % (S // CH)) + i) + 1)
                nc.scalar.activation(PT[c % 2][:, 1, M_ORDER[i], :], Rq[i % 2][:, :], ACT.Copy).then_inc(split_step[1], 1)

            hT_evict(0)
            act.wait_ge(qk_in, 32)
            for c in range(NC):
                if c + 2 < NC:
                    root_first(c + 2)
                for i, m in enumerate(M_ORDER):
                    n = 4 * c + i
                    bank = allb[QK_RING + n % QK_RING]
                    act.wait_ge(qk_ps, n + 1)
                    if n >= 4:
                        before = (n - 4) // (4 * (S // CH))
                        act.wait_ge(parts_done[before], n - 3 - before * 4 * (S // CH))
                    nc.scalar.activation(Fq[m], bank, ACT.Identity, bias=Bqk[:, m:m + 1]).then_inc(qk_read, 1)
                    if c >= 2:
                        act.wait_ge(parts_out[c % 2], 16 * 12)
                    nc.scalar.activation(PT[c % 2][:, 0, m, :], bank, ACT.Identity,
                                         bias=Bqk[:, m:m + 1]).then_inc(qk_read, 1)
                    if n > 4 * (S // CH):
                        round_tile((n - 1) // 4, (n - 1) % 4)
                if c + 1 < NC:
                    hT_evict(c + 1)

            def evict(o, qc):
                act.wait_ge(pv_done, (o - qc) * (NS // 2) + (TPC if qc == 0 else NS))
                if not (isinstance(o, int) and o < 2):
                    act.wait_ge(oT_ps, o - 1)
                nc.scalar.activation(OT[qc][:, :], pvb, ACT.Copy).then_inc(ot_ready, 1)

            def split_weights(c, f):
                r = f % WRING
                act.wait_ge(w_raw[r], c * (16 * (NFT // WRING)) + 16 * (f // WRING + 1))
                if not (isinstance(c, int) and c == 0 and f < WRING):
                    act.wait_ge(down_done, c * NFT + (f - WRING + 1))
                nc.scalar.activation(Wh[r][:, :], Wr[r][:, :], ACT.Copy).then_inc(w_hi, 1)

            def copy_out(c, k):
                act.wait_ge(aT_ps, KH * c + k + 1)
                if c:
                    act.wait_ge(y_ps, 2 * c)
                nc.scalar.activation(AT[:, k, :], allb[LATE_BANK(c, k)], ACT.Copy).then_inc(aT_ready, 1)

            def root(q):
                act.wait_ge(ln2_step, q * LN2_STEPS + LN2_STEPS)
                nc.scalar.activation(rstd2[:, :], rvar2[:, :], ACT.Sqrt).then_inc(rstd2_done, 1)

            def shift(q, k, bank):
                act.wait_ge(x2T_ps, q * KH + (k + 1))
                if isinstance(q, int) and q == 0:
                    act.wait_ge(modC_done, 4)
                else:
                    act.wait_ge(h2_split, q * KH)
                    act.wait_ge(logit_ps, q)
                nc.scalar.activation(hv[:, k, :], bank, ACT.Identity, scale=modC[:, 2 + k, bass.ds(q, 1)],
                                     bias=modC[:, k, bass.ds(q, 1)]).then_inc(h2_ready, 1)

            def exponential(q):
                act.wait_ge(route_step, q * ROUTE_STEPS + 2)
                nc.scalar.activation(rt["exp"][:, :, :], rt["logit"][:, :, :], ACT.Exp).then_inc(rexp_done, 1)

            def late(s):
                if s in (1, 7):
                    for k in range(KH):
                        copy_out(s // 7, k)
                if s == 3:
                    root(0)
                if s == 5:
                    for k in range(KH):
                        shift(0, k, allb[k])
                if s == 6:
                    exponential(0)
                if s >= NS - AHEAD:
                    if s == NS - AHEAD:
                        act.wait_ge(staged_v[LAST_SLOT], 16 * (1 + (NIT - 1) // SLOTS))
                    split_weights(0, s - (NS - AHEAD))

            def body(n, at, first, last):
                if isinstance(n, int) and n == -1:
                    round_tile(NC - 1, 3)
                    act.wait_ge(parts_done[B - 1], 4 * (S // CH))
                    return
                for s in range(NS):
                    qc, kt = STEPS[s]
                    w = CH - (max(0, kt - TPC * qc)) * P
                    for j in range(HG):
                        p = HG * s + j
                        act.wait_ge(e_ps, n * HEADS + (p + 1))
                        if j == 0 and not (first and s < 2):
                            act.wait_ge(pv_done, n * NS + (s - 1))
                        nc.scalar.activation(Pr[(2 * s + j // 2) % 4][:, j % 2, 0:w], ebank[p % RING][:, 0:w],
                                             ACT.Exp, scale=SCALE).then_inc(exp_done, EXP)
                    if s == 0 and not first:
                        evict(n * 2 - 1, 1)
                    if s == TPC:
                        evict(n * 2, 0)
                    if last:
                        late(s)
            attention(body)(act)
            evict(2 * NIT - 1, 1)

            def scale_out(c):
                act.wait_ge(down_done, c * NFT + NFT)
                if not (isinstance(c, int) and c == 0):
                    act.wait_ge(yT_ps, c * 2)
                for k in range(KH):
                    nc.scalar.activation(Ys[:, k, :], allb[5 + k], ACT.Copy,
                                         scale=modC[:, 4 + k, bass.ds(c, 1)]).then_inc(y_read, 1)

            def ffn(c, first, last):
                later = []
                for f in range(NFT):
                    act.wait_ge(g_ps, c * NFT + (f + 1))
                    if not (isinstance(c, int) and c == 0 and f < 2):
                        act.wait_ge(u_read, c * NFT + (f if f == 0 else f - 1))
                    nc.scalar.activation(sg[f % 2][:, :], allb[2 * (f % 2)], ACT.Silu).then_inc(silu_done, 1)
                    if f == 0 and not (isinstance(c, int) and c == 0):
                        scale_out(c - 1)
                    if f + AHEAD < NFT or not last:
                        split_weights(c, f + AHEAD)
                    if first and f in PROJECT:
                        for what, cc, i in PROJECT[f]:
                            if what == "turn":
                                later.append((f + 1, cc, i))
                    if first:
                        for _, cc, i in [e for e in later if e[0] == f]:
                            copy_out(cc, i)
                    if not last:
                        if f == ROOT_AT:
                            root(c + 1)
                        if f - 1 in TURN2_AT:
                            shift(c + 1, TURN2_AT.index(f - 1), allb[7])
                        if f == EXP_AT:
                            exponential(c + 1)

            chunks(ffn)(act)
            scale_out(NC - 1)

        @block.vector
        def _(dve):
            def first_statistics(c):
                k = c * LN2_STEPS
                tiles = range(c * TPC, (c + 1) * TPC)
                cols = slice(c * TPC, (c + 1) * TPC)
                dve.wait_ge(x_in[c], 16)
                for t in tiles:
                    nc.vector.bn_stats(stats[:, t, :], X[:, t, :]).then_inc(ln_step, 1)
                for i, t in enumerate(tiles):
                    dve.wait_ge(ln_step, k + i + 1)
                    nc.vector.bn_aggr(mv[:, t, :], stats[:, t, :]).then_inc(ln_step, 1)
                dve.wait_ge(ln_step, k + 2 * TPC)
                nc.vector.tensor_scalar(vare[:, cols], mv[:, cols, 1], EPS, None, ALU.add).then_inc(ln_step, 1)
                dve.wait_ge(ln_step, k + 2 * TPC + 1)
                nc.vector.reciprocal(rvar[:, cols], vare[:, cols]).then_inc(ln_step, 1)

            first_statistics(0)

            def normalise_tokens(c, dst):
                for t in range(c * TPC, (c + 1) * TPC):
                    nc.vector.tensor_scalar(dst[:, t - c * TPC, :], X[:, t, :], mv[:, t, 0:1], rstd[:, t:t + 1],
                                            ALU.subtract, ALU.mult).then_inc(xn_ready, 1)

            dve.wait_ge(negc_exp, 1)
            nc.vector.tensor_scalar(cE[:, 1], cE[:, 0], 1.0, None, ALU.add).then_inc(silu_c, 1)
            dve.wait_ge(silu_c, 1)
            nc.vector.reciprocal(cE[:, 2], cE[:, 1]).then_inc(silu_c, 1)
            dve.wait_ge(silu_c, 2)
            nc.vector.tensor_tensor(cS[:, :, :], cS[:, :, :], cE[:, 2], ALU.mult).then_inc(silu_c, 1)
            dve.wait_ge(rstd_done, 1)
            normalise_tokens(0, xn[0])
            first_statistics(1)

            def read_mod(n):
                nc.vector.tensor_copy(modT[:, 4 * n:4 * n + 2, :],
                                      allb[7][:, 8 * n:8 * n + 4].rearrange("p (m b) -> p m b", b=B)).then_inc(mod_read, 1)
                nc.vector.tensor_scalar(modT[:, 4 * n + 2:4 * n + 4, :],
                                        allb[7][:, 8 * n + 4:8 * n + 8].rearrange("p (m b) -> p m b", b=B),
                                        1.0, None, ALU.add).then_inc(mod_read, 1)

            def row_maximum(n, u):
                i, diag, _, w = ROWS[u // HG]
                j = u % HG
                dve.wait_ge(m_ps, n * UNITS + (u + 1))
                dst = mxA[:, i, j:j + 1] if diag else mxB[:, i - TPC, j:j + 1]
                nc.vector.tensor_reduce(dst, mbank[u % RING][:, 0:w], AX.X, ALU.max).then_inc(m_red, 1)

            dve.wait_ge(mod_ps, 1)
            read_mod(0)
            dve.wait_ge(silu_c, 3)
            nc.vector.tensor_copy(cB[:, :, :, :], cS[:, :, :].unsqueeze(3).broadcast_to([P, KH, B, P])).then_inc(silu_c, 1)

            def gates():
                dve.wait_ge(mod_ps, 2)
                read_mod(1)
                nc.vector.tensor_copy(modT[:, 8:10, :], allb[7][:, 16:20].rearrange("p (m b) -> p m b", b=B)).then_inc(mod_read, 1)
                dve.wait_ge(gate_ps, 1)
                dve.wait_ge(mod_read, 5)
                ps = allb[6].rearrange("p (b h) -> p b h", b=B)
                for g, sgn, neg in ((ps, gsgn, gneg), (modT[:, 8:10, :], gbS[:, :, :], gbN[:, :, :])):
                    nc.vector.tensor_scalar(sgn, g, 0.0, 2.0, ALU.is_ge, ALU.mult).then_inc(gate_step, 1)
                    nc.vector.tensor_scalar(neg, g, -1.0, 0.25, ALU.mult, ALU.max).then_inc(gate_step, 1)
                dve.wait_ge(gate_step, 4)
                nc.vector.tensor_tensor(gabs, ps, gneg, ALU.max).then_inc(gate_step, 1)
                nc.vector.tensor_tensor(gbA[:, :, :], modT[:, 8:10, :], gbN[:, :, :], ALU.max).then_inc(gate_step, 1)
                dve.wait_ge(gate_step, 6)
                for dst, sgn, mag in ((gate[:, :, :], gsgn, gabs), (modT[:, 8:10, :], gbS[:, :, :], gbA[:, :, :])):
                    nc.vector.scalar_tensor_tensor(out=dst, in0=sgn, scalar=-1.0, in1=mag,
                                                   op0=ALU.add, op1=ALU.mult).then_inc(gate_step, 1)
                dve.wait_ge(gate_step, 8)
                for c in range(NC):
                    nc.vector.tensor_copy(modC[:, :, c], modT[:, 4:10, c // (S // CH)]).then_inc(modC_done, 1)

            for c in range(NC):
                if c + 1 < NC:
                    if c >= 1:
                        dve.wait_ge(xnT_ps, KH * c)
                    dve.wait_ge(rstd_done, c + 2)
                    normalise_tokens(c + 1, xn[(c + 1) % 2])
                if c + 2 < NC:
                    first_statistics(c + 2)
                if c == 1:
                    gates()
                if c < S // CH:
                    for i in range(4):
                        split_tile(dve, nc.vector, c, i)
                for v in range(2):
                    if c == NC - 1:
                        for u in (range(OVER - 2 * PER) if v == 0 else range(OVER - 2 * PER, OVER)):
                            row_maximum(0, u)
                    dve.wait_ge(v_ps, 2 * c + v + 1)
                    if c == 0 and v == 0:
                        dve.wait_ge(v_in, 32)
                    b, kt = c // (S // CH), (c % (S // CH)) * TPC + 2 * v
                    for u in range(2):
                        ins = nc.vector.tensor_tensor(
                            Vall[:, b * NG:(b + 1) * NG, kt + u, :, 0:HD],
                            allb[6 + v][:, u * H:(u + 1) * H].rearrange("p (g j d) -> p g j d", g=NG, j=HG),
                            Bv[:, :].rearrange("p (g j d) -> p g j d", g=NG, j=HG), ALU.add)
                    ins.then_inc(v_read, 1)
            def max_parts(n, half):
                k = n * 9 + 4 * half
                src = mxA[:, half * TPC:(half + 1) * TPC, :]
                if half:
                    dve.wait_ge(m_red, n * UNITS + UNITS)
                    nc.vector.tensor_tensor(src, src, mxB[:, :, :], ALU.max).then_inc(mp_step, 1)
                    dve.wait_ge(mp_step, k + 1)
                    k = k + 1
                else:
                    dve.wait_ge(m_red, n * UNITS + TPC * HG)
                v = src.rearrange("p i j -> p j i")
                if not (isinstance(n, int) and n == 0 and half == 0):
                    dve.wait_ge(mp_step, k)
                nc.vector.tensor_scalar(MP[:, 0], v, -1.0, None, ALU.mult).then_inc(mp_step, 1)
                dve.wait_ge(mp_step, k + 1)
                nc.vector.scalar_tensor_tensor(out=mr[:, :, :], in0=v, scalar=-1.0, in1=MP[:, 0],
                                               op0=ALU.mult, op1=ALU.subtract).then_inc(mp_step, 1)
                dve.wait_ge(mp_step, k + 2)
                nc.vector.tensor_copy(MP[:, 1], mr[:, :, :]).then_inc(mp_step, 1)
                dve.wait_ge(mp_step, k + 3)
                nc.vector.tensor_tensor(MP[:, 2], mr[:, :, :], MP[:, 1], ALU.subtract).then_inc(mp_step, 1)

            def max_copy(n, half, before):
                dve.wait_ge(mpT_ps, n * 2 + (half + 1))
                if before is not None:
                    dve.wait_ge(aug_in[before[0]][half], before[1] * 48 + 48)
                nc.vector.tensor_copy(MT[half][:, :], tb.bitcast(BF16)[0:3 * HG * TPC, 0:P]).then_inc(
                    t_read, 2 if before is None else 1)

            def normalise(o, n, qc):
                ps = tb.rearrange("p (t j d) -> p t j d", t=TPC, j=HG)
                dve.wait_ge(oT_ps, o + 1)
                nc.vector.reciprocal(R[:, :, :], ps[:, :, :, HD]).then_inc(rec_done, 1)
                dve.wait_ge(rec_done, o + 1)
                dst = A[:, qc, :, bass.ds(n, 1), :].rearrange("p t a (j d) -> p (t a) j d", j=HG)
                nc.vector.tensor_tensor(dst, ps[:, :, :, 0:HD],
                                        R[:, :, :].unsqueeze(3).broadcast_to([P, TPC, HG, HD]), ALU.mult).then_inc(t_read, 1)

            def residual(c, i):
                dve.wait_ge(y_ps, 2 * c + i + 1)
                dve.wait_ge(xb_ready, NT + B)
                t = X[:, c * TPC + 2 * i:c * TPC + 2 * i + 2, :]
                nc.vector.tensor_tensor(t, t, allb[LATE_BANK(c, i)].rearrange("p (t h) -> p t h", h=H),
                                        ALU.add).then_inc(x1_ready, 1)

            def tile_of(q, t):
                return X[:, bass.ds(q * TPC + t, 1), :].rearrange("p a h -> p (a h)")

            def statistics(q):
                if isinstance(q, int):
                    dve.wait_ge(x1_ready, 2 * q + 2)
                else:
                    dve.wait_ge(x1_ready, 2 * NC)
                for t in range(TPC):
                    nc.vector.bn_stats(stats2[:, t, :], tile_of(q, t)).then_inc(ln2_step, 1)

            def averages(q):
                k = q * LN2_STEPS
                if isinstance(q, int) and q == 0:
                    dve.wait_ge(ln2_step, TPC)
                for t in range(TPC):
                    nc.vector.bn_aggr(mv2[:, t, :], stats2[:, t, :]).then_inc(ln2_step, 1)
                dve.wait_ge(ln2_step, k + 2 * TPC)
                nc.vector.tensor_scalar(vare2[:, :], mv2[:, :, 1], EPS, None, ALU.add).then_inc(ln2_step, 1)
                dve.wait_ge(ln2_step, k + (2 * TPC + 1))
                nc.vector.reciprocal(rvar2[:, :], vare2[:, :]).then_inc(ln2_step, 1)

            def second_norm(q):
                dve.wait_ge(rstd2_done, q + 1)
                for t in range(TPC):
                    nc.vector.tensor_scalar(xm[:, t, :], tile_of(q, t), mv2[:, t, 0:1], rstd2[:, t:t + 1],
                                            ALU.subtract, ALU.mult).then_inc(xm_ready, 1)

            def split(q, k):
                dve.wait_ge(h2_ready, q * KH + (k + 1))
                hi, lo = (h[:, bass.ds(q, 1), k, :].rearrange("p a t -> p (a t)") for h in (Hh, Hl))
                nc.vector.tensor_copy(hi, hv[:, k, :]).then_inc(h2_hi, 1)
                dve.wait_ge(h2_hi, q * KH + (k + 1))
                nc.vector.tensor_tensor(lo, hv[:, k, :], hi.bitcast(F32), ALU.subtract).then_inc(h2_split, 1)

            def route(c, lo, hi):
                did = [0]
                r = {k: (v[:, :, :] if len(v.shape) == 3 else v[:, :, :, :] if len(v.shape) == 4 else v[:, :])
                     for k, v in rt.items()}

                def step(op, *args, **kw):
                    if lo <= did[0] < hi:
                        if did[0] == 0:
                            dve.wait_ge(logit_ps, c + 1)
                        if did[0] == 2:
                            dve.wait_ge(rexp_done, c + 1)
                        if did[0] or not (isinstance(c, int) and c == 0):
                            dve.wait_ge(route_step, c * ROUTE_STEPS + did[0])
                        op(*args, **kw).then_inc(route_step, 1)
                    did[0] += 1

                def wide(ap, n):
                    return ap.unsqueeze(3).broadcast_to([P, TPC, ap.shape[2], n])

                def each(ap, n):
                    return ap.unsqueeze(2).broadcast_to([P, TPC, n])

                def other(ap):
                    n = ap.shape[2]
                    return ap.unsqueeze(2).broadcast_to([P, TPC, n, n])

                tt, ts, red = nc.vector.tensor_tensor, nc.vector.tensor_scalar, nc.vector.tensor_reduce
                bank = allb[0] if isinstance(c, int) and c == 0 else allb[7]
                logits = bank[:, 0:TPC * NE].rearrange("p (t e) -> p t e", e=NE)
                step(red, r["max"], logits, AX.X, ALU.max)
                step(tt, r["logit"], logits, each(r["max"], NE), ALU.subtract)
                step(red, r["sum"], r["exp"], AX.X, ALU.add)
                step(nc.vector.reciprocal, r["rec"], r["sum"])
                step(tt, r["score"], r["exp"], each(r["rec"], NE), ALU.mult)
                step(red, r["group"], r["score"].rearrange("p t (g e) -> p t g e", g=NGR), AX.X, ALU.max)
                step(tt, r["ggt"], other(r["group"]), wide(r["group"], NGR), ALU.is_gt)
                step(tt, r["geq"], other(r["group"]), wide(r["group"], NGR), ALU.is_equal)
                step(tt, r["geq"], r["geq"], lowg[:, :, :].unsqueeze(1).broadcast_to([P, TPC, NGR, NGR]), ALU.mult)
                step(tt, r["ggt"], r["ggt"], r["geq"], ALU.add)
                step(red, r["grank"], r["ggt"], AX.X, ALU.add)
                step(ts, r["gsel"], r["grank"], float(TOPG), None, ALU.is_lt)
                by_group = "p t (g e) -> p t g e"
                step(tt, r["kept"].rearrange(by_group, g=NGR), r["score"].rearrange(by_group, g=NGR),
                        wide(r["gsel"], EPG), ALU.mult)
                step(nc.vector.scalar_tensor_tensor, out=r["masked"].rearrange(by_group, g=NGR), in0=wide(r["gsel"], EPG),
                                                    scalar=-1.0, in1=r["kept"].rearrange(by_group, g=NGR),
                                                    op0=ALU.add, op1=ALU.add)
                step(tt, r["gt"], other(r["masked"]), wide(r["masked"], NE), ALU.is_gt)
                step(tt, r["eq"], other(r["masked"]), wide(r["masked"], NE), ALU.is_equal)
                step(tt, r["eq"], r["eq"], lower[:, :, :].unsqueeze(1).broadcast_to([P, TPC, NE, NE]), ALU.mult)
                step(tt, r["gt"], r["gt"], r["eq"], ALU.add)
                step(red, r["rank"], r["gt"], AX.X, ALU.add)
                step(nc.vector.scalar_tensor_tensor, out=r["w"], in0=r["rank"], scalar=float(TOPK), in1=r["score"],
                                                    op0=ALU.is_lt, op1=ALU.mult)
                step(red, r["wsum"], r["w"], AX.X, ALU.add)
                step(ts, r["weps"], r["wsum"], 1e-20, None, ALU.add)
                step(nc.vector.reciprocal, r["wrec"], r["weps"])
                step(tt, r["cw"], r["w"], each(r["wrec"], NE), ALU.mult)
                assert did[0] == ROUTE_STEPS

            def copy_weights(q, bank):
                dve.wait_ge(cwT_ps, q + 1)
                if not (isinstance(q, int) and q == 0):
                    dve.wait_ge(cw_out, q * 16)
                nc.vector.tensor_copy(cwT[:, :], bank[0:NE, 0:CH]).then_inc(cwT_ready, 1)

            def body(n, at, first, last):
                if isinstance(n, int) and n == -1:
                    for u in range(OVER, UNITS):
                        row_maximum(0, u)
                        if u == max(OVER, HG * TPC):
                            max_parts(0, 0)
                        if u == max(OVER, HG * TPC) + HG:
                            max_copy(0, 0, None)
                    return
                if last:
                    return late(n)
                max_parts(n, 1)
                for what, i in ORDER:
                    if what == "unit":
                        row_maximum(n + 1, i)
                    if what == "parts":
                        max_parts(n + 1, 0)
                    if what == "max" and i == 1:
                        max_copy(n, 1, None if first else at(-1))
                    if what == "max" and i == 0:
                        max_copy(n + 1, 0, at(0))
                    if what == "out" and i == 1 and not first:
                        normalise(n * 2 - 1, n - 1, 1)
                    if what == "out" and i == 0:
                        normalise(n * 2, n, 0)

            def late(n):
                max_parts(n, 1)
                max_copy(n, 1, ((n - 1) % SLOTS, (n - 1) // SLOTS))
                for i in range(2):
                    residual(0, i)
                statistics(0)
                averages(0)
                normalise(n * 2 - 1, n - 1, 1)
                second_norm(0)
                dve.wait_ge(e_ps, n * HEADS)
                dve.wait_ge(pv_done, n * NS)
                for k in range(KH):
                    split(0, k)
                dve.wait_ge(fconst, 4)
                route(0, 0, 2)
                route(0, 2, 20)
                normalise(n * 2, n, 0)
                for i in range(2):
                    residual(1, i)
                route(0, 20, ROUTE_STEPS)

            attention(body)(dve)

            def finish(c, half):
                dve.wait_ge(yT_ps, c * 2 + (half + 1))
                t = X[:, bass.ds(c * TPC + 2 * half, 2), :]
                nc.vector.tensor_tensor(t, allb[7].rearrange("p (t h) -> p t h", h=H), t, ALU.add).then_inc(fin_done, 1)

            def ffn(c, start, last):
                for f in range(NFT):
                    free = f if f == 0 else f - 1
                    if f == AGGR_AT and not last:
                        dve.wait_ge(ln2_step, c * LN2_STEPS + (LN2_STEPS + TPC))
                    dve.wait_ge(u_ps, c * NFT + (f + 1))
                    dve.wait_ge(silu_done, c * NFT + (f + 1))
                    if not (start and f < 2):
                        dve.wait_ge(a_ready, c * NFT + free)
                    nc.vector.tensor_tensor(su[f % 2][:, :], allb[2 * (f % 2) + 1], sg[f % 2][:, :], ALU.mult).then_inc(u_read, 1)
                    dve.wait_ge(u_read, c * NFT + (f + 1))
                    src = su[f % 2]
                    if f >= NSH:
                        i = f - NSH
                        dve.wait_ge(cw_in[i % CWRING], c * cw_count(NRT - CWRING + i % CWRING) + cw_count(i))
                        nc.vector.tensor_tensor(sw[f % 2][:, :], cwb[i % CWRING][:, :], su[f % 2][:, :],
                                                ALU.mult).then_inc(cwb_read, 1)
                        dve.wait_ge(cwb_read, c * NRT + (f - NSH + 1))
                        src = sw[f % 2]
                    if not (start and f < 2):
                        dve.wait_ge(down_done, c * NFT + free)
                    nc.vector.tensor_copy(ah[f % 2][:, :], src[:, :]).then_inc(hi_done, 1)
                    dve.wait_ge(hi_done, c * NFT + (f + 1))
                    nc.vector.tensor_tensor(al[f % 2][:, :], src[:, :], ah[f % 2][:, :].bitcast(F32),
                                            ALU.subtract).then_inc(a_ready, 1)
                    if f in (3, 5) and not start:
                        finish(c - 1, (f - 3) // 2)
                    if start and f == 0:
                        normalise(2 * NIT - 1, NIT - 1, 1)
                    if start and f == NSH - 1:
                        copy_weights(0, allb[7])
                    if start and f - 1 in PROJECT:
                        for what, cc, i in PROJECT[f - 1]:
                            if what == "project":
                                residual(cc, i)
                    if last:
                        continue
                    if f == STATS_AT:
                        statistics(c + 1)
                    if f == AGGR_AT:
                        averages(c + 1)
                    if f == NORM_AT:
                        second_norm(c + 1)
                    if f - 2 in TURN2_AT:
                        split(c + 1, TURN2_AT.index(f - 2))
                    if f == SOFTMAX_AT:
                        route(c + 1, 0, 2)
                    if ROUTE_AT <= f < TURNW_AT:
                        steps = [2 + (ROUTE_STEPS - 2) * (f + d - ROUTE_AT) // (TURNW_AT - ROUTE_AT) for d in range(2)]
                        route(c + 1, *steps)
                    if f == TURNW_AT:
                        copy_weights(c + 1, allb[7])

            chunks(ffn)(dve)
            finish(NC - 1, 0)
            finish(NC - 1, 1)

        @block.tensor
        def _(pe):
            def modulation(ms, n0):
                for n, m in enumerate(ms):
                    for k in range(KH):
                        ins = nc.tensor.matmul(allb[7][:, (n0 + n) * B:(n0 + n + 1) * B], Wm[:, k, m * P:(m + 1) * P],
                                               cS[:, k, :], start=(k == 0), stop=(k == KH - 1))
                ins.then_inc(mod_ps, 1)

            def gate_rows():
                for b in range(B):
                    for k in range(KH):
                        ins = nc.tensor.matmul(allb[6][:, b * H:(b + 1) * H], cB[:, k, b, :],
                                               Wm[:, k, 2 * H:3 * H], start=(k == 0), stop=(k == KH - 1))
                ins.then_inc(gate_ps, 1)

            def turn(c):
                for k in range(KH):
                    n = KH * c + k
                    pe.wait_ge(xn_ready, TPC * (c + 1))
                    if n >= KH:
                        pe.wait_ge(hT_ready, n - KH + 1)
                    for t in range(TPC):
                        ins = nc.tensor.transpose(allb[k][:, t * P:(t + 1) * P], xn[c % 2][:, t, k * P:(k + 1) * P], ident[:, :])
                    ins.then_inc(xnT_ps, 1)

            def score_unit(n, slot, u):
                i, diag, k0, w = ROWS[u // HG]
                j = u % HG
                if not (isinstance(n, int) and n == 0 and u < RING):
                    pe.wait_ge(m_red, n * UNITS + (u - RING + 1))
                if diag:
                    nc.tensor.matmul(mbank[u % RING][:, w - P:w], identb[:, :], mask[:, :], start=True, stop=False,
                                     skip_group_check=True)
                nc.tensor.matmul(mbank[u % RING][:, 0:w], Qs[slot][0:NPR, i // TPC, j, (i % TPC) * P:(i % TPC + 1) * P],
                                 Ks[slot][0:NPR, j, k0:k0 + w], start=not diag, stop=True,
                                 skip_group_check=True).then_inc(m_ps, 1)

            pe.wait_ge(ident_done, 2)
            turn(0)
            pe.wait_ge(mod_in, 16)
            pe.wait_ge(silu_c, 3)
            modulation(range(4), 0)
            pe.wait_ge(qk_in, 32)
            for c in range(NC):
                pe.wait_ge(hT_ready, KH * (c + 1))
                if c == NC - 1:
                    pe.wait_ge(const_done, N_CONST)
                    pe.wait_ge(staged[0], 16 * STAGE_DMAS)
                for i, m in enumerate(M_ORDER):
                    n = 4 * c + i
                    if n >= QK_RING:
                        pe.wait_ge(qk_read, 2 * (n - QK_RING + 1))
                    for k in range(KH):
                        ins = nc.tensor.matmul(allb[QK_RING + n % QK_RING], Wqk[:, k, m * P:(m + 1) * P],
                                               hT[:, k, c * CH:(c + 1) * CH], start=(k == 0), stop=(k == KH - 1))
                        if k == KH - 1:
                            ins.then_inc(qk_ps, 1)
                        if c == NC - 1:
                            for u in range(PER):
                                score_unit(0, 0, PER * (KH * i + k) + u)
                if c + 1 < NC:
                    turn(c + 1)
                if c == 0:
                    pe.wait_ge(v_in, 32)
                    pe.wait_ge(mod_read, 2)
                if c == 1:
                    pe.wait_ge(gate_step, 6)
                    pe.wait_ge(mod_read, 5)
                for v in range(2):
                    if c:
                        pe.wait_ge(v_read, 2 * (c - 1) + v + 1)
                    for u in range(2):
                        t0 = c * CH + (2 * v + u) * P
                        for k in range(KH):
                            ins = nc.tensor.matmul(allb[6 + v][:, u * H:(u + 1) * H], hT[:, k, t0:t0 + P], Wv[:, k, :],
                                                   start=(k == 0), stop=(k == KH - 1))
                        if u == 1:
                            ins.then_inc(v_ps, 1)
                        if c == NC - 1:
                            for w in range(PER):
                                score_unit(0, 0, OVER - PER * (4 - 2 * v - u) + w)
                if c == 0:
                    pe.wait_ge(w_in, 16 * W_DMAS)
                    pe.wait_ge(v_read, 2)
                    modulation(range(6, 12), 4)
                    pe.wait_ge(silu_c, 4)
                    gate_rows()

            def turn_max_waits(n, half, event):
                pe.wait_ge(mp_step, n * 9 + (9 if half else 4))
                if event is not None:
                    pe.wait_ge(t_read, event)

            def turn_max():
                nc.tensor.transpose(tb.bitcast(BF16)[0:3 * HG * TPC, 0:P],
                                    MP[:, :, :, :].rearrange("p a j i -> p (a j i)"), identb[:, :]).then_inc(mpT_ps, 1)

            def turn_out(o, qc, event):
                pe.wait_ge(ot_ready, o + 1)
                pe.wait_ge(t_read, event)
                for t in range(TPC):
                    ins = nc.tensor.transpose(tb[:, t * P:(t + 1) * P], OT[qc][:, t * P:(t + 1) * P], ident[:, :])
                ins.then_inc(oT_ps, 1)

            def products(n, slot, s):
                qc, kt = STEPS[s]
                q0 = max(0, kt - TPC * qc) * P
                w = CH - q0
                pe.wait_ge(exp_done, n * (EXP * HEADS) + EXP * HG * (s + 1))
                if kt == 0 and not (isinstance(n, int) and n == 0 and qc == 0):
                    pe.wait_ge(ot_ready, n * 2 + qc)
                for j in range(HG):
                    ins = nc.tensor.matmul(pvb[32 * j:32 * j + 32, q0:CH], Vst[slot][:, kt, 32 * j:32 * j + 32],
                                           Pr[(2 * s + j // 2) % 4][:, j % 2, 0:w],
                                           start=(kt == 0), stop=(kt == TPC * (qc + 1) - 1), skip_group_check=True)
                ins.then_inc(pv_done, 1)

            def scores(n, slot, turn, p):
                s, j = p // HG, p % HG
                qc, kt = STEPS[s]
                q0 = max(0, kt - TPC * qc) * P
                if kt == 0 and j == 0:
                    pe.wait_ge(aug_in[slot][qc], turn * 48 + 48)
                if not (isinstance(n, int) and n == 0 and p < RING):
                    pe.wait_ge(exp_done, n * (EXP * HEADS) + EXP * (p - RING + 1))
                if on_diagonal(s):
                    nc.tensor.matmul(ebank[p % RING][:, 0:P], identb[:, :], maskT[:, :], start=True, stop=False,
                                     skip_group_check=True)
                nc.tensor.matmul(ebank[p % RING][:, 0:CH - q0], Ks[slot][0:NAUG, j, kt * P:(kt + 1) * P],
                                 Qs[slot][0:NAUG, qc, j, q0:CH], start=not on_diagonal(s), stop=True,
                                 skip_group_check=True).then_inc(e_ps, 1)

            def turn_attention(c, k):
                b, qc = c // (S // CH), c % (S // CH)
                for t in range(TPC):
                    src = A[:, qc, t, b * NG + 2 * k:b * NG + 2 * k + 2, :].rearrange("p g d -> p (g d)")
                    ins = nc.tensor.transpose(allb[LATE_BANK(c, k)][:, t * P:(t + 1) * P], src, ident[:, :])
                ins.then_inc(aT_ps, 1)

            def project(c, i):
                pe.wait_ge(aT_ready, KH * (c + 1))
                if c == 0 and i == 0:
                    pe.wait_ge(wog_done, B * KH)
                for u in range(2):
                    t = 2 * i + u
                    for k in range(KH):
                        ins = nc.tensor.matmul(allb[LATE_BANK(c, i)][:, u * H:(u + 1) * H], AT[:, k, t * P:(t + 1) * P],
                                               Wog[:, c // (S // CH), k, :], start=(k == 0), stop=(k == KH - 1))
                ins.then_inc(y_ps, 1)

            def turn2(q, k, bank):
                pe.wait_ge(xm_ready, q * TPC + TPC)
                for t in range(TPC):
                    ins = nc.tensor.transpose(bank[:, t * P:(t + 1) * P], xm[:, t, k * P:(k + 1) * P], ident[:, :])
                ins.then_inc(x2T_ps, 1)

            def logits(q, bank):
                pe.wait_ge(h2_ready, q * KH + KH)
                for t in range(TPC):
                    for k in range(KH):
                        ins = nc.tensor.matmul(bank[:, t * NE:(t + 1) * NE], hv[:, k, t * P:(t + 1) * P],
                                               Wg[:, k, :], start=(k == 0), stop=(k == KH - 1))
                ins.then_inc(logit_ps, 1)

            def turn_weights(q, bank):
                pe.wait_ge(route_step, q * ROUTE_STEPS + ROUTE_STEPS)
                for t in range(TPC):
                    ins = nc.tensor.transpose(bank[0:NE, t * P:(t + 1) * P], rt["cw"][:, t, :], ident[:, :])
                ins.then_inc(cwT_ps, 1)

            def late(s):
                if s == 0:
                    pe.wait_ge(m_red, NIT * UNITS)
                if s in (0, 6):
                    if s == 6:
                        pe.wait_ge(route_step, 2)
                    for k in range(KH):
                        turn_attention(s // 6, k)
                if s in (1, 7):
                    for i in range(2):
                        project(s // 7, i)
                if s == 4:
                    for k in range(KH):
                        turn2(0, k, allb[k])
                if s == 5:
                    pe.wait_ge(wg_in, 16)
                    logits(0, allb[0])

            def body(n, at, first, last):
                if isinstance(n, int) and n == -1:
                    for u in range(OVER, UNITS):
                        score_unit(0, 0, u)
                        if u == max(OVER, HG * TPC) + HG:
                            pe.wait_ge(v_read, 2 * NC)
                            turn_max_waits(0, 0, None)
                            turn_max()
                    pe.wait_ge(qk_read, 2 * 4 * NC)
                    return
                (slot, turn), (nxt, nxt_turn) = at(0), at(1)
                pe.wait_ge(staged_v[slot], turn * 16 + 16)
                if not last:
                    pe.wait_ge(staged[nxt], nxt_turn * (16 * STAGE_DMAS) + 16 * STAGE_DMAS)
                for what, i in ORDER:
                    if what == "scores":
                        scores(n, slot, turn, i)
                    if what == "unit" and not last:
                        score_unit(n + 1, nxt, i)
                    if what == "products":
                        if i == 0:
                            turn_max_waits(n, 1, t_event(n, "max1"))
                        if i == 5 and not last:
                            turn_max_waits(n + 1, 0, t_event(n, "max0"))
                        if i >= 0:
                            products(n, slot, i)
                        elif not first:
                            products(n - 1, at(-1)[0], NS - 1)
                    if what == "max" and (i == 1 or not last):
                        turn_max()
                    if what == "out" and i == 1 and not first:
                        turn_out(n * 2 - 1, 1, t_event(n, "out1"))
                    if what == "out" and i == 0:
                        turn_out(n * 2, 0, t_event(n, "out0"))
                    if what == "products" and last:
                        late(i + 1)
            attention(body)(pe)
            products(NIT - 1, (NIT - 1) % SLOTS, NS - 1)
            pe.wait_ge(exp_done, NIT * EXP * HEADS)
            pe.wait_ge(x1_ready, 2 * (S // CH))
            pe.wait_ge(h2_split, KH)

            def up(c, f):
                r = f % WRING
                pe.wait_ge(w_lo, c * NFT + (f + 1))
                if not (isinstance(c, int) and c == 0 and f < 2):
                    pe.wait_ge(u_read, c * NFT + (f if f == 0 else f - 1))
                for which, done in ((0, g_ps), (1, u_ps)):
                    for k in range(KH):
                        def part(h):
                            return h[:, bass.ds(c, 1), k, :].rearrange("p a t -> p (a t)")
                        w = slice((which * KH + k) * P, (which * KH + k + 1) * P)
                        for n, (wt, ht) in enumerate(((Wh, Hh), (Wh, Hl), (Wl, Hh))):
                            ins = nc.tensor.matmul(allb[2 * (f % 2) + which], wt[r][:, w], part(ht),
                                                   start=(k == 0 and n == 0), stop=(k == KH - 1 and n == 2))
                    ins.then_inc(done, 1)

            def down(c, f):
                r = f % WRING
                pe.wait_ge(a_ready, c * NFT + (f + 1))
                if f == 0:
                    if isinstance(c, int) and c == 0:
                        pe.wait_ge(ot_ready, 2 * NIT)
                    else:
                        pe.wait_ge(y_read, c * 2)
                for m in range(KH):
                    w = slice(2 * KH * P + m * P, 2 * KH * P + (m + 1) * P)
                    for n, (wt, at) in enumerate(((Wh, ah), (Wh, al), (Wl, ah))):
                        ins = nc.tensor.matmul(allb[5 + m], wt[r][:, w], at[f % 2][:, :],
                                               start=(f == 0 and n == 0), stop=(f == NFT - 1 and n == 2))
                ins.then_inc(down_done, 1)

            def turn_back(c, half):
                pe.wait_ge(y_read, c * 2 + 2)
                if half == 0:
                    if not (isinstance(c, int) and c == NC - 1):
                        pe.wait_ge(cwT_ready, c + 2)
                else:
                    pe.wait_ge(fin_done, c * 2 + 1)
                for t in range(2):
                    for m in range(KH):
                        ins = nc.tensor.transpose(allb[7][:, t * H + m * P:t * H + (m + 1) * P],
                                                  Ys[:, m, (2 * half + t) * P:(2 * half + t + 1) * P], ident[:, :])
                ins.then_inc(yT_ps, 1)

            def beside(c, f, start):
                if f == TURN2_AT[0]:
                    if start:
                        pe.wait_ge(cwT_ready, 1)
                    else:
                        pe.wait_ge(fin_done, c * 2)
                    turn2(c + 1, 0, allb[7])
                if f == TURN2_AT[1]:
                    pe.wait_ge(h2_ready, c * KH + (KH + 1))
                    turn2(c + 1, 1, allb[7])
                if f == LOGITS_AT:
                    logits(c + 1, allb[7])
                if f == TURNW_AT:
                    turn_weights(c + 1, allb[7])

            def ffn(c, start, last):
                for f in range(NFT):
                    up(c, f)
                    if f:
                        down(c, f - 1)
                    elif not start:
                        down(c - 1, NFT - 1)
                    if f in (2, 4) and not start:
                        turn_back(c - 1, (f - 2) // 2)
                    if start and f == 0:
                        turn_out(2 * NIT - 1, 1, t_event(NIT - 1, "out0") + 1)
                    if start and f == NSH - 1:
                        pe.wait_ge(t_read, t_event(NIT - 1, "out0") + 2)
                        turn_weights(0, allb[7])
                    if start:
                        for what, cc, i in PROJECT.get(f, ()):
                            if what == "turn":
                                if i:
                                    pe.wait_ge(aT_ready, KH * cc + 1)
                                elif cc == S // CH:
                                    pe.wait_ge(route_step, ROUTE_STEPS + 2)
                                else:
                                    pe.wait_ge(x1_ready, 2 * cc)
                                turn_attention(cc, i)
                            else:
                                if i:
                                    pe.wait_ge(x1_ready, 2 * cc + 1)
                                project(cc, i)
                    if not last:
                        if start and f == TURNW_AT:
                            pe.wait_ge(x1_ready, 2 * NC)
                        beside(c, f, start)

            chunks(ffn)(pe)
            down(NC - 1, NFT - 1)
            turn_back(NC - 1, 0)
            turn_back(NC - 1, 1)


def kernel(**inputs):
    import numpy as np
    import concourse.bacc as bacc
    from concourse.bass_utils import run_bass_kernel_spmd as run

    def kmajor(w):
        w = np.asarray(w).T
        return np.ascontiguousarray(w.reshape(w.shape[0] // 128, 128, w.shape[1]).transpose(1, 0, 2))

    nc = bacc.Bacc("TRN2", target_bir_lowering=False, num_devices=1)
    wqkv = np.asarray(inputs["L0_attn_W_qkv"])
    bqkv = np.asarray(inputs["L0_attn_b_qkv"])
    arrays = {
        "x": np.asarray(inputs["L0_attn_x"]).reshape(T, H),
        "wqk": kmajor(wqkv[:2 * H]),
        "bqk": bqkv[:2 * H].reshape(4, 128).T,
        "wv": kmajor(wqkv[2 * H:]),
        "bv": bqkv[2 * H:],
        "wout": kmajor(inputs["L0_attn_W_out"]),
        "bout": np.asarray(inputs["L0_attn_b_out"]),
        "cT": kmajor(inputs["L0_c"]),
        "wmod": kmajor(np.asarray(inputs["L0_wmod"]).T),
    }
    up, down = np.asarray(inputs["L0_ffn_expert_up_w"]), np.asarray(inputs["L0_ffn_expert_down_w"])
    sup, sdown = np.asarray(inputs["L0_ffn_shared_up_w"]), np.asarray(inputs["L0_ffn_shared_down_w"])

    def tiles(gate, upw, downw):
        n = -(-gate.shape[0] // 128)
        room = ((0, n * 128 - gate.shape[0]), (0, 0))
        g, u, d = (np.pad(a, room).reshape(n, 128, 256) for a in (gate, upw, downw.T))
        g, u = (a.reshape(n, 128, 2, 128).transpose(0, 3, 2, 1).reshape(n, 128, 256) for a in (g, u))
        return np.concatenate([g, u, d], axis=2)

    arrays["wgate"] = kmajor(inputs["L0_ffn_gate_w"])
    arrays["wffn"] = np.concatenate([
        tiles(sup[:SI], sup[SI:], sdown),
        tiles(up[:, :EI].reshape(-1, H), up[:, EI:].reshape(-1, H), down.transpose(1, 0, 2).reshape(H, -1)),
    ])
    maps, args = {}, []
    for name, a in arrays.items():
        a = np.ascontiguousarray(a)
        maps["in_" + name] = a
        args.append(nc.dram_tensor("in_" + name, a.shape, mybir.dt.from_np(a.dtype), kind="ExternalInput").ap())
    args.append(nc.dram_tensor("qk_parts", (2, B, H, len(Q_PARTS), S), BF16, kind="Internal").ap())
    args.append(nc.dram_tensor("routing_weights", (NE, T), F32, kind="Internal").ap())
    args.append(nc.dram_tensor("out", (T, H), F32, kind="ExternalOutput").ap())
    program(nc, *args)
    r = run(nc, [maps], core_ids=[0])
    return r.results[0]["out"].reshape(B, S, H)
```

```python
from contextlib import ExitStack

import concourse.bass as bass
from concourse import mybir

F32 = mybir.dt.float32
BF16 = mybir.dt.bfloat16
ALU = mybir.AluOpType
ACT = mybir.ActivationFunctionType
AX = mybir.AxisListType

P = 128
B, S, H = 2, 1024, 256
NH, HD = 16, 16
T = B * S
KH = H // P
NT = T // P
CH = 512
NC = T // CH
TPC = CH // P
HG = 4
NG = NH // HG
NIT = B * NG
KT = S // P
EPS = 1e-5
SCALE = float(HD) ** -0.5
NEG = -1.0e30
F32R = mybir.dt.float32r

NE, EI = 16, 176
NGR, TOPG, TOPK = 4, 2, 4
EPG = NE // NGR
SI = 2 * EI
NSH = -(-SI // P)
NRT = NE * EI // P
NFT = NSH + NRT
WF = 2 * KH * P + H
CWRING = 2
CW_LAG = 4
WRING = 5
AHEAD = 2
assert NFT % WRING == 0 and NRT % CWRING == 0
CW_RUNS = [[(e, max(0, e * EI - i * P), min(P, (e + 1) * EI - i * P))
            for e in range(i * P // EI, ((i + 1) * P - 1) // EI + 1)] for i in range(NRT)]


def cw_count(i):
    return 16 * sum(len(CW_RUNS[k]) for k in range(i % CWRING, i + 1, CWRING))


ROUTE_STEPS = 24
SLOTS = 3
LAST_SLOT = (NIT - 1) % SLOTS
SLOT_ORDER = [i for i in range(SLOTS) if i != LAST_SLOT] + [LAST_SLOT]
EARLY_BYTES = 4 * (4 * KH * CH + 2 * CH + 2 * KH * 2 * H + 2 * KH * H + KH * 6 * H + 4 + H)
LATE_BYTES = 4 * (2 * KH * CH + TPC * H + B * KH * H + KH * NE + NE * NE + NGR * NGR
                  + TPC * (6 + 8 * NE + 3 * NGR + 2 * NGR * NGR + 2 * NE * NE)
                  + (CWRING + 1) * CH)

Q_PARTS = (0, 1, 2, 0, 1, 0)
K_PARTS = (0, 0, 0, 1, 1, 2)
NPR = len(Q_PARTS) * HD
NAUG = NPR + 3
STAGE_DMAS = S // CH + 1
PART_RUNS = (((0, 3, 0), (3, 2, 0), (5, 1, 0)), ((0, 3, 0), (3, 2, 1), (5, 1, 2)))
assert all(Q_PARTS[f + i] == p + i for f, n, p in PART_RUNS[0] for i in range(n))
assert all(K_PARTS[f + i] == p for f, n, p in PART_RUNS[1] for i in range(n))

ROWS = [(i, True, 0, (i + 1) * P) for i in range(TPC)]
for _i in range(TPC, KT):
    ROWS += [(_i, False, 0, CH), (_i, True, CH, (_i + 1) * P - CH)]
STEPS = [(qc, kt) for qc in range(S // CH) for kt in range(TPC * (qc + 1))]
NS = len(STEPS)
UNITS = len(ROWS) * HG
HEADS = NS * HG
EXP = 2
RING = 3
assert UNITS % RING == 0 and HEADS % RING == 0
assert len(ROWS) == NS


def on_diagonal(s):
    qc, kt = STEPS[s]
    return kt >= TPC * qc


EXTRA = 120
PRODUCTS_AFTER = HG - 1


def masked_before(s):
    return sum(HG // 2 for t in range(s) if on_diagonal(t))


NMASK = masked_before(NS)


def interleave():
    unit_cost = [w + 200 for _, _, _, w in ROWS for _ in range(HG)]
    head_cost = [CH - max(0, kt - TPC * qc) * P + EXTRA for qc, kt in STEPS for _ in range(HG)]
    order, u, units, heads = [], 0, 0, 0
    for p in range(HEADS):
        s = p // HG
        order.append(("scores", p))
        heads += head_cost[p]
        while u < UNITS and units * sum(head_cost) < heads * sum(unit_cost):
            order.append(("unit", u))
            units += unit_cost[u]
            u += 1
            if u == HG * TPC:
                order.append(("parts", 0))
        if p % HG == PRODUCTS_AFTER:
            order.append(("products", s - 1))
            if s == 1:
                order.append(("max", 1))
            if s == 3:
                order.append(("out", 1))
            if s == 6:
                order.append(("max", 0))
            if s == 8:
                order.append(("out", 0))
    assert u == UNITS and order.index(("parts", 0)) < order.index(("max", 0))
    return order


ORDER = interleave()

BACK = (7, 4)
LATE_PROJECT = (5, 7, 9, 12, 34, 36, 39, 42)
LATE_TURN, LATE_ROOT, LATE_TURN2 = (0, 7), 3, 5
M_ORDER = (0, 2, 1, 3)
QK_RING = 3
PER = 3
OVER = PER * (4 * KH + 4)

LN2_STEPS = 2 * TPC + 2
STATS_AT, AGGR_AT, ROOT_AT, NORM_AT = 1, 2, 3, 4
TURN2_AT = (6, 8)
LOGITS_AT = 10
SOFTMAX_AT, EXP_AT, ROUTE_AT = 11, 12, 13
TURNW_AT = NFT - 1
ROUTE_CUTS = (2, 5, 8, 11, 14, 15, 16, 17, 18, 19, 22, ROUTE_STEPS)
assert len(ROUTE_CUTS) == TURNW_AT - ROUTE_AT + 1
PROJECT = {}
for _c, _f in ((2, 12), (3, 18)):
    PROJECT.update({_f: [("turn", _c, 0)], _f + 1: [("turn", _c, 1)], _f + 2: [("project", _c, 0)],
                    _f + 4: [("project", _c, 1)]})


def LATE_BANK(c, i):
    return i if c < S // CH else 7


def program(nc, x, wqk, bqk, wv, bv, wout, bout, cT, wmod, wgate, wffn, qkd, cwd, out):
    with ExitStack() as ctx:
        scope = [ctx]

        def sb(name, shape, dt):
            return scope[-1].enter_context(nc.sbuf_tensor(name, shape, dt))

        def sem(name):
            return ctx.enter_context(nc.semaphore(name))

        X = sb("X", [P, NT, H], F32)
        Wo = sb("Wo", [P, KH, H], F32)
        Bo = sb("Bo", [P, H], F32)
        cS = sb("cS", [P, KH, B], F32)
        cE = sb("cE", [P, 3, KH, B], F32)
        modT = sb("modT", [P, 10, B], F32)
        gbS, gbN, gbA = (sb(n, [P, KH, B], F32) for n in ("gbS", "gbN", "gbA"))
        gate = sb("gate", [P, B, H], F32)
        gbias = sb("gbias", [P, B, H], F32)
        ident = sb("ident", [P, P], F32)
        identb = sb("identb", [P, P], BF16)
        mask = sb("mask", [P, P], BF16)
        stats = sb("stats", [P, NT, 6], F32)
        mv = sb("mv", [P, NT, 2], F32)
        vare, rvar, rstd = (sb(n, [P, NT], F32) for n in ("vare", "rvar", "rstd"))
        stats2 = sb("stats2", [P, TPC, 6], F32)
        mv2 = sb("mv2", [P, TPC, 2], F32)
        vare2, rvar2, rstd2 = (sb(n, [P, TPC], F32) for n in ("vare2", "rvar2", "rstd2"))
        modC = sb("modC", [P, 6, NC], F32)
        AP = sb("AP", [P, 2, 3, 4, CH], BF16)
        PT = [AP[:, i] for i in range(2)]
        A = AP[:, :, :, :, :].rearrange("p i a m c -> p (i a m c)").bitcast(F32)[:, 0:NIT * CH].rearrange(
            "p (q t n d) -> p q t n d", n=NIT, q=S // CH, t=TPC)
        OT = [sb(f"OT{i}", [P, CH], F32) for i in range(2)]
        mxA = sb("mxA", [P, KT, HG], F32)
        mxB = sb("mxB", [P, TPC, HG], F32)
        mr = sb("mr", [P, HG, TPC], F32)
        MP = sb("MP", [P, 3, HG, TPC], BF16)
        MT = [sb(f"MT{i}", [3 * HG * TPC, P], BF16) for i in range(2)]
        R = sb("R", [P, TPC, HG], F32)
        tick = sb("tick", [P, NMASK], F32)

        early = ctx.enter_context(ExitStack())
        scope.append(early)
        hh = [sb(f"hh{i}", [P, KH, CH], F32R) for i in range(2)]
        hl = [sb(f"hl{i}", [P, KH, CH], F32R) for i in range(2)]
        Rq = [sb(f"Rq{i}", [P, CH], F32) for i in range(2)]
        Wqkh, Wqkl = (sb(n, [P, KH, 2 * H], F32R) for n in ("Wqkh", "Wqkl"))
        Wvh, Wvl = (sb(n, [P, KH, H], F32R) for n in ("Wvh", "Wvl"))
        Wm = sb("Wm", [P, KH, 6 * H], F32)
        Bqk = sb("Bqk", [P, 4], F32)
        Bv = sb("Bv", [P, H], F32)
        scope.pop().close()

        AT = sb("AT", [P, KH, CH], F32)
        xm = sb("xm", [P, TPC, H], F32)
        hv = sb("hv", [P, KH, CH], F32)
        Wog = sb("Wog", [P, B, KH, H], F32)
        Wg = sb("Wg", [P, KH, NE], F32)
        lower = sb("lower", [P, NE, NE], F32)
        lowg = sb("lowg", [P, NGR, NGR], F32)
        cwT = sb("cwT", [NE, CH], F32)
        cwb = [sb(f"cwb{i}", [P, CH], F32) for i in range(CWRING)]
        rt = {name: sb("rt_" + name, [P, TPC] + shape, F32) for name, shape in (
            ("max", []), ("sum", []), ("rec", []), ("logit", [NE]), ("exp", [NE]), ("score", [NE]), ("group", [NGR]),
            ("ggt", [NGR, NGR]), ("geq", [NGR, NGR]), ("grank", [NGR]),
            ("gsel", [NGR]), ("kept", [NE]), ("masked", [NE]), ("gt", [NE, NE]), ("eq", [NE, NE]),
            ("rank", [NE]), ("w", [NE]), ("wsum", []), ("weps", []), ("wrec", []), ("cw", [NE]))}
        pad = EARLY_BYTES - LATE_BYTES
        if pad > 0:
            sb("room", [P, pad // 4], F32)

        scope.append(ctx.enter_context(ExitStack()))
        Vall = sb("Vall", [P, NIT, KT, HG, 32], F32)
        Qs, Ks, Vst = {}, {}, {}
        for i in SLOT_ORDER:
            Qs[i] = sb(f"Qs{i}", [P, S // CH, HG, CH], BF16)
            Ks[i] = sb(f"Ks{i}", [P, HG, S], BF16)
            Vst[i] = sb(f"Vst{i}", [P, KT, HG * 32], F32)
        Pr = [sb(f"Pr{i}", [P, 2, CH], F32) for i in range(4)]
        raw = Qs[2][:, :, :, :].rearrange("p a j c -> p (a j c)").bitcast(F32)
        Wqk = raw[:, 0:KH * 2 * H].rearrange("p (k n) -> p k n", k=KH)
        Wv = raw[:, KH * 2 * H:KH * 3 * H].rearrange("p (k n) -> p k n", k=KH)
        cB = raw[:, KH * 3 * H:KH * 3 * H + KH * B * P].rearrange("p (k b n) -> p k b n", k=KH, b=B)
        xn = [Pr[i][:, :, :].rearrange("p a (t h) -> p (a t) h", h=H) for i in range(2)]
        Fq = [Pr[2 + m // 2][:, m % 2, :] for m in range(4)]
        gsgn, gneg, gabs = (Vst[i][:, 0:KT // 2, :].rearrange("p k (b h) -> p (k b h)", b=1).rearrange(
            "p (b h) -> p b h", b=B) for i in range(3))
        scope.pop().close()

        Wr = [sb(f"Wr{i}", [P, WF], F32) for i in range(WRING)]
        Wh = [sb(f"Wh{i}", [P, WF], F32R) for i in range(WRING)]
        Wl = [sb(f"Wl{i}", [P, WF], F32R) for i in range(WRING)]
        Hh = sb("Hh", [P, NC, KH, CH], F32R)
        Hl = sb("Hl", [P, NC, KH, CH], F32R)
        sg = [sb(f"sg{i}", [P, CH], F32) for i in range(2)]
        su = [sb(f"su{i}", [P, CH], F32) for i in range(2)]
        sw = [sb(f"sw{i}", [P, CH], F32) for i in range(2)]
        ah = [sb(f"ah{i}", [P, CH], F32R) for i in range(2)]
        al = [sb(f"al{i}", [P, CH], F32R) for i in range(2)]
        Ys = sb("Ys", [P, KH, CH], F32)

        allb = [ctx.enter_context(nc.psum_tensor(f"bank{i}", [P, CH], F32))[:, :] for i in range(8)]
        mbank, ebank, pvb, tb = allb[0:RING], allb[RING:2 * RING], allb[6], allb[7]

        x_in = [sem(f"x_in{c}") for c in range(NC)]
        c_in = sem("c_in")
        mod_in = sem("mod_in")
        qk_in = sem("qk_in")
        v_in = sem("v_in")
        w_in = sem("w_in")
        ident_done = sem("ident_done")
        const_done = sem("const_done")
        negc_exp = sem("negc_exp")
        silu_c = sem("silu_c")
        mod_ps = sem("mod_ps")
        mod_read = sem("mod_read")
        gate_ps = sem("gate_ps")
        gate_step = sem("gate_step")
        modC_done = sem("modC_done")
        ln_step = sem("ln_step")
        rstd_done = sem("rstd_done")
        xn_ready = sem("xn_ready")
        xnT_ps = sem("xnT_ps")
        hT_ready = sem("hT_ready")
        hT_low = sem("hT_low")
        wsplit_hi = sem("wsplit_hi")
        wsplit_lo = sem("wsplit_lo")
        qk_ps = sem("qk_ps")
        qk_read = sem("qk_read")
        parts_done = [sem(f"parts_done{i}") for i in range(B)]
        split_step = sem("split_step")
        rest_done = sem("rest_done")
        round_done = sem("round_done")
        parts_out = [sem(f"parts_out{i}") for i in range(2)]
        v_ps = sem("v_ps")
        v_read = sem("v_read")
        staged_v = [sem(f"staged_v{i}") for i in range(SLOTS)]
        staged = [sem(f"staged{i}") for i in range(SLOTS)]
        m_ps = sem("m_ps")
        m_red = sem("m_red")
        mp_step = sem("mp_step")
        mpT_ps = sem("mpT_ps")
        t_read = sem("t_read")
        aug_in = [[sem(f"aug_in{i}_{h}") for h in range(2)] for i in range(SLOTS)]
        e_ps = sem("e_ps")
        exp_done = sem("exp_done")
        masked = sem("masked")
        pv_done = sem("pv_done")
        xg_ready = sem("xg_ready")
        ot_ready = sem("ot_ready")
        oT_ps = sem("oT_ps")
        rec_done = sem("rec_done")
        aT_ps = sem("aT_ps")
        aT_ready = sem("aT_ready")
        y_ps = sem("y_ps")
        xb_ready = sem("xb_ready")
        wog_done = sem("wog_done")
        x1_ready = sem("x1_ready")
        out_done = sem("out_done")
        fconst = sem("fconst")
        ln2_step = sem("ln2_step")
        rstd2_done = sem("rstd2_done")
        xm_ready = sem("xm_ready")
        wg_in = sem("wg_in")
        x2T_ps = sem("x2T_ps")
        h2_ready = sem("h2_ready")
        h2_hi = sem("h2_hi")
        h2_split = sem("h2_split")
        logit_ps = sem("logit_ps")
        rexp_done = sem("rexp_done")
        route_step = sem("route_step")
        cwT_ps = sem("cwT_ps")
        cwT_ready = sem("cwT_ready")
        w_raw = [sem(f"w_raw{i}") for i in range(WRING)]
        w_hi = sem("w_hi")
        w_lo = sem("w_lo")
        cw_out = sem("cw_out")
        cw_in = [sem(f"cw_in{i}") for i in range(CWRING)]
        silu_done = sem("silu_done")
        u_read = sem("u_read")
        u_ps = sem("u_ps")
        g_ps = sem("g_ps")
        hi_done = sem("hi_done")
        cwb_read = sem("cwb_read")
        a_ready = sem("a_ready")
        down_done = sem("down_done")
        y_read = sem("y_read")
        yT_ps = sem("yT_ps")
        fin_done = sem("fin_done")

        W_DMAS = 3
        N_CONST = 5 + SLOTS
        block = ctx.enter_context(nc.Block())

        def t_event(n, kind):
            last = isinstance(n, int) and n == NIT - 1
            return n * 4 + {"max1": 2, "out1": 3, "max0": 4, "out0": 4 if last else 5}[kind]

        def low_part(eng, ops, c):
            for k in range(KH):
                eng.wait_ge(hT_ready, 2 * (KH * c + k) + 2)
                ops.tensor_tensor(hl[c % 2][:, k, :], OT[k][:, :], hh[c % 2][:, k, :].bitcast(F32),
                                  ALU.subtract).then_inc(hT_low, 1)

        def aug(queue, slot, half):
            for part in range(3):
                queue.dma_start(
                    Qs[slot][NPR + part:NPR + part + 1, half, :, :].rearrange("o j (i q) -> o (j i) q", i=TPC),
                    MT[half][part * HG * TPC:(part + 1) * HG * TPC, :]
                ).then_inc(aug_in[slot][half], 16)

        def attention(body):
            def place(n, k=0):
                return lambda d=0: ((n + d) % SLOTS, k + (n + d) // SLOTS)

            def run(eng):
                body(-1, place(-1), True, False)
                body(0, place(0), True, False)
                with eng.Fori(0, (NIT - 2) // SLOTS) as k:
                    for j in range(SLOTS):
                        body(k * SLOTS + (1 + j), place(1 + j, k), False, False)
                body(NIT - 1, place(NIT - 1), False, True)
            return run

        def attention_loads(body):
            def run(eng):
                body(-1, 2, False)
                with eng.Fori(0, (NIT - 2) // SLOTS) as k:
                    for j in range(SLOTS):
                        body(k * SLOTS + j, j, True)
                for n in (NIT - 2, NIT - 1):
                    body(n, n % SLOTS, False)
            return run

        def chunks(body):
            def run(eng):
                body(0, True, False)
                with eng.Fori(1, NC - 1) as c:
                    body(c, False, False)
                body(NC - 1, False, True)
            return run

        @block.sync
        def _(sp):
            def load_x(c):
                sp.dma_start(X[:, c * TPC:(c + 1) * TPC, :],
                             x[c * CH:(c + 1) * CH, :].rearrange("(t p) h -> p t h", p=P)).then_inc(x_in[c], 16)

            load_x(0)
            sp.dma_start(cS[:, :, :], cT).then_inc(c_in, 16)
            sp.dma_start(Wm[:, :, 0:2 * H], wmod[:, :, 0:2 * H]).then_inc(mod_in, 16)
            sp.dma_start(Wqk, wqk).then_inc(qk_in, 16)
            sp.dma_start(Bqk[:, :], bqk).then_inc(qk_in, 16)
            load_x(1)
            sp.dma_start(Wv, wv).then_inc(v_in, 16)
            sp.dma_start(Bv[:, :], bv.rearrange("(a n) -> a n", a=1).broadcast_to([P, H])).then_inc(v_in, 16)
            for c in range(2, NC):
                load_x(c)
            sp.dma_start(Wm[:, :, 2 * H:6 * H], wmod[:, :, 2 * H:6 * H]).then_inc(w_in, 16)
            sp.dma_start(Wo[:, :, :], wout).then_inc(w_in, 16)
            sp.dma_start(Bo[:, :], bout.rearrange("(a n) -> a n", a=1).broadcast_to([P, H])).then_inc(w_in, 16)

            def write_parts(c):
                for i in range(4):
                    write_tile(c, i)

            def write_tile(c, i):
                b, half, m = c // (S // CH), c % (S // CH), M_ORDER[i]
                sp.wait_ge(parts_done[b], 4 * half + i + 1)
                rows = qkd[m // KH, b, (m % KH) * P:(m % KH + 1) * P, :, half * CH:(half + 1) * CH]
                for first, count, part in PART_RUNS[m // KH]:
                    src = PT[c % 2][:, part:part + 1, m, :].broadcast_to([P, count, CH]) if m // KH else (
                        PT[c % 2][:, part:part + count, m, :])
                    sp.dma_start(rows[:, first:first + count, :], src).then_inc(parts_out[c % 2], 16)

            def stage(n, slot):
                q, k = (qkd[t].rearrange("b (g j d) i s -> (b g) (d i) j s", g=NG, j=HG)[bass.ds(n, 1)].rearrange(
                    "a d j s -> (a d) j s") for t in range(2))
                for half in range(S // CH):
                    sp.dma_start(Qs[slot][0:NPR, half, :, :], q[:, :, half * CH:(half + 1) * CH]).then_inc(staged[slot], 16)
                sp.dma_start(Ks[slot][0:NPR, :, :], k).then_inc(staged[slot], 16)

            def stage_values(n, slot):
                sp.dma_start(Vst[slot][:, :, :],
                             Vall[:, bass.ds(n, 1), :, :, :].rearrange("p a k j d -> p (a k) (j d)")).then_inc(staged_v[slot], 16)

            def body(n, slot, stages):
                if isinstance(n, int) and n == -1:
                    write_parts(0)
                    write_tile(1, 0)
                    write_tile(1, 1)
                    sp.wait_ge(parts_out[0], 16 * 12)
                    sp.wait_ge(parts_out[1], 16 * 6)
                    stage(0, 0)
                    write_tile(1, 2)
                    write_tile(1, 3)
                    stage(1, 1)
                    sp.wait_ge(v_read, 2 * (S // CH))
                    sp.wait_ge(const_done, N_CONST)
                    for s in range(SLOTS - 1):
                        stage_values(s, s)
                    write_parts(2)
                    write_parts(3)
                    for i in range(2):
                        sp.wait_ge(parts_out[i], 16 * 12 * B)
                    sp.wait_ge(v_read, 2 * NC)
                    sp.dma_start(Wg[:, :, :], wgate).then_inc(wg_in, 16)
                    return
                sp.wait_ge(t_read, t_event(n, "max1") + 1)
                aug(sp, slot, 1)
                if stages:
                    sp.wait_ge(e_ps, n * HEADS + 1)
                    sp.wait_ge(pv_done, n * NS + 1)
                    stage(n + (SLOTS - 1), (slot + SLOTS - 1) % SLOTS)
                    stage_values(n + (SLOTS - 1), (slot + SLOTS - 1) % SLOTS)
                if not (isinstance(n, int) and n == NIT - 1):
                    sp.wait_ge(t_read, t_event(n, "max0") + 1)
                    aug(sp, (slot + 1) % SLOTS, 0)

            attention_loads(body)(sp)

            sp.wait_ge(staged_v[LAST_SLOT], 16 * (1 + (NIT - 1) // SLOTS))

            def ffn(c):
                for f in range(NFT):
                    r = f % WRING
                    if not (isinstance(c, int) and c == 0 and f < WRING):
                        sp.wait_ge(w_hi, c * NFT + (f - WRING + 1))
                        sp.wait_ge(w_lo, c * NFT + (f - WRING + 1))
                    sp.dma_start(Wr[r][:, :], wffn[f]).then_inc(w_raw[r], 16)
                    if f == NSH + CW_LAG - 1:
                        sp.wait_ge(cwT_ready, c + 1)
                        sp.dma_start(cwd[:, bass.ds(c * CH, CH)], cwT[:, :]).then_inc(cw_out, 16)
                    if f == NSH + CW_LAG:
                        sp.wait_ge(cw_out, c * 16 + 16)
                    if f >= CW_LAG:
                        spread(c, f - CW_LAG)
                    elif not (isinstance(c, int) and c == 0):
                        spread(c - 1, f - CW_LAG + NFT)
                    if f == 12 and not (isinstance(c, int) and c == 0):
                        store(c - 1)

            def spread(c, f):
                i = f - NSH
                if i < 0:
                    return
                if not (isinstance(c, int) and c == 0 and i < CWRING):
                    sp.wait_ge(cwb_read, c * NRT + (i - CWRING + 1))
                for e, lo, hi in CW_RUNS[i]:
                    sp.dma_start(cwb[i % CWRING][lo:hi, :],
                                 cwd[e:e + 1, bass.ds(c * CH, CH)].broadcast_to([hi - lo, CH])).then_inc(cw_in[i % CWRING], 16)

            def store(c):
                sp.wait_ge(fin_done, c * 2 + 2)
                sp.dma_start(out[bass.ds(c * CH, CH), :].rearrange("(t p) h -> p t h", p=P),
                             X[:, bass.ds(c * TPC, TPC), :]).then_inc(out_done, 16)

            ffn(0)
            with sp.Fori(1, NC) as c:
                ffn(c)
            for f in range(NFT - CW_LAG, NFT):
                spread(NC - 1, f)
            for half in range(2):
                t = (NC - 1) * TPC + 2 * half
                sp.wait_ge(fin_done, (NC - 1) * 2 + half + 1)
                sp.dma_start(out[t * P:(t + 2) * P, :].rearrange("(t p) h -> p t h", p=P),
                             X[:, t:t + 2, :]).then_inc(out_done, 16)
            sp.wait_ge(out_done, 16 * (NC + 1))

        @block.gpsimd
        def _(pool):
            nc.gpsimd.memset(ident[:, :], 0.0).then_inc(ident_done, 1)
            pool.wait_ge(ident_done, 1)
            nc.gpsimd.affine_select(out=ident[:, :], in_=ident[:, :], compare_op=ALU.not_equal, fill=1.0,
                                    base=0, pattern=[[-1, P]], channel_multiplier=1).then_inc(ident_done, 1)
            nc.gpsimd.memset(mask[:, :], 0.0).then_inc(const_done, 1)
            nc.gpsimd.memset(Vall[:, :, :, :, HD:HD + 1], 1.0).then_inc(const_done, 1)
            nc.gpsimd.memset(Vall[:, :, :, :, HD + 1:32], 0.0).then_inc(const_done, 1)
            pool.wait_ge(ident_done, 2)
            nc.gpsimd.tensor_copy(identb[:, :], ident[:, :]).then_inc(const_done, 1)
            pool.wait_ge(const_done, 4)
            nc.gpsimd.affine_select(out=mask[:, :], in_=mask[:, :], compare_op=ALU.is_ge, fill=NEG,
                                    base=0, pattern=[[-1, P]], channel_multiplier=1).then_inc(const_done, 1)
            pool.wait_ge(const_done, 5)
            pool.wait_ge(wsplit_hi, 1)
            nc.gpsimd.tensor_tensor(Wqkl[:, :, :], Wqk, Wqkh[:, :, :].bitcast(F32), ALU.subtract).then_inc(wsplit_lo, 1)
            pool.wait_ge(wsplit_hi, 2)
            nc.gpsimd.tensor_tensor(Wvl[:, :, :], Wv, Wvh[:, :, :].bitcast(F32), ALU.subtract).then_inc(wsplit_lo, 1)
            low_part(pool, nc.gpsimd, 1)
            pool.wait_ge(hT_low, 2 * KH)
            for i in range(SLOTS):
                if i == SLOTS - 1:
                    pool.wait_ge(const_done, N_CONST - 1)
                    low_part(pool, nc.gpsimd, 2)
                    pool.wait_ge(hT_low, 3 * KH)
                nc.gpsimd.memset(Ks[i][NPR:P, :, :], 1.0).then_inc(const_done, 1)
            pool.wait_ge(const_done, N_CONST)
            pool.wait_ge(parts_done[0], 4 * (S // CH))
            tiles = 4 * (NC - S // CH)
            for k in range(tiles + 1):
                if k < tiles:
                    c, i, m = S // CH + k // 4, k % 4, M_ORDER[k % 4]
                    pool.wait_ge(qk_read, 2 * (4 * c + i) + 2)
                    if k >= 2:
                        pool.wait_ge(parts_done[1], k - 1)
                    nc.gpsimd.tensor_tensor(Rq[k % 2][:, :], Fq[m], PT[c % 2][:, 0, m, :],
                                            ALU.subtract).then_inc(rest_done, 1)
                if k:
                    c, m = S // CH + (k - 1) // 4, M_ORDER[(k - 1) % 4]
                    pool.wait_ge(round_done, k)
                    nc.gpsimd.tensor_tensor(PT[c % 2][:, 2, m, :], Rq[(k - 1) % 2][:, :], PT[c % 2][:, 1, m, :],
                                            ALU.subtract).then_inc(parts_done[1], 1)
            def setup():
                pool.wait_ge(gate_step, 8)
                pool.wait_ge(w_in, 16 * W_DMAS)
                for b in range(B):
                    nc.gpsimd.tensor_tensor(gbias[:, b, :], gate[:, b, :], Bo[:, :], ALU.mult).then_inc(xb_ready, 1)
                pool.wait_ge(v_read, 2 * NC)
                pool.wait_ge(parts_done[B - 1], 4 * (S // CH))
                for b in range(B):
                    for k in range(KH):
                        nc.gpsimd.tensor_tensor(Wog[:, b, k, :], Wo[:, k, :], gate[:, b, :], ALU.mult).then_inc(wog_done, 1)

                nc.gpsimd.memset(lower[:, :, :], 0.0).then_inc(fconst, 1)
                nc.gpsimd.memset(lowg[:, :, :], 0.0).then_inc(fconst, 1)
                pool.wait_ge(fconst, 2)
                nc.gpsimd.affine_select(out=lower[:, :, :], in_=lower[:, :, :], compare_op=ALU.is_ge, fill=1.0,
                                        base=0, pattern=[[-1, NE], [1, NE]], channel_multiplier=0).then_inc(fconst, 1)
                nc.gpsimd.affine_select(out=lowg[:, :, :], in_=lowg[:, :, :], compare_op=ALU.is_ge, fill=1.0,
                                        base=0, pattern=[[-1, NGR], [1, NGR]], channel_multiplier=0).then_inc(fconst, 1)

            def body(n, at, first, last):
                if isinstance(n, int) and n == -1:
                    return
                for s in range(NS):
                    if on_diagonal(s):
                        for pair in range(HG // 2):
                            k = masked_before(s) + pair
                            pool.wait_ge(exp_done, n * (EXP * HEADS) + EXP * (HG * s + 2 * pair + 2))
                            nc.gpsimd.tensor_tensor(tick[:, k:k + 1], ident[:, 0:1], ident[:, 0:1], ALU.mult)
                            v = Pr[(2 * s + pair) % 4][:, :, 0:P]
                            nc.gpsimd.affine_select(out=v, in_=v, compare_op=ALU.is_ge, fill=0.0, base=0,
                                                    pattern=[[0, 2], [1, P]], channel_multiplier=-1).then_inc(masked, 1)
                    if first and s == TPC:
                        pool.wait_ge(masked, masked_before(TPC))
                        setup()
                        pool.wait_ge(fconst, 4)
            attention(body)(pool)
            pool.wait_ge(masked, NIT * NMASK)

            def ffn(c):
                for f in range(NFT):
                    r = f % WRING
                    pool.wait_ge(w_hi, c * NFT + (f + 1))
                    if not (isinstance(c, int) and c == 0 and f < WRING):
                        pool.wait_ge(down_done, c * NFT + (f - WRING + 1))
                    nc.gpsimd.tensor_tensor(Wl[r][:, :], Wr[r][:, :], Wh[r][:, :].bitcast(F32), ALU.subtract).then_inc(w_lo, 1)

            pool.wait_ge(e_ps, (NIT - 1) * HEADS)
            pool.wait_ge(pv_done, (NIT - 1) * NS)
            ffn(0)
            with pool.Fori(1, NC) as c:
                ffn(c)

        @block.scalar
        def _(act):
            act.wait_ge(c_in, 16)
            nc.scalar.activation(cE[:, 0], cS[:, :, :], ACT.Exp, scale=-1.0).then_inc(negc_exp, 1)

            def root_first(c):
                act.wait_ge(ln_step, LN2_STEPS * (c + 1))
                cols = slice(c * TPC, (c + 1) * TPC)
                nc.scalar.activation(rstd[:, cols], rvar[:, cols], ACT.Sqrt).then_inc(rstd_done, 1)

            root_first(0)
            act.wait_ge(qk_in, 32)
            nc.scalar.activation(Wqkh[:, :, :], Wqk, ACT.Copy).then_inc(wsplit_hi, 1)
            root_first(1)
            act.wait_ge(v_in, 32)
            nc.scalar.activation(Wvh[:, :, :], Wv, ACT.Copy).then_inc(wsplit_hi, 1)

            def hT_evict(c):
                b = c // (S // CH)
                for k in range(KH):
                    n = KH * c + k
                    act.wait_ge(xnT_ps, n + 1)
                    if n == 0:
                        act.wait_ge(mod_read, 2)
                    if c:
                        act.wait_ge(hT_low, n - KH + 1)
                    nc.scalar.activation(OT[k][:, :], allb[k], ACT.Identity,
                                         scale=modT[:, 2 + k, b:b + 1], bias=modT[:, k, b:b + 1]).then_inc(hT_ready, 1)
                    if c >= 2:
                        act.wait_ge(v_ps, 2 * (c - 1))
                    nc.scalar.activation(hh[c % 2][:, k, :], allb[k], ACT.Identity,
                                         scale=modT[:, 2 + k, b:b + 1], bias=modT[:, k, b:b + 1]).then_inc(hT_ready, 1)
            def round_tile(c, i):
                act.wait_ge(rest_done, 4 * (c % (S // CH)) + i + 1)
                nc.scalar.activation(PT[c % 2][:, 1, M_ORDER[i], :], Rq[i % 2][:, :], ACT.Copy).then_inc(round_done, 1)

            hT_evict(0)
            for c in range(NC):
                if c + 2 < NC:
                    root_first(c + 2)
                for i, m in enumerate(M_ORDER):
                    n = 4 * c + i
                    bank = allb[QK_RING + n % QK_RING]
                    act.wait_ge(qk_ps, n + 1)
                    if n >= 4:
                        before = (n - 4) // (4 * (S // CH))
                        act.wait_ge(parts_done[before], n - 3 - before * 4 * (S // CH))
                    nc.scalar.activation(Fq[m], bank, ACT.Identity, bias=Bqk[:, m:m + 1]).then_inc(qk_read, 1)
                    if c >= 2:
                        act.wait_ge(parts_out[c % 2], 16 * 12)
                    nc.scalar.activation(PT[c % 2][:, 0, m, :], bank, ACT.Identity,
                                         bias=Bqk[:, m:m + 1]).then_inc(qk_read, 1)
                    if n > 4 * (S // CH):
                        round_tile((n - 1) // 4, (n - 1) % 4)
                    if i == 1 and c + 1 < NC:
                        hT_evict(c + 1)
            def evict(o, qc):
                act.wait_ge(pv_done, (o - qc) * (NS // 2) + (TPC if qc == 0 else NS))
                if not (isinstance(o, int) and o < 2):
                    act.wait_ge(oT_ps, o - 1)
                nc.scalar.activation(OT[qc][:, :], pvb, ACT.Copy).then_inc(ot_ready, 1)

            def split_weights(c, f):
                r = f % WRING
                act.wait_ge(w_raw[r], c * (16 * (NFT // WRING)) + 16 * (f // WRING + 1))
                if not (isinstance(c, int) and c == 0 and f < WRING):
                    act.wait_ge(down_done, c * NFT + (f - WRING + 1))
                nc.scalar.activation(Wh[r][:, :], Wr[r][:, :], ACT.Copy).then_inc(w_hi, 1)

            def copy_out(c, k):
                act.wait_ge(aT_ps, KH * c + k + 1)
                if c:
                    act.wait_ge(y_ps, 2 * c)
                nc.scalar.activation(AT[:, k, :], allb[LATE_BANK(c, k)], ACT.Copy).then_inc(aT_ready, 1)

            def root(q):
                act.wait_ge(ln2_step, q * LN2_STEPS + LN2_STEPS)
                nc.scalar.activation(rstd2[:, :], rvar2[:, :], ACT.Sqrt).then_inc(rstd2_done, 1)

            def shift(q, k, bank):
                act.wait_ge(x2T_ps, q * KH + (k + 1))
                if isinstance(q, int) and q == 0:
                    act.wait_ge(modC_done, 4)
                else:
                    act.wait_ge(h2_split, q * KH)
                    act.wait_ge(logit_ps, q)
                nc.scalar.activation(hv[:, k, :], bank, ACT.Identity, scale=modC[:, 2 + k, bass.ds(q, 1)],
                                     bias=modC[:, k, bass.ds(q, 1)]).then_inc(h2_ready, 1)

            def exponential(q):
                act.wait_ge(route_step, q * ROUTE_STEPS + 2)
                nc.scalar.activation(rt["exp"][:, :, :], rt["logit"][:, :, :], ACT.Exp).then_inc(rexp_done, 1)

            def late(s):
                for c, at in enumerate(LATE_TURN):
                    if s == at:
                        for k in range(KH):
                            copy_out(c, k)
                if s == LATE_ROOT:
                    root(0)
                if s == LATE_TURN2:
                    for k in range(KH):
                        shift(0, k, allb[k])
                if s == LATE_TURN2 + 1:
                    exponential(0)
                if s >= NS - AHEAD:
                    if s == NS - AHEAD:
                        act.wait_ge(staged_v[LAST_SLOT], 16 * (1 + (NIT - 1) // SLOTS))
                    split_weights(0, s - (NS - AHEAD))

            def body(n, at, first, last):
                if isinstance(n, int) and n == -1:
                    round_tile(NC - 1, 3)
                    act.wait_ge(t_read, 1)
                    aug(act, 0, 0)
                    act.wait_ge(parts_done[B - 1], 4 * (S // CH))
                    return
                for s in range(NS):
                    qc, kt = STEPS[s]
                    w = CH - (max(0, kt - TPC * qc)) * P
                    for j in range(HG):
                        p = HG * s + j
                        act.wait_ge(e_ps, n * HEADS + (p + 1))
                        if j == 0 and not (first and s < 2):
                            act.wait_ge(pv_done, n * NS + (s - 1))
                        nc.scalar.activation(Pr[(2 * s + j // 2) % 4][:, j % 2, 0:w], ebank[p % RING][:, 0:w],
                                             ACT.Exp, scale=SCALE).then_inc(exp_done, EXP)
                    if s == 0 and not first:
                        evict(n * 2 - 1, 1)
                    if s == TPC:
                        evict(n * 2, 0)
                    if last:
                        late(s)
            attention(body)(act)
            evict(2 * NIT - 1, 1)

            def scale_out(c):
                act.wait_ge(down_done, c * NFT + NFT)
                if not (isinstance(c, int) and c == 0):
                    act.wait_ge(yT_ps, c * 2)
                for k in range(KH):
                    nc.scalar.activation(Ys[:, k, :], allb[5 + k], ACT.Copy,
                                         scale=modC[:, 4 + k, bass.ds(c, 1)]).then_inc(y_read, 1)

            def ffn(c, first, last):
                later = []
                for f in range(NFT):
                    act.wait_ge(g_ps, c * NFT + (f + 1))
                    if not (isinstance(c, int) and c == 0 and f < 2):
                        act.wait_ge(u_read, c * NFT + (f if f == 0 else f - 1))
                    nc.scalar.activation(sg[f % 2][:, :], allb[2 * (f % 2)], ACT.Silu).then_inc(silu_done, 1)
                    if f == 0 and not (isinstance(c, int) and c == 0):
                        scale_out(c - 1)
                    if f + AHEAD < NFT or not last:
                        split_weights(c, f + AHEAD)
                    if first and f in PROJECT:
                        for what, cc, i in PROJECT[f]:
                            if what == "turn":
                                later.append((f + 1, cc, i))
                    if first:
                        for _, cc, i in [e for e in later if e[0] == f]:
                            copy_out(cc, i)
                    if not last:
                        if f == ROOT_AT:
                            root(c + 1)
                        if f - 1 in TURN2_AT:
                            shift(c + 1, TURN2_AT.index(f - 1), allb[7])
                        if f == EXP_AT:
                            exponential(c + 1)

            chunks(ffn)(act)
            scale_out(NC - 1)

        @block.vector
        def _(dve):
            def first_statistics(c):
                k = c * LN2_STEPS
                tiles = range(c * TPC, (c + 1) * TPC)
                cols = slice(c * TPC, (c + 1) * TPC)
                dve.wait_ge(x_in[c], 16)
                for t in tiles:
                    nc.vector.bn_stats(stats[:, t, :], X[:, t, :]).then_inc(ln_step, 1)
                for i, t in enumerate(tiles):
                    dve.wait_ge(ln_step, k + i + 1)
                    nc.vector.bn_aggr(mv[:, t, :], stats[:, t, :]).then_inc(ln_step, 1)
                dve.wait_ge(ln_step, k + 2 * TPC)
                nc.vector.tensor_scalar(vare[:, cols], mv[:, cols, 1], EPS, None, ALU.add).then_inc(ln_step, 1)
                dve.wait_ge(ln_step, k + 2 * TPC + 1)
                nc.vector.reciprocal(rvar[:, cols], vare[:, cols]).then_inc(ln_step, 1)

            first_statistics(0)

            def normalise_tokens(c, dst):
                for t in range(c * TPC, (c + 1) * TPC):
                    nc.vector.tensor_scalar(dst[:, t - c * TPC, :], X[:, t, :], mv[:, t, 0:1], rstd[:, t:t + 1],
                                            ALU.subtract, ALU.mult).then_inc(xn_ready, 1)

            dve.wait_ge(negc_exp, 1)
            nc.vector.tensor_scalar(cE[:, 1], cE[:, 0], 1.0, None, ALU.add).then_inc(silu_c, 1)
            dve.wait_ge(silu_c, 1)
            nc.vector.reciprocal(cE[:, 2], cE[:, 1]).then_inc(silu_c, 1)
            dve.wait_ge(silu_c, 2)
            nc.vector.tensor_tensor(cS[:, :, :], cS[:, :, :], cE[:, 2], ALU.mult).then_inc(silu_c, 1)
            dve.wait_ge(rstd_done, 1)
            normalise_tokens(0, xn[0])
            first_statistics(1)

            def read_mod(n, bank):
                nc.vector.tensor_copy(modT[:, 4 * n:4 * n + 2, :],
                                      bank[:, 8 * n:8 * n + 4].rearrange("p (m b) -> p m b", b=B)).then_inc(mod_read, 1)
                nc.vector.tensor_scalar(modT[:, 4 * n + 2:4 * n + 4, :],
                                        bank[:, 8 * n + 4:8 * n + 8].rearrange("p (m b) -> p m b", b=B),
                                        1.0, None, ALU.add).then_inc(mod_read, 1)

            def row_maximum(n, u):
                i, diag, _, w = ROWS[u // HG]
                j = u % HG
                dve.wait_ge(m_ps, n * UNITS + (u + 1))
                dst = mxA[:, i, j:j + 1] if diag else mxB[:, i - TPC, j:j + 1]
                nc.vector.tensor_reduce(dst, mbank[u % RING][:, 0:w], AX.X, ALU.max).then_inc(m_red, 1)

            dve.wait_ge(mod_ps, 1)
            read_mod(0, allb[7])
            dve.wait_ge(silu_c, 3)
            nc.vector.tensor_copy(cB, cS[:, :, :].unsqueeze(3).broadcast_to([P, KH, B, P])).then_inc(silu_c, 1)

            def normalise_chunk(c):
                if c >= 2:
                    dve.wait_ge(xnT_ps, KH * (c - 1))
                dve.wait_ge(rstd_done, c + 1)
                normalise_tokens(c, xn[c % 2])

            low_part(dve, nc.vector, 0)

            def split_tile(c, i):
                m, k = M_ORDER[i], 4 * c + i
                dve.wait_ge(qk_read, 2 * k + 2)
                if k >= 2:
                    dve.wait_ge(parts_done[0], k - 1)
                nc.vector.tensor_tensor(Rq[i % 2][:, :], Fq[m], PT[c % 2][:, 0, m, :], ALU.subtract).then_inc(split_step, 1)
                dve.wait_ge(split_step, 2 * k + 1)
                nc.vector.tensor_copy(PT[c % 2][:, 1, m, :], Rq[i % 2][:, :]).then_inc(split_step, 1)
                dve.wait_ge(split_step, 2 * k + 2)
                nc.vector.tensor_tensor(PT[c % 2][:, 2, m, :], Rq[i % 2][:, :], PT[c % 2][:, 1, m, :],
                                        ALU.subtract).then_inc(parts_done[0], 1)

            def gates():
                dve.wait_ge(mod_ps, 2)
                read_mod(1, allb[2])
                nc.vector.tensor_copy(modT[:, 8:10, :], allb[2][:, 16:20].rearrange("p (m b) -> p m b", b=B)).then_inc(mod_read, 1)
                dve.wait_ge(gate_ps, 1)
                dve.wait_ge(mod_read, 5)
                ps = allb[0].rearrange("p (b h) -> p b h", b=B)
                for g, sgn, neg in ((ps, gsgn, gneg), (modT[:, 8:10, :], gbS[:, :, :], gbN[:, :, :])):
                    nc.vector.tensor_scalar(sgn, g, 0.0, 2.0, ALU.is_ge, ALU.mult).then_inc(gate_step, 1)
                    nc.vector.tensor_scalar(neg, g, -1.0, 0.25, ALU.mult, ALU.max).then_inc(gate_step, 1)
                dve.wait_ge(gate_step, 4)
                nc.vector.tensor_tensor(gabs, ps, gneg, ALU.max).then_inc(gate_step, 1)
                nc.vector.tensor_tensor(gbA[:, :, :], modT[:, 8:10, :], gbN[:, :, :], ALU.max).then_inc(gate_step, 1)
                dve.wait_ge(gate_step, 6)
                for dst, sgn, mag in ((gate[:, :, :], gsgn, gabs), (modT[:, 8:10, :], gbS[:, :, :], gbA[:, :, :])):
                    nc.vector.scalar_tensor_tensor(out=dst, in0=sgn, scalar=-1.0, in1=mag,
                                                   op0=ALU.add, op1=ALU.mult).then_inc(gate_step, 1)
                dve.wait_ge(gate_step, 8)
                for c in range(NC):
                    nc.vector.tensor_copy(modC[:, :, c], modT[:, 4:10, c // (S // CH)]).then_inc(modC_done, 1)

            for c in range(NC):
                if c == 0:
                    normalise_chunk(1)
                if c + 2 < NC:
                    first_statistics(c + 2)
                if c == 1:
                    gates()
                if c < S // CH:
                    for i in range(4):
                        split_tile(c, i)
                        if i == 1:
                            normalise_chunk(c + 2)
                if c + 1 == NC - 1:
                    low_part(dve, nc.vector, c + 1)
                for v in range(2):
                    if c == NC - 1:
                        for u in (range(OVER - 2 * PER) if v == 0 else range(OVER - 2 * PER, OVER)):
                            row_maximum(0, u)
                    dve.wait_ge(v_ps, 2 * c + v + 1)
                    if c == 0 and v == 0:
                        dve.wait_ge(v_in, 32)
                    b, kt = c // (S // CH), (c % (S // CH)) * TPC + 2 * v
                    for u in range(2):
                        ins = nc.vector.tensor_tensor(
                            Vall[:, b * NG:(b + 1) * NG, kt + u, :, 0:HD],
                            allb[6 + v][:, u * H:(u + 1) * H].rearrange("p (g j d) -> p g j d", g=NG, j=HG),
                            Bv[:, :].rearrange("p (g j d) -> p g j d", g=NG, j=HG), ALU.add)
                    ins.then_inc(v_read, 1)
            def max_parts(n, half):
                k = n * 9 + 4 * half
                src = mxA[:, half * TPC:(half + 1) * TPC, :]
                if half:
                    dve.wait_ge(m_red, n * UNITS + UNITS)
                    nc.vector.tensor_tensor(src, src, mxB[:, :, :], ALU.max).then_inc(mp_step, 1)
                    dve.wait_ge(mp_step, k + 1)
                    k = k + 1
                else:
                    dve.wait_ge(m_red, n * UNITS + TPC * HG)
                v = src.rearrange("p i j -> p j i")
                if not (isinstance(n, int) and n == 0 and half == 0):
                    dve.wait_ge(mp_step, k)
                nc.vector.tensor_scalar(MP[:, 0], v, -1.0, None, ALU.mult).then_inc(mp_step, 1)
                dve.wait_ge(mp_step, k + 1)
                nc.vector.scalar_tensor_tensor(out=mr[:, :, :], in0=v, scalar=-1.0, in1=MP[:, 0],
                                               op0=ALU.mult, op1=ALU.subtract).then_inc(mp_step, 1)
                dve.wait_ge(mp_step, k + 2)
                nc.vector.tensor_copy(MP[:, 1], mr[:, :, :]).then_inc(mp_step, 1)
                dve.wait_ge(mp_step, k + 3)
                nc.vector.tensor_tensor(MP[:, 2], mr[:, :, :], MP[:, 1], ALU.subtract).then_inc(mp_step, 1)

            def max_copy(n, half, before):
                dve.wait_ge(mpT_ps, n * 2 + (half + 1))
                if before is not None:
                    dve.wait_ge(aug_in[before[0]][half], before[1] * 48 + 48)
                nc.vector.tensor_copy(MT[half][:, :], tb.bitcast(BF16)[0:3 * HG * TPC, 0:P]).then_inc(
                    t_read, 2 if before is None else 1)

            def normalise(o, n, qc):
                ps = tb.rearrange("p (t j d) -> p t j d", t=TPC, j=HG)
                dve.wait_ge(oT_ps, o + 1)
                nc.vector.reciprocal(R[:, :, :], ps[:, :, :, HD]).then_inc(rec_done, 1)
                dve.wait_ge(rec_done, o + 1)
                dst = A[:, qc, :, bass.ds(n, 1), :].rearrange("p t a (j d) -> p (t a) j d", j=HG)
                nc.vector.tensor_tensor(dst, ps[:, :, :, 0:HD],
                                        R[:, :, :].unsqueeze(3).broadcast_to([P, TPC, HG, HD]), ALU.mult).then_inc(t_read, 1)

            def residual(c, i):
                if c == 0 and i == 0:
                    dve.wait_ge(xb_ready, B)
                t = X[:, c * TPC + 2 * i:c * TPC + 2 * i + 2, :]
                nc.vector.tensor_tensor(t, t, gbias[:, c // (S // CH), :].unsqueeze(1).broadcast_to([P, 2, H]),
                                        ALU.add).then_inc(xg_ready, 1)
                dve.wait_ge(xg_ready, 2 * c + i + 1)
                dve.wait_ge(y_ps, 2 * c + i + 1)
                nc.vector.tensor_tensor(t, t, allb[LATE_BANK(c, i)].rearrange("p (t h) -> p t h", h=H),
                                        ALU.add).then_inc(x1_ready, 1)

            def tile_of(q, t):
                return X[:, bass.ds(q * TPC + t, 1), :].rearrange("p a h -> p (a h)")

            def statistics(q):
                if isinstance(q, int):
                    dve.wait_ge(x1_ready, 2 * q + 2)
                else:
                    dve.wait_ge(x1_ready, 2 * NC)
                for t in range(TPC):
                    nc.vector.bn_stats(stats2[:, t, :], tile_of(q, t)).then_inc(ln2_step, 1)

            def averages(q):
                k = q * LN2_STEPS
                if isinstance(q, int) and q == 0:
                    dve.wait_ge(ln2_step, TPC)
                for t in range(TPC):
                    nc.vector.bn_aggr(mv2[:, t, :], stats2[:, t, :]).then_inc(ln2_step, 1)
                dve.wait_ge(ln2_step, k + 2 * TPC)
                nc.vector.tensor_scalar(vare2[:, :], mv2[:, :, 1], EPS, None, ALU.add).then_inc(ln2_step, 1)
                dve.wait_ge(ln2_step, k + (2 * TPC + 1))
                nc.vector.reciprocal(rvar2[:, :], vare2[:, :]).then_inc(ln2_step, 1)

            def second_norm(q):
                dve.wait_ge(rstd2_done, q + 1)
                for t in range(TPC):
                    nc.vector.tensor_scalar(xm[:, t, :], tile_of(q, t), mv2[:, t, 0:1], rstd2[:, t:t + 1],
                                            ALU.subtract, ALU.mult).then_inc(xm_ready, 1)

            def split(q, k):
                dve.wait_ge(h2_ready, q * KH + (k + 1))
                hi, lo = (h[:, bass.ds(q, 1), k, :].rearrange("p a t -> p (a t)") for h in (Hh, Hl))
                nc.vector.tensor_copy(hi, hv[:, k, :]).then_inc(h2_hi, 1)
                dve.wait_ge(h2_hi, q * KH + (k + 1))
                nc.vector.tensor_tensor(lo, hv[:, k, :], hi.bitcast(F32), ALU.subtract).then_inc(h2_split, 1)

            def route(c, lo, hi):
                did = [0]
                r = {k: (v[:, :, :] if len(v.shape) == 3 else v[:, :, :, :] if len(v.shape) == 4 else v[:, :])
                     for k, v in rt.items()}

                def step(op, *args, **kw):
                    if lo <= did[0] < hi:
                        if did[0] == 0:
                            dve.wait_ge(logit_ps, c + 1)
                        if did[0] == 2:
                            dve.wait_ge(rexp_done, c + 1)
                        if did[0] or not (isinstance(c, int) and c == 0):
                            dve.wait_ge(route_step, c * ROUTE_STEPS + did[0])
                        op(*args, **kw).then_inc(route_step, 1)
                    did[0] += 1

                def wide(ap, n):
                    return ap.unsqueeze(3).broadcast_to([P, TPC, ap.shape[2], n])

                def each(ap, n):
                    return ap.unsqueeze(2).broadcast_to([P, TPC, n])

                def other(ap):
                    n = ap.shape[2]
                    return ap.unsqueeze(2).broadcast_to([P, TPC, n, n])

                tt, ts, red = nc.vector.tensor_tensor, nc.vector.tensor_scalar, nc.vector.tensor_reduce
                bank = allb[0] if isinstance(c, int) and c == 0 else allb[7]
                logits = bank[:, 0:TPC * NE].rearrange("p (t e) -> p t e", e=NE)
                step(red, r["max"], logits, AX.X, ALU.max)
                step(tt, r["logit"], logits, each(r["max"], NE), ALU.subtract)
                step(red, r["sum"], r["exp"], AX.X, ALU.add)
                step(nc.vector.reciprocal, r["rec"], r["sum"])
                step(tt, r["score"], r["exp"], each(r["rec"], NE), ALU.mult)
                step(red, r["group"], r["score"].rearrange("p t (g e) -> p t g e", g=NGR), AX.X, ALU.max)
                step(tt, r["ggt"], other(r["group"]), wide(r["group"], NGR), ALU.is_gt)
                step(tt, r["geq"], other(r["group"]), wide(r["group"], NGR), ALU.is_equal)
                step(tt, r["geq"], r["geq"], lowg[:, :, :].unsqueeze(1).broadcast_to([P, TPC, NGR, NGR]), ALU.mult)
                step(tt, r["ggt"], r["ggt"], r["geq"], ALU.add)
                step(red, r["grank"], r["ggt"], AX.X, ALU.add)
                step(ts, r["gsel"], r["grank"], float(TOPG), None, ALU.is_lt)
                by_group = "p t (g e) -> p t g e"
                step(tt, r["kept"].rearrange(by_group, g=NGR), r["score"].rearrange(by_group, g=NGR),
                        wide(r["gsel"], EPG), ALU.mult)
                step(nc.vector.scalar_tensor_tensor, out=r["masked"].rearrange(by_group, g=NGR), in0=wide(r["gsel"], EPG),
                                                    scalar=-1.0, in1=r["kept"].rearrange(by_group, g=NGR),
                                                    op0=ALU.add, op1=ALU.add)
                step(tt, r["gt"], other(r["masked"]), wide(r["masked"], NE), ALU.is_gt)
                step(tt, r["eq"], other(r["masked"]), wide(r["masked"], NE), ALU.is_equal)
                step(tt, r["eq"], r["eq"], lower[:, :, :].unsqueeze(1).broadcast_to([P, TPC, NE, NE]), ALU.mult)
                step(tt, r["gt"], r["gt"], r["eq"], ALU.add)
                step(red, r["rank"], r["gt"], AX.X, ALU.add)
                step(nc.vector.scalar_tensor_tensor, out=r["w"], in0=r["rank"], scalar=float(TOPK), in1=r["score"],
                                                    op0=ALU.is_lt, op1=ALU.mult)
                step(red, r["wsum"], r["w"], AX.X, ALU.add)
                step(ts, r["weps"], r["wsum"], 1e-20, None, ALU.add)
                step(nc.vector.reciprocal, r["wrec"], r["weps"])
                step(tt, r["cw"], r["w"], each(r["wrec"], NE), ALU.mult)
                assert did[0] == ROUTE_STEPS

            def copy_weights(q, bank):
                dve.wait_ge(cwT_ps, q + 1)
                if not (isinstance(q, int) and q == 0):
                    dve.wait_ge(cw_out, q * 16)
                nc.vector.tensor_copy(cwT[:, :], bank[0:NE, 0:CH]).then_inc(cwT_ready, 1)

            def body(n, at, first, last):
                if isinstance(n, int) and n == -1:
                    for u in range(OVER, UNITS):
                        row_maximum(0, u)
                        if u == max(OVER, HG * TPC):
                            max_parts(0, 0)
                        if u == max(OVER, HG * TPC) + HG:
                            max_copy(0, 0, None)
                    return
                if last:
                    return late(n)
                max_parts(n, 1)
                for what, i in ORDER:
                    if what == "unit":
                        row_maximum(n + 1, i)
                    if what == "parts":
                        max_parts(n + 1, 0)
                    if what == "max" and i == 1:
                        max_copy(n, 1, None if first else at(-1))
                    if what == "max" and i == 0:
                        max_copy(n + 1, 0, at(0))
                    if what == "out" and i == 1 and not first:
                        normalise(n * 2 - 1, n - 1, 1)
                    if what == "out" and i == 0:
                        if first:
                            for c in range(2):
                                dve.wait_ge(parts_out[c], 16 * 12 * B)
                        normalise(n * 2, n, 0)

            def late(n):
                max_parts(n, 1)
                max_copy(n, 1, ((n - 1) % SLOTS, (n - 1) // SLOTS))
                for i in range(2):
                    residual(0, i)
                statistics(0)
                averages(0)
                normalise(n * 2 - 1, n - 1, 1)
                second_norm(0)
                dve.wait_ge(e_ps, n * HEADS)
                dve.wait_ge(pv_done, n * NS)
                for k in range(KH):
                    split(0, k)
                dve.wait_ge(fconst, 4)
                route(0, 0, 2)
                route(0, 2, 20)
                normalise(n * 2, n, 0)
                for i in range(2):
                    residual(1, i)
                route(0, 20, ROUTE_STEPS)

            attention(body)(dve)

            def finish(c, half):
                dve.wait_ge(yT_ps, c * 2 + (half + 1))
                t = X[:, bass.ds(c * TPC + 2 * half, 2), :]
                nc.vector.tensor_tensor(t, allb[BACK[half]].rearrange("p (t h) -> p t h", h=H), t, ALU.add).then_inc(fin_done, 1)

            def ffn(c, start, last):
                for f in range(NFT):
                    free = f if f == 0 else f - 1
                    if f == AGGR_AT and not last:
                        dve.wait_ge(ln2_step, c * LN2_STEPS + (LN2_STEPS + TPC))
                    dve.wait_ge(u_ps, c * NFT + (f + 1))
                    dve.wait_ge(silu_done, c * NFT + (f + 1))
                    if not (start and f < 2):
                        dve.wait_ge(a_ready, c * NFT + free)
                    nc.vector.tensor_tensor(su[f % 2][:, :], allb[2 * (f % 2) + 1], sg[f % 2][:, :], ALU.mult).then_inc(u_read, 1)
                    dve.wait_ge(u_read, c * NFT + (f + 1))
                    src = su[f % 2]
                    if f >= NSH:
                        i = f - NSH
                        dve.wait_ge(cw_in[i % CWRING], c * cw_count(NRT - CWRING + i % CWRING) + cw_count(i))
                        nc.vector.tensor_tensor(sw[f % 2][:, :], cwb[i % CWRING][:, :], su[f % 2][:, :],
                                                ALU.mult).then_inc(cwb_read, 1)
                        dve.wait_ge(cwb_read, c * NRT + (f - NSH + 1))
                        src = sw[f % 2]
                    if not (start and f < 2):
                        dve.wait_ge(down_done, c * NFT + free)
                    nc.vector.tensor_copy(ah[f % 2][:, :], src[:, :]).then_inc(hi_done, 1)
                    dve.wait_ge(hi_done, c * NFT + (f + 1))
                    nc.vector.tensor_tensor(al[f % 2][:, :], src[:, :], ah[f % 2][:, :].bitcast(F32),
                                            ALU.subtract).then_inc(a_ready, 1)
                    if f in (3, 5) and not start:
                        finish(c - 1, (f - 3) // 2)
                    if start and f == 0:
                        normalise(2 * NIT - 1, NIT - 1, 1)
                    if start and f == NSH - 1:
                        copy_weights(0, allb[7])
                    if start and f - 1 in PROJECT:
                        for what, cc, i in PROJECT[f - 1]:
                            if what == "project":
                                residual(cc, i)
                    if last:
                        continue
                    if f == STATS_AT:
                        statistics(c + 1)
                    if f == AGGR_AT:
                        averages(c + 1)
                    if f == NORM_AT:
                        second_norm(c + 1)
                    if f - 2 in TURN2_AT:
                        split(c + 1, TURN2_AT.index(f - 2))
                    if f == SOFTMAX_AT:
                        route(c + 1, 0, 2)
                    if ROUTE_AT <= f < TURNW_AT:
                        route(c + 1, ROUTE_CUTS[f - ROUTE_AT], ROUTE_CUTS[f - ROUTE_AT + 1])
                    if f == TURNW_AT:
                        copy_weights(c + 1, allb[7])

            chunks(ffn)(dve)
            finish(NC - 1, 0)
            finish(NC - 1, 1)

        @block.tensor
        def _(pe):
            def modulation(ms, n0, bank):
                for n, m in enumerate(ms):
                    for k in range(KH):
                        ins = nc.tensor.matmul(bank[:, (n0 + n) * B:(n0 + n + 1) * B], Wm[:, k, m * P:(m + 1) * P],
                                               cS[:, k, :], start=(k == 0), stop=(k == KH - 1))
                ins.then_inc(mod_ps, 1)

            def gate_rows():
                for b in range(B):
                    for k in range(KH):
                        ins = nc.tensor.matmul(allb[0][:, b * H:(b + 1) * H], cB[:, k, b, :],
                                               Wm[:, k, 2 * H:3 * H], start=(k == 0), stop=(k == KH - 1))
                ins.then_inc(gate_ps, 1)

            def turn(c):
                for k in range(KH):
                    n = KH * c + k
                    pe.wait_ge(xn_ready, TPC * (c + 1))
                    if n >= KH:
                        pe.wait_ge(hT_ready, 2 * (n - KH + 1))
                    for t in range(TPC):
                        ins = nc.tensor.transpose(allb[k][:, t * P:(t + 1) * P], xn[c % 2][:, t, k * P:(k + 1) * P], ident[:, :])
                    ins.then_inc(xnT_ps, 1)

            def score_unit(n, slot, u):
                i, diag, k0, w = ROWS[u // HG]
                j = u % HG
                if not (isinstance(n, int) and n == 0 and u < RING):
                    pe.wait_ge(m_red, n * UNITS + (u - RING + 1))
                if diag:
                    nc.tensor.matmul(mbank[u % RING][:, w - P:w], identb[:, :], mask[:, :], start=True, stop=False,
                                     skip_group_check=True)
                nc.tensor.matmul(mbank[u % RING][:, 0:w], Qs[slot][0:NPR, i // TPC, j, (i % TPC) * P:(i % TPC + 1) * P],
                                 Ks[slot][0:NPR, j, k0:k0 + w], start=not diag, stop=True,
                                 skip_group_check=True).then_inc(m_ps, 1)

            pe.wait_ge(ident_done, 2)
            turn(0)
            pe.wait_ge(mod_in, 16)
            pe.wait_ge(silu_c, 3)
            modulation(range(4), 0, allb[7])
            for c in range(NC):
                pe.wait_ge(hT_low, KH * (c + 1))
                if c == 0:
                    pe.wait_ge(wsplit_lo, 1)
                if c == NC - 1:
                    pe.wait_ge(const_done, N_CONST)
                    pe.wait_ge(staged[0], 16 * STAGE_DMAS)
                for i, m in enumerate(M_ORDER):
                    n = 4 * c + i
                    if n >= QK_RING:
                        pe.wait_ge(qk_read, 2 * (n - QK_RING + 1))
                    for k in range(KH):
                        for a, (w, h) in enumerate(((Wqkh, hh), (Wqkh, hl), (Wqkl, hh))):
                            ins = nc.tensor.matmul(allb[QK_RING + n % QK_RING], w[:, k, m * P:(m + 1) * P],
                                                   h[c % 2][:, k, :], start=(k == 0 and a == 0),
                                                   stop=(k == KH - 1 and a == 2))
                        if k == KH - 1:
                            ins.then_inc(qk_ps, 1)
                        if c == NC - 1:
                            for u in range(PER):
                                score_unit(0, 0, PER * (KH * i + k) + u)
                    if i == 1 and c + 1 < NC:
                        if c == 1:
                            pe.wait_ge(gate_step, 6)
                        turn(c + 1)
                if c == 0:
                    pe.wait_ge(wsplit_lo, 2)
                    pe.wait_ge(mod_read, 2)
                for v in range(2):
                    if c:
                        pe.wait_ge(v_read, 2 * (c - 1) + v + 1)
                    for u in range(2):
                        t0 = (2 * v + u) * P
                        for k in range(KH):
                            for a, (h, w) in enumerate(((hh, Wvh), (hl, Wvh), (hh, Wvl))):
                                ins = nc.tensor.matmul(allb[6 + v][:, u * H:(u + 1) * H], h[c % 2][:, k, t0:t0 + P],
                                                       w[:, k, :], start=(k == 0 and a == 0),
                                                       stop=(k == KH - 1 and a == 2))
                        if u == 1:
                            ins.then_inc(v_ps, 1)
                        if c == NC - 1:
                            for w in range(PER):
                                score_unit(0, 0, OVER - PER * (4 - 2 * v - u) + w)
                if c == 0:
                    pe.wait_ge(w_in, 16 * W_DMAS)
                    modulation(range(6, 12), 4, allb[2])
                    pe.wait_ge(silu_c, 4)
                    pe.wait_ge(hT_ready, 2 * (KH + 1))
                    gate_rows()

            def turn_max_waits(n, half, event):
                pe.wait_ge(mp_step, n * 9 + (9 if half else 4))
                if event is not None:
                    pe.wait_ge(t_read, event)

            def turn_max():
                nc.tensor.transpose(tb.bitcast(BF16)[0:3 * HG * TPC, 0:P],
                                    MP[:, :, :, :].rearrange("p a j i -> p (a j i)"), identb[:, :]).then_inc(mpT_ps, 1)

            def turn_out(o, qc, event):
                pe.wait_ge(ot_ready, o + 1)
                pe.wait_ge(t_read, event)
                for t in range(TPC):
                    ins = nc.tensor.transpose(tb[:, t * P:(t + 1) * P], OT[qc][:, t * P:(t + 1) * P], ident[:, :])
                ins.then_inc(oT_ps, 1)

            def products(n, slot, s):
                qc, kt = STEPS[s]
                q0 = max(0, kt - TPC * qc) * P
                w = CH - q0
                if on_diagonal(s):
                    pe.wait_ge(masked, n * NMASK + masked_before(s + 1))
                else:
                    pe.wait_ge(exp_done, n * (EXP * HEADS) + EXP * HG * (s + 1))
                if kt == 0 and not (isinstance(n, int) and n == 0 and qc == 0):
                    pe.wait_ge(ot_ready, n * 2 + qc)
                for j in range(HG):
                    ins = nc.tensor.matmul(pvb[32 * j:32 * j + 32, q0:CH], Vst[slot][:, kt, 32 * j:32 * j + 32],
                                           Pr[(2 * s + j // 2) % 4][:, j % 2, 0:w],
                                           start=(kt == 0), stop=(kt == TPC * (qc + 1) - 1), skip_group_check=True)
                ins.then_inc(pv_done, 1)

            def scores(n, slot, turn, p):
                s, j = p // HG, p % HG
                qc, kt = STEPS[s]
                q0 = max(0, kt - TPC * qc) * P
                if kt == 0 and j == 0:
                    pe.wait_ge(aug_in[slot][qc], turn * 48 + 48)
                if not (isinstance(n, int) and n == 0 and p < RING):
                    pe.wait_ge(exp_done, n * (EXP * HEADS) + EXP * (p - RING + 1))
                nc.tensor.matmul(ebank[p % RING][:, 0:CH - q0], Ks[slot][0:NAUG, j, kt * P:(kt + 1) * P],
                                 Qs[slot][0:NAUG, qc, j, q0:CH], start=True, stop=True).then_inc(e_ps, 1)

            def turn_attention(c, k):
                b, qc = c // (S // CH), c % (S // CH)
                for t in range(TPC):
                    src = A[:, qc, t, b * NG + 2 * k:b * NG + 2 * k + 2, :].rearrange("p g d -> p (g d)")
                    ins = nc.tensor.transpose(allb[LATE_BANK(c, k)][:, t * P:(t + 1) * P], src, ident[:, :])
                ins.then_inc(aT_ps, 1)

            def project(c, i, tiles=(0, 1)):
                pe.wait_ge(aT_ready, KH * (c + 1))
                if c == 0 and i == 0:
                    pe.wait_ge(wog_done, B * KH)
                for u in tiles:
                    t = 2 * i + u
                    for k in range(KH):
                        ins = nc.tensor.matmul(allb[LATE_BANK(c, i)][:, u * H:(u + 1) * H], AT[:, k, t * P:(t + 1) * P],
                                               Wog[:, c // (S // CH), k, :], start=(k == 0), stop=(k == KH - 1))
                if 1 in tiles:
                    ins.then_inc(y_ps, 1)

            def turn2(q, k, bank):
                pe.wait_ge(xm_ready, q * TPC + TPC)
                for t in range(TPC):
                    ins = nc.tensor.transpose(bank[:, t * P:(t + 1) * P], xm[:, t, k * P:(k + 1) * P], ident[:, :])
                ins.then_inc(x2T_ps, 1)

            def logits(q, bank):
                pe.wait_ge(h2_ready, q * KH + KH)
                for t in range(TPC):
                    for k in range(KH):
                        ins = nc.tensor.matmul(bank[:, t * NE:(t + 1) * NE], hv[:, k, t * P:(t + 1) * P],
                                               Wg[:, k, :], start=(k == 0), stop=(k == KH - 1))
                ins.then_inc(logit_ps, 1)

            def turn_weights(q, bank):
                pe.wait_ge(route_step, q * ROUTE_STEPS + ROUTE_STEPS)
                for t in range(TPC):
                    ins = nc.tensor.transpose(bank[0:NE, t * P:(t + 1) * P], rt["cw"][:, t, :], ident[:, :])
                ins.then_inc(cwT_ps, 1)

            def late(p):
                s, j = p // HG, p % HG
                if p == 0:
                    pe.wait_ge(m_red, NIT * UNITS)
                for c, at in enumerate(LATE_TURN):
                    if s == at and j < KH:
                        if c and j == 0:
                            pe.wait_ge(route_step, 2)
                        turn_attention(c, j)
                if p in LATE_PROJECT:
                    piece = LATE_PROJECT.index(p)
                    project(piece // TPC, piece % TPC // 2, (piece % 2,))
                if s == LATE_TURN2 and j < KH:
                    turn2(0, j, allb[j])
                if s == LATE_TURN2 + 1 and j == 0:
                    pe.wait_ge(wg_in, 16)
                    logits(0, allb[0])

            def body(n, at, first, last):
                if isinstance(n, int) and n == -1:
                    for u in range(OVER, UNITS):
                        score_unit(0, 0, u)
                        if u == max(OVER, HG * TPC) + HG:
                            pe.wait_ge(v_read, 2 * NC)
                            turn_max_waits(0, 0, None)
                            turn_max()
                    pe.wait_ge(qk_read, 2 * 4 * NC)
                    return
                (slot, turn), (nxt, nxt_turn) = at(0), at(1)
                pe.wait_ge(staged_v[slot], turn * 16 + 16)
                if not last:
                    pe.wait_ge(staged[nxt], nxt_turn * (16 * STAGE_DMAS) + 16 * STAGE_DMAS)
                for what, i in ORDER:
                    if what == "scores":
                        scores(n, slot, turn, i)
                    if what == "unit" and not last:
                        score_unit(n + 1, nxt, i)
                    if what == "products":
                        if i == 0:
                            turn_max_waits(n, 1, t_event(n, "max1"))
                        if i == 5 and not last:
                            turn_max_waits(n + 1, 0, t_event(n, "max0"))
                        if i >= 0:
                            products(n, slot, i)
                        elif not first:
                            products(n - 1, at(-1)[0], NS - 1)
                    if what == "max" and (i == 1 or not last):
                        turn_max()
                    if what == "out" and i == 1 and not first:
                        turn_out(n * 2 - 1, 1, t_event(n, "out1"))
                    if what == "out" and i == 0:
                        turn_out(n * 2, 0, t_event(n, "out0"))
                    if what == "scores" and last:
                        late(i)
            attention(body)(pe)
            products(NIT - 1, (NIT - 1) % SLOTS, NS - 1)
            pe.wait_ge(exp_done, NIT * EXP * HEADS)
            pe.wait_ge(x1_ready, 2 * (S // CH))
            pe.wait_ge(h2_split, KH)

            def up(c, f):
                r = f % WRING
                pe.wait_ge(w_lo, c * NFT + (f + 1))
                if not (isinstance(c, int) and c == 0 and f < 2):
                    pe.wait_ge(u_read, c * NFT + (f if f == 0 else f - 1))
                for which, done in ((0, g_ps), (1, u_ps)):
                    for k in range(KH):
                        def part(h):
                            return h[:, bass.ds(c, 1), k, :].rearrange("p a t -> p (a t)")
                        w = slice((which * KH + k) * P, (which * KH + k + 1) * P)
                        for n, (wt, ht) in enumerate(((Wh, Hh), (Wh, Hl), (Wl, Hh))):
                            ins = nc.tensor.matmul(allb[2 * (f % 2) + which], wt[r][:, w], part(ht),
                                                   start=(k == 0 and n == 0), stop=(k == KH - 1 and n == 2))
                    ins.then_inc(done, 1)

            def down(c, f):
                r = f % WRING
                pe.wait_ge(a_ready, c * NFT + (f + 1))
                if f == 0:
                    if isinstance(c, int) and c == 0:
                        pe.wait_ge(ot_ready, 2 * NIT)
                    else:
                        pe.wait_ge(y_read, c * 2)
                for m in range(KH):
                    w = slice(2 * KH * P + m * P, 2 * KH * P + (m + 1) * P)
                    for n, (wt, at) in enumerate(((Wh, ah), (Wh, al), (Wl, ah))):
                        ins = nc.tensor.matmul(allb[5 + m], wt[r][:, w], at[f % 2][:, :],
                                               start=(f == 0 and n == 0), stop=(f == NFT - 1 and n == 2))
                ins.then_inc(down_done, 1)

            def turn_back(c, half):
                pe.wait_ge(y_read, c * 2 + 2)
                if half == 0:
                    if not (isinstance(c, int) and c == NC - 1):
                        pe.wait_ge(cwT_ready, c + 2)
                elif not (isinstance(c, int) and c == 0):
                    pe.wait_ge(fin_done, c * 2)
                for t in range(2):
                    for m in range(KH):
                        ins = nc.tensor.transpose(allb[BACK[half]][:, t * H + m * P:t * H + (m + 1) * P],
                                                  Ys[:, m, (2 * half + t) * P:(2 * half + t + 1) * P], ident[:, :])
                ins.then_inc(yT_ps, 1)

            def beside(c, f, start):
                if f == TURN2_AT[0]:
                    if start:
                        pe.wait_ge(cwT_ready, 1)
                    else:
                        pe.wait_ge(fin_done, c * 2)
                    turn2(c + 1, 0, allb[7])
                if f == TURN2_AT[1]:
                    pe.wait_ge(h2_ready, c * KH + (KH + 1))
                    turn2(c + 1, 1, allb[7])
                if f == LOGITS_AT:
                    logits(c + 1, allb[7])
                if f == TURNW_AT:
                    turn_weights(c + 1, allb[7])

            def ffn(c, start, last):
                for f in range(NFT):
                    up(c, f)
                    if f:
                        down(c, f - 1)
                    elif not start:
                        down(c - 1, NFT - 1)
                    if f in (2, 4) and not start:
                        turn_back(c - 1, (f - 2) // 2)
                    if start and f == 0:
                        turn_out(2 * NIT - 1, 1, t_event(NIT - 1, "out0") + 1)
                    if start and f == NSH - 1:
                        pe.wait_ge(t_read, t_event(NIT - 1, "out0") + 2)
                        turn_weights(0, allb[7])
                    if start:
                        for what, cc, i in PROJECT.get(f, ()):
                            if what == "turn":
                                if i:
                                    pe.wait_ge(aT_ready, KH * cc + 1)
                                elif cc == S // CH:
                                    pe.wait_ge(route_step, ROUTE_STEPS + 2)
                                else:
                                    pe.wait_ge(x1_ready, 2 * cc)
                                turn_attention(cc, i)
                            else:
                                if i:
                                    pe.wait_ge(x1_ready, 2 * cc + 1)
                                project(cc, i)
                    if not last:
                        if start and f == TURNW_AT:
                            pe.wait_ge(x1_ready, 2 * NC)
                        beside(c, f, start)

            chunks(ffn)(pe)
            down(NC - 1, NFT - 1)
            turn_back(NC - 1, 0)
            turn_back(NC - 1, 1)


def kernel(**inputs):
    import numpy as np
    import concourse.bacc as bacc
    from concourse.bass_utils import run_bass_kernel_spmd as run

    def kmajor(w):
        w = np.asarray(w).T
        return np.ascontiguousarray(w.reshape(w.shape[0] // 128, 128, w.shape[1]).transpose(1, 0, 2))

    nc = bacc.Bacc("TRN2", target_bir_lowering=False, num_devices=1)
    wqkv = np.asarray(inputs["L0_attn_W_qkv"])
    bqkv = np.asarray(inputs["L0_attn_b_qkv"])
    arrays = {
        "x": np.asarray(inputs["L0_attn_x"]).reshape(T, H),
        "wqk": kmajor(wqkv[:2 * H]),
        "bqk": bqkv[:2 * H].reshape(4, 128).T,
        "wv": kmajor(wqkv[2 * H:]),
        "bv": bqkv[2 * H:],
        "wout": kmajor(inputs["L0_attn_W_out"]),
        "bout": np.asarray(inputs["L0_attn_b_out"]),
        "cT": kmajor(inputs["L0_c"]),
        "wmod": kmajor(np.asarray(inputs["L0_wmod"]).T),
    }
    up, down = np.asarray(inputs["L0_ffn_expert_up_w"]), np.asarray(inputs["L0_ffn_expert_down_w"])
    sup, sdown = np.asarray(inputs["L0_ffn_shared_up_w"]), np.asarray(inputs["L0_ffn_shared_down_w"])

    def tiles(gate, upw, downw):
        n = -(-gate.shape[0] // 128)
        room = ((0, n * 128 - gate.shape[0]), (0, 0))
        g, u, d = (np.pad(a, room).reshape(n, 128, 256) for a in (gate, upw, downw.T))
        g, u = (a.reshape(n, 128, 2, 128).transpose(0, 3, 2, 1).reshape(n, 128, 256) for a in (g, u))
        return np.concatenate([g, u, d], axis=2)

    arrays["wgate"] = kmajor(inputs["L0_ffn_gate_w"])
    arrays["wffn"] = np.concatenate([
        tiles(sup[:SI], sup[SI:], sdown),
        tiles(up[:, :EI].reshape(-1, H), up[:, EI:].reshape(-1, H), down.transpose(1, 0, 2).reshape(H, -1)),
    ])
    maps, args = {}, []
    for name, a in arrays.items():
        a = np.ascontiguousarray(a)
        maps["in_" + name] = a
        args.append(nc.dram_tensor("in_" + name, a.shape, mybir.dt.from_np(a.dtype), kind="ExternalInput").ap())
    args.append(nc.dram_tensor("qk_parts", (2, B, H, len(Q_PARTS), S), BF16, kind="Internal").ap())
    args.append(nc.dram_tensor("routing_weights", (NE, T), F32, kind="Internal").ap())
    args.append(nc.dram_tensor("out", (T, H), F32, kind="ExternalOutput").ap())
    program(nc, *args)
    r = run(nc, [maps], core_ids=[0])
    return r.results[0]["out"].reshape(B, S, H)
```
